# Optimizing a Trainium2 kernel written in Bass

```python
import numpy as np
import jax
import jax.numpy as jnp

def _softmax(x, axis=-1):
    return jax.nn.softmax(x, axis=axis)

def _gelu(x):
    return jax.nn.gelu(x, approximate=True)

def _silu(x):
    return jax.nn.silu(x)

def _sigmoid(x):
    return jax.nn.sigmoid(x)

def _layernorm(x, axis=-1, eps=1e-05):
    m = jnp.mean(x, axis=axis, keepdims=True)
    v = jnp.var(x, axis=axis, keepdims=True)
    return (x - m) / jnp.sqrt(v + eps)

def _scatter_add(tgt, idx, src, axis=0):
    return tgt.at[idx].add(src)

def _segment_sum(src, seg, n):
    return jax.ops.segment_sum(src, seg, n)
kernel_name = 'mk_hybrid_d2_jaxref_r8_87a45f'

def setup_inputs(seed: int=0):
    np.random.seed(seed)
    _w = jnp.asarray

    def _L0_attn_a_setup():
        import math
        import jax, jax.numpy as jnp
        import numpy as np
        LN_EPS = 1e-05

        def _relative_sinusoidal(t, hd, dtype):
            pos = jnp.arange(-(t - 1), t, dtype=dtype)[:, None]
            div = jnp.exp(jnp.arange(0, hd, 2, dtype=dtype) * (-math.log(10000.0) / hd))
            pe = jnp.zeros((2 * t - 1, hd), dtype=dtype)
            pe = pe.at[:, 0::2].set(jnp.sin(pos * div))
            pe = pe.at[:, 1::2].set(jnp.cos(pos * div))
            return pe
        key = jax.random.key(seed)
        ks = jax.random.split(key, 4)
        b, t, dim, H = (2, 256, 128, 16)
        hd = dim // H
        s = 0.02
        return {'x': jax.random.normal(ks[0], (b, t, dim), jnp.float32), 'ln_g': jnp.ones((dim,), jnp.float32), 'ln_b': jnp.zeros((dim,), jnp.float32), 'w_qkv': jax.random.normal(ks[1], (dim, 3 * dim), jnp.float32) * s, 'b_qkv': jnp.zeros((3 * dim,), jnp.float32), 'w_rel': jax.random.normal(ks[2], (hd, H), jnp.float32) * s, 'w_out': jax.random.normal(ks[3], (dim, dim), jnp.float32) * s, 'b_out': jnp.zeros((dim,), jnp.float32)}
    _L0_attn_a_in = _L0_attn_a_setup()

    def _L0_attn_b_setup():
        import jax, jax.numpy as jnp
        import numpy as np
        DM, EXP, N, K, FRAC = (128, 2, 16, 4, 16)
        D = DM * EXP
        DTR = D // FRAC
        EPS = 1e-06

        def _mamba_block(x, rms_w, in_W, in_b, conv_w, conv_b, A_log, dbc_W, dbc_b, dup_W, dup_b, out_W, out_b):
            residual = x
            h = x * jax.lax.rsqrt(jnp.mean(x * x, axis=-1, keepdims=True) + EPS) * rms_w
            proj = h @ in_W + in_b
            x1, g = (proj[..., :D], proj[..., D:])
            xt = jnp.transpose(x1, (0, 2, 1))
            xc = jax.lax.conv_general_dilated(xt, conv_w[:, None, :], window_strides=(1,), padding=[(K - 1, 0)], feature_group_count=D, dimension_numbers=('NCH', 'OIH', 'NCH'))
            xc = xc + conv_b[:, None]
            x1 = jax.nn.silu(jnp.transpose(xc, (0, 2, 1)))
            A = -jnp.exp(A_log)
            dbc = x1 @ dbc_W + dbc_b
            delta, Bm, Cm = (dbc[..., :DTR], dbc[..., DTR:DTR + N], dbc[..., DTR + N:])
            delta = jax.nn.softplus(delta @ dup_W + dup_b)
            A_disc = jnp.exp(delta[..., None] * A)
            B_x = delta[..., None] * Bm[:, :, None, :] * x1[..., None]
            Ad_t = jnp.transpose(A_disc, (1, 0, 2, 3))
            Bx_t = jnp.transpose(B_x, (1, 0, 2, 3))

            def step(hc, inp):
                a, b = inp
                hc = a * hc + b
                return (hc, hc)
            h0 = jnp.zeros((x.shape[0], D, N), x1.dtype)
            _, hs = jax.lax.scan(step, h0, (Ad_t, Bx_t))
            y = jnp.einsum('tbdn,btn->btd', hs, Cm)
            y = jax.nn.silu(g) * y
            out = y @ out_W + out_b
            return out + residual
        key = jax.random.key(seed)
        ks = jax.random.split(key, 12)
        s = lambda fan: 1.0 / np.sqrt(fan)
        x = jax.random.normal(ks[0], (2, 128, DM), jnp.float32)
        rms_w = jnp.ones((DM,), jnp.float32)
        in_W = jax.random.normal(ks[1], (DM, 2 * D), jnp.float32) * s(DM)
        in_b = jax.random.normal(ks[2], (2 * D,), jnp.float32) * s(DM)
        conv_w = jax.random.normal(ks[3], (D, K), jnp.float32) * s(K)
        conv_b = jax.random.normal(ks[4], (D,), jnp.float32) * s(K)
        A_log = jnp.log(jnp.tile(jnp.arange(1, N + 1, dtype=jnp.float32), (D, 1)))
        dbc_W = jax.random.normal(ks[5], (D, DTR + 2 * N), jnp.float32) * s(D)
        dbc_b = jax.random.normal(ks[6], (DTR + 2 * N,), jnp.float32) * s(D)
        dup_W = jax.random.normal(ks[7], (DTR, D), jnp.float32) * s(DTR)
        dup_b = jax.random.normal(ks[8], (D,), jnp.float32) * s(DTR)
        out_W = jax.random.normal(ks[9], (D, DM), jnp.float32) * s(D)
        out_b = jax.random.normal(ks[10], (DM,), jnp.float32) * s(D)
        return dict(x=x, rms_w=rms_w, in_W=in_W, in_b=in_b, conv_w=conv_w, conv_b=conv_b, A_log=A_log, dbc_W=dbc_W, dbc_b=dbc_b, dup_W=dup_W, dup_b=dup_b, out_W=out_W, out_b=out_b)
    _L0_attn_b_in = _L0_attn_b_setup()

    def _L0_ffn_setup():
        import jax, jax.numpy as jnp
        import numpy as np
        E, H, I, K = (8, 128, 256, 2)
        B, S = (4, 256)
        key = jax.random.key(seed)
        k1, k2, k3, k4 = jax.random.split(key, 4)
        x = jax.random.normal(k1, (B, S, H), dtype=jnp.float32)
        router_w = jax.random.uniform(k2, (E, H), dtype=jnp.float32, minval=-1.0, maxval=1.0) / np.sqrt(H).astype(np.float32)
        w13 = jax.random.normal(k3, (E, H, 2 * I), dtype=jnp.float32) * 0.02
        w2 = jax.random.normal(k4, (E, I, H), dtype=jnp.float32) * 0.02
        return {'x': x, 'router_w': router_w, 'w13': w13, 'w2': w2}
    _L0_ffn_in = _L0_ffn_setup()

    def _L1_attn_a_setup():
        import jax, jax.numpy as jnp
        import numpy as np
        HIDDEN = 128
        NUM_HEADS = 16
        HEAD_DIM = HIDDEN // NUM_HEADS
        BLOCK = 32
        TOPK = 8
        WINDOW = 128

        def _attn(q, k, v, mask=None):
            scale = 1.0 / jnp.sqrt(jnp.asarray(q.shape[-1], q.dtype))
            scores = jnp.einsum('bhqd,bhkd->bhqk', q, k) * scale
            if mask is not None:
                scores = jnp.where(mask, scores, jnp.asarray(-1000000000.0, scores.dtype))
            probs = jax.nn.softmax(scores, axis=-1)
            return jnp.einsum('bhqk,bhkd->bhqd', probs, v)
        key = jax.random.key(seed)
        ks = jax.random.split(key, 12)
        B, L, H = (2, 128, HIDDEN)
        s = 1.0 / np.sqrt(H)
        inp = {'hidden_states': jax.random.normal(ks[0], (B, L, H), jnp.float32), 'Wq': jax.random.normal(ks[1], (H, H), jnp.float32) * s, 'bq': jnp.zeros((H,), jnp.float32), 'Wk': jax.random.normal(ks[2], (H, H), jnp.float32) * s, 'bk': jnp.zeros((H,), jnp.float32), 'Wv': jax.random.normal(ks[3], (H, H), jnp.float32) * s, 'bv': jnp.zeros((H,), jnp.float32), 'Wg': jax.random.normal(ks[4], (H, 3), jnp.float32) * s, 'bg': jnp.zeros((3,), jnp.float32), 'Wo': jax.random.normal(ks[5], (H, H), jnp.float32) * s, 'bo': jnp.zeros((H,), jnp.float32)}
        return inp
    _L1_attn_a_in = _L1_attn_a_setup()

    def _L1_attn_b_setup():
        import jax, jax.numpy as jnp
        import numpy as np
        H, P, CH = (4, 6, 32)
        DK, DV, D = (32, 32, 128)
        FLOOR = 0.05

        def _dwconv_causal(x, w):
            k = w.shape[-1]
            xp = jnp.pad(x, ((0, 0), (k - 1, 0), (0, 0)))
            return jax.lax.conv_general_dilated(xp, w.T[:, None, :], (1,), 'VALID', dimension_numbers=('NWC', 'WIO', 'NWC'), feature_group_count=x.shape[-1])

        def _l2norm(x):
            return x / jnp.sqrt(jnp.sum(x * x, -1, keepdims=True) + 1e-12)

        def _delta_rule_chunkwise(q, k, v, beta):
            B, Hh, L, dk = q.shape
            dv = v.shape[-1]
            n = L // CH
            q = _l2norm(q)
            k = _l2norm(k)
            v = v * beta[..., None]
            kb = k * beta[..., None]
            rs = lambda t: t.reshape(B, Hh, n, CH, -1)
            q, k, v, kb = (rs(q), rs(k), rs(v), rs(kb))
            A = -jnp.einsum('bhncd,bhnsd->bhncs', kb, k)
            A = A * jnp.tril(jnp.ones((CH, CH), A.dtype), -1)
            for i in range(1, CH):
                A = A.at[..., i, :].add(jnp.einsum('bhns,bhnsc->bhnc', A[..., i, :], A))
            inv = A + jnp.eye(CH, dtype=A.dtype)
            u = jnp.einsum('bhncs,bhnsd->bhncd', inv, v)
            w = jnp.einsum('bhncs,bhnsd->bhncd', inv, kb)
            mt = jnp.tril(jnp.ones((CH, CH), q.dtype))

            def step(S, xs):
                qi, ki, ui0, wi = xs
                attn = jnp.einsum('bhcd,bhsd->bhcs', qi, ki) * mt
                ui = ui0 - jnp.einsum('bhck,bhkv->bhcv', wi, S)
                oi = jnp.einsum('bhck,bhkv->bhcv', qi, S) + jnp.einsum('bhcs,bhsv->bhcv', attn, ui)
                S = S + jnp.einsum('bhcd,bhcv->bhdv', ki, ui)
                return (S, oi)
            mv = lambda t: jnp.moveaxis(t, 2, 0)
            S0 = jnp.zeros((B, Hh, dk, dv), q.dtype)
            S, o = jax.lax.scan(step, S0, (mv(q), mv(k), mv(u), mv(w)))
            o = jnp.moveaxis(o, 0, 2).reshape(B, Hh, L, dv)
            return (o, S)
        key = jax.random.key(seed)
        ks = jax.random.split(key, 24)
        s = 0.02
        gate_in = D + H * P
        gb2 = s * jax.random.normal(ks[15], (H * P,))
        gb2 = gb2.reshape(H, P).at[:, P - 1].add(2.0).reshape(-1)

        def fir(k_, kernel):
            f = s * jax.random.normal(k_, (H * DV, kernel))
            return f.at[:, -1].add(1.0)
        return {'hidden_states': jax.random.normal(ks[0], (2, 256, D), jnp.float32), 'q_proj_w': s * jax.random.normal(ks[1], (H * DK, D)), 'k_proj_w': s * jax.random.normal(ks[2], (H * DK, D)), 'v_proj_w': s * jax.random.normal(ks[3], (H * DV, D)), 'b_proj_w': s * jax.random.normal(ks[4], (H, D)), 'q_conv_w': s * jax.random.normal(ks[5], (H * DK, 4)), 'k_conv_w': s * jax.random.normal(ks[6], (H * DK, 4)), 'v_conv_w': s * jax.random.normal(ks[7], (H * DV, 4)), 'fir_w3': fir(ks[8], 3), 'fir_w7': fir(ks[9], 7), 'fir_w15': fir(ks[10], 15), 'fir_w31': fir(ks[11], 31), 'gate_w1': s * jax.random.normal(ks[12], (2 * D, gate_in)), 'gate_b1': jnp.zeros((2 * D,)), 'gate_w2': s * jax.random.normal(ks[13], (H * P, 2 * D)), 'gate_b2': gb2, 'gate_log_temp': jnp.ones((H,)), 'alpha_stat': 0.1 * jnp.ones((P,)), 'o_norm_w': jnp.ones((DV,)), 'o_proj_w': s * jax.random.normal(ks[14], (D, H * DV))}
    _L1_attn_b_in = _L1_attn_b_setup()

    def _L1_ffn_setup():
        import jax, jax.numpy as jnp
        import numpy as np
        D_IN, D_HID = (128, 512)

        def _ternary(key, shape):
            return jax.random.randint(key, shape, -1, 2).astype(jnp.float32)

        def _tlin(x, w, s):
            return jnp.einsum('bsi,oi->bso', x, w) * s
        key = jax.random.key(seed)
        ks = jax.random.split(key, 12)
        inv = lambda fan: 1.0 / np.sqrt(fan).astype(np.float32)
        return {'x': jax.random.normal(ks[0], (4, 256, D_IN), dtype=jnp.float32), 'w1_w': _ternary(ks[1], (D_HID, D_IN)), 'w1_s': jax.random.uniform(ks[2], (D_HID,), dtype=jnp.float32) * inv(D_IN), 'w2_w': _ternary(ks[3], (D_HID, D_IN)), 'w2_s': jax.random.uniform(ks[4], (D_HID,), dtype=jnp.float32) * inv(D_IN), 'h1_w': _ternary(ks[5], (D_HID, D_HID)), 'h1_s': jax.random.uniform(ks[6], (D_HID,), dtype=jnp.float32) * inv(D_HID), 'h2_w': _ternary(ks[7], (D_HID, D_HID)), 'h2_s': jax.random.uniform(ks[8], (D_HID,), dtype=jnp.float32) * inv(D_HID), 'w3_w': _ternary(ks[9], (D_IN, D_HID)), 'w3_s': jax.random.uniform(ks[10], (D_IN,), dtype=jnp.float32) * inv(D_HID)}
    _L1_ffn_in = _L1_ffn_setup()
    _d = {'L0_attn_a_x': _L0_attn_a_in['x'], 'L0_attn_a_ln_g': _L0_attn_a_in['ln_g'], 'L0_attn_a_ln_b': _L0_attn_a_in['ln_b'], 'L0_attn_a_w_qkv': _L0_attn_a_in['w_qkv'], 'L0_attn_a_b_qkv': _L0_attn_a_in['b_qkv'], 'L0_attn_a_w_rel': _L0_attn_a_in['w_rel'], 'L0_attn_a_w_out': _L0_attn_a_in['w_out'], 'L0_attn_a_b_out': _L0_attn_a_in['b_out'], 'L0_attn_b_rms_w': _L0_attn_b_in['rms_w'], 'L0_attn_b_in_W': _L0_attn_b_in['in_W'], 'L0_attn_b_in_b': _L0_attn_b_in['in_b'], 'L0_attn_b_conv_w': _L0_attn_b_in['conv_w'], 'L0_attn_b_conv_b': _L0_attn_b_in['conv_b'], 'L0_attn_b_A_log': _L0_attn_b_in['A_log'], 'L0_attn_b_dbc_W': _L0_attn_b_in['dbc_W'], 'L0_attn_b_dbc_b': _L0_attn_b_in['dbc_b'], 'L0_attn_b_dup_W': _L0_attn_b_in['dup_W'], 'L0_attn_b_dup_b': _L0_attn_b_in['dup_b'], 'L0_attn_b_out_W': _L0_attn_b_in['out_W'], 'L0_attn_b_out_b': _L0_attn_b_in['out_b'], 'L0_ffn_router_w': _L0_ffn_in['router_w'], 'L0_ffn_w13': _L0_ffn_in['w13'], 'L0_ffn_w2': _L0_ffn_in['w2'], 'L1_attn_a_Wq': _L1_attn_a_in['Wq'], 'L1_attn_a_bq': _L1_attn_a_in['bq'], 'L1_attn_a_Wk': _L1_attn_a_in['Wk'], 'L1_attn_a_bk': _L1_attn_a_in['bk'], 'L1_attn_a_Wv': _L1_attn_a_in['Wv'], 'L1_attn_a_bv': _L1_attn_a_in['bv'], 'L1_attn_a_Wg': _L1_attn_a_in['Wg'], 'L1_attn_a_bg': _L1_attn_a_in['bg'], 'L1_attn_a_Wo': _L1_attn_a_in['Wo'], 'L1_attn_a_bo': _L1_attn_a_in['bo'], 'L1_attn_b_q_proj_w': _L1_attn_b_in['q_proj_w'], 'L1_attn_b_k_proj_w': _L1_attn_b_in['k_proj_w'], 'L1_attn_b_v_proj_w': _L1_attn_b_in['v_proj_w'], 'L1_attn_b_b_proj_w': _L1_attn_b_in['b_proj_w'], 'L1_attn_b_q_conv_w': _L1_attn_b_in['q_conv_w'], 'L1_attn_b_k_conv_w': _L1_attn_b_in['k_conv_w'], 'L1_attn_b_v_conv_w': _L1_attn_b_in['v_conv_w'], 'L1_attn_b_fir_w3': _L1_attn_b_in['fir_w3'], 'L1_attn_b_fir_w7': _L1_attn_b_in['fir_w7'], 'L1_attn_b_fir_w15': _L1_attn_b_in['fir_w15'], 'L1_attn_b_fir_w31': _L1_attn_b_in['fir_w31'], 'L1_attn_b_gate_w1': _L1_attn_b_in['gate_w1'], 'L1_attn_b_gate_b1': _L1_attn_b_in['gate_b1'], 'L1_attn_b_gate_w2': _L1_attn_b_in['gate_w2'], 'L1_attn_b_gate_b2': _L1_attn_b_in['gate_b2'], 'L1_attn_b_gate_log_temp': _L1_attn_b_in['gate_log_temp'], 'L1_attn_b_alpha_stat': _L1_attn_b_in['alpha_stat'], 'L1_attn_b_o_norm_w': _L1_attn_b_in['o_norm_w'], 'L1_attn_b_o_proj_w': _L1_attn_b_in['o_proj_w'], 'L1_ffn_w1_w': _L1_ffn_in['w1_w'], 'L1_ffn_w1_s': _L1_ffn_in['w1_s'], 'L1_ffn_w2_w': _L1_ffn_in['w2_w'], 'L1_ffn_w2_s': _L1_ffn_in['w2_s'], 'L1_ffn_h1_w': _L1_ffn_in['h1_w'], 'L1_ffn_h1_s': _L1_ffn_in['h1_s'], 'L1_ffn_h2_w': _L1_ffn_in['h2_w'], 'L1_ffn_h2_s': _L1_ffn_in['h2_s'], 'L1_ffn_w3_w': _L1_ffn_in['w3_w'], 'L1_ffn_w3_s': _L1_ffn_in['w3_s']}
    _x0 = _d['L0_attn_a_x']
    _d['L0_attn_a_x'] = jax.random.normal(jax.random.fold_in(jax.random.key(seed), 1), (4, 1024, 128), dtype=_x0.dtype)
    del _x0
    return _d

def reference(L0_attn_a_x, L0_attn_a_ln_g, L0_attn_a_ln_b, L0_attn_a_w_qkv, L0_attn_a_b_qkv, L0_attn_a_w_rel, L0_attn_a_w_out, L0_attn_a_b_out, L0_attn_b_rms_w, L0_attn_b_in_W, L0_attn_b_in_b, L0_attn_b_conv_w, L0_attn_b_conv_b, L0_attn_b_A_log, L0_attn_b_dbc_W, L0_attn_b_dbc_b, L0_attn_b_dup_W, L0_attn_b_dup_b, L0_attn_b_out_W, L0_attn_b_out_b, L0_ffn_router_w, L0_ffn_w13, L0_ffn_w2, L1_attn_a_Wq, L1_attn_a_bq, L1_attn_a_Wk, L1_attn_a_bk, L1_attn_a_Wv, L1_attn_a_bv, L1_attn_a_Wg, L1_attn_a_bg, L1_attn_a_Wo, L1_attn_a_bo, L1_attn_b_q_proj_w, L1_attn_b_k_proj_w, L1_attn_b_v_proj_w, L1_attn_b_b_proj_w, L1_attn_b_q_conv_w, L1_attn_b_k_conv_w, L1_attn_b_v_conv_w, L1_attn_b_fir_w3, L1_attn_b_fir_w7, L1_attn_b_fir_w15, L1_attn_b_fir_w31, L1_attn_b_gate_w1, L1_attn_b_gate_b1, L1_attn_b_gate_w2, L1_attn_b_gate_b2, L1_attn_b_gate_log_temp, L1_attn_b_alpha_stat, L1_attn_b_o_norm_w, L1_attn_b_o_proj_w, L1_ffn_w1_w, L1_ffn_w1_s, L1_ffn_w2_w, L1_ffn_w2_s, L1_ffn_h1_w, L1_ffn_h1_s, L1_ffn_h2_w, L1_ffn_h2_s, L1_ffn_w3_w, L1_ffn_w3_s):

    def _L0_attn_a_ref(x, ln_g, ln_b, w_qkv, b_qkv, w_rel, w_out, b_out):
        import math
        import jax, jax.numpy as jnp
        import numpy as np
        LN_EPS = 1e-05

        def _relative_sinusoidal(t, hd, dtype):
            pos = jnp.arange(-(t - 1), t, dtype=dtype)[:, None]
            div = jnp.exp(jnp.arange(0, hd, 2, dtype=dtype) * (-math.log(10000.0) / hd))
            pe = jnp.zeros((2 * t - 1, hd), dtype=dtype)
            pe = pe.at[:, 0::2].set(jnp.sin(pos * div))
            pe = pe.at[:, 1::2].set(jnp.cos(pos * div))
            return pe
        b, t, dim = x.shape
        hd, H = w_rel.shape
        scale = hd ** (-0.5)
        mu = jnp.mean(x, axis=-1, keepdims=True)
        var = jnp.mean(jnp.square(x - mu), axis=-1, keepdims=True)
        xn = (x - mu) * jax.lax.rsqrt(var + LN_EPS) * ln_g + ln_b
        qkv = (xn @ w_qkv + b_qkv).reshape(b, t, 3, H, hd)
        qkv = jnp.transpose(qkv, (2, 0, 3, 1, 4))
        q, k, v = (qkv[0], qkv[1], qkv[2])
        scores = jnp.einsum('bhqd,bhkd->bhqk', q, k) * scale
        rel_pe = _relative_sinusoidal(t, hd, scores.dtype)
        rel_bias = rel_pe @ w_rel
        idx = jnp.arange(t)[:, None] - jnp.arange(t)[None, :] + (t - 1)
        bias = jnp.transpose(rel_bias[idx], (2, 0, 1))[None]
        attn = jax.nn.softmax(scores + bias, axis=-1)
        out = jnp.einsum('bhqk,bhkd->bhqd', attn, v)
        out = jnp.transpose(out, (0, 2, 1, 3)).reshape(b, t, dim)
        return out @ w_out + b_out

    def _L0_attn_b_ref(x, rms_w, in_W, in_b, conv_w, conv_b, A_log, dbc_W, dbc_b, dup_W, dup_b, out_W, out_b):
        import jax, jax.numpy as jnp
        import numpy as np
        DM, EXP, N, K, FRAC = (128, 2, 16, 4, 16)
        D = DM * EXP
        DTR = D // FRAC
        EPS = 1e-06

        def _mamba_block(x, rms_w, in_W, in_b, conv_w, conv_b, A_log, dbc_W, dbc_b, dup_W, dup_b, out_W, out_b):
            residual = x
            h = x * jax.lax.rsqrt(jnp.mean(x * x, axis=-1, keepdims=True) + EPS) * rms_w
            proj = h @ in_W + in_b
            x1, g = (proj[..., :D], proj[..., D:])
            xt = jnp.transpose(x1, (0, 2, 1))
            xc = jax.lax.conv_general_dilated(xt, conv_w[:, None, :], window_strides=(1,), padding=[(K - 1, 0)], feature_group_count=D, dimension_numbers=('NCH', 'OIH', 'NCH'))
            xc = xc + conv_b[:, None]
            x1 = jax.nn.silu(jnp.transpose(xc, (0, 2, 1)))
            A = -jnp.exp(A_log)
            dbc = x1 @ dbc_W + dbc_b
            delta, Bm, Cm = (dbc[..., :DTR], dbc[..., DTR:DTR + N], dbc[..., DTR + N:])
            delta = jax.nn.softplus(delta @ dup_W + dup_b)
            A_disc = jnp.exp(delta[..., None] * A)
            B_x = delta[..., None] * Bm[:, :, None, :] * x1[..., None]
            Ad_t = jnp.transpose(A_disc, (1, 0, 2, 3))
            Bx_t = jnp.transpose(B_x, (1, 0, 2, 3))

            def step(hc, inp):
                a, b = inp
                hc = a * hc + b
                return (hc, hc)
            h0 = jnp.zeros((x.shape[0], D, N), x1.dtype)
            _, hs = jax.lax.scan(step, h0, (Ad_t, Bx_t))
            y = jnp.einsum('tbdn,btn->btd', hs, Cm)
            y = jax.nn.silu(g) * y
            out = y @ out_W + out_b
            return out + residual
        return _mamba_block(x, rms_w, in_W, in_b, conv_w, conv_b, A_log, dbc_W, dbc_b, dup_W, dup_b, out_W, out_b)

    def _L0_ffn_ref(x, router_w, w13, w2):
        import jax, jax.numpy as jnp
        import numpy as np
        E, H, I, K = (8, 128, 256, 2)
        B, S = (4, 256)
        logits = jnp.einsum('bsh,eh->bse', x, router_w)
        probs = jax.nn.softmax(logits, axis=-1)
        weights, indices = jax.lax.top_k(probs, K)
        weights = weights / (weights.sum(axis=-1, keepdims=True) + 1e-06)
        h13 = jnp.einsum('bsh,ehi->bsei', x, w13)
        gate, up = jnp.split(h13, 2, axis=-1)
        h = jax.nn.silu(gate) * up
        y = jnp.einsum('bsei,eih->bseh', h, w2)
        y_sel = jnp.take_along_axis(y, indices[..., None], axis=2)
        return (y_sel * weights[..., None]).sum(axis=2)

    def _L1_attn_a_ref(hidden_states, Wq, bq, Wk, bk, Wv, bv, Wg, bg, Wo, bo):
        import jax, jax.numpy as jnp
        import numpy as np
        HIDDEN = 128
        NUM_HEADS = 16
        HEAD_DIM = HIDDEN // NUM_HEADS
        BLOCK = 32
        TOPK = 8
        WINDOW = 128

        def _attn(q, k, v, mask=None):
            scale = 1.0 / jnp.sqrt(jnp.asarray(q.shape[-1], q.dtype))
            scores = jnp.einsum('bhqd,bhkd->bhqk', q, k) * scale
            if mask is not None:
                scores = jnp.where(mask, scores, jnp.asarray(-1000000000.0, scores.dtype))
            probs = jax.nn.softmax(scores, axis=-1)
            return jnp.einsum('bhqk,bhkd->bhqd', probs, v)
        B, L, H = hidden_states.shape
        nh, hd = (NUM_HEADS, HEAD_DIM)
        nblocks = L // BLOCK

        def proj(W, b):
            return (hidden_states @ W + b).reshape(B, L, nh, hd).transpose(0, 2, 1, 3)
        q = proj(Wq, bq)
        k = proj(Wk, bk)
        v = proj(Wv, bv)
        gates = jax.nn.sigmoid(hidden_states @ Wg + bg)
        ck = k.reshape(B, nh, nblocks, BLOCK, hd).mean(axis=3)
        cv = v.reshape(B, nh, nblocks, BLOCK, hd).mean(axis=3)
        compressed_out = _attn(q, ck, cv)
        scale = 1.0 / jnp.sqrt(jnp.asarray(hd, q.dtype))
        imp = jnp.einsum('bhqd,bhkd->bhqk', q, ck) * scale
        block_scores = jax.nn.softmax(imp, axis=-1).sum(axis=2)
        _, idx = jax.lax.top_k(block_scores, TOPK)
        kb = k.reshape(B, nh, nblocks, BLOCK, hd)
        vb = v.reshape(B, nh, nblocks, BLOCK, hd)
        gidx = idx[..., None, None]
        sel_k = jnp.take_along_axis(kb, gidx, axis=2).reshape(B, nh, TOPK * BLOCK, hd)
        sel_v = jnp.take_along_axis(vb, gidx, axis=2).reshape(B, nh, TOPK * BLOCK, hd)
        selected_out = _attn(q, sel_k, sel_v)
        i = jnp.arange(L)[:, None]
        j = jnp.arange(L)[None, :]
        wmask = (j <= i) & (j > i - WINDOW)
        sliding_out = _attn(q, k, v, mask=wmask[None, None])
        g = gates[:, None]
        out = g[..., 0:1] * compressed_out + g[..., 1:2] * selected_out + g[..., 2:3] * sliding_out
        out = out.transpose(0, 2, 1, 3).reshape(B, L, H)
        return out @ Wo + bo

    def _L1_attn_b_ref(hidden_states, q_proj_w, k_proj_w, v_proj_w, b_proj_w, q_conv_w, k_conv_w, v_conv_w, fir_w3, fir_w7, fir_w15, fir_w31, gate_w1, gate_b1, gate_w2, gate_b2, gate_log_temp, alpha_stat, o_norm_w, o_proj_w):
        import jax, jax.numpy as jnp
        import numpy as np
        H, P, CH = (4, 6, 32)
        DK, DV, D = (32, 32, 128)
        FLOOR = 0.05

        def _dwconv_causal(x, w):
            k = w.shape[-1]
            xp = jnp.pad(x, ((0, 0), (k - 1, 0), (0, 0)))
            return jax.lax.conv_general_dilated(xp, w.T[:, None, :], (1,), 'VALID', dimension_numbers=('NWC', 'WIO', 'NWC'), feature_group_count=x.shape[-1])

        def _l2norm(x):
            return x / jnp.sqrt(jnp.sum(x * x, -1, keepdims=True) + 1e-12)

        def _delta_rule_chunkwise(q, k, v, beta):
            B, Hh, L, dk = q.shape
            dv = v.shape[-1]
            n = L // CH
            q = _l2norm(q)
            k = _l2norm(k)
            v = v * beta[..., None]
            kb = k * beta[..., None]
            rs = lambda t: t.reshape(B, Hh, n, CH, -1)
            q, k, v, kb = (rs(q), rs(k), rs(v), rs(kb))
            A = -jnp.einsum('bhncd,bhnsd->bhncs', kb, k)
            A = A * jnp.tril(jnp.ones((CH, CH), A.dtype), -1)
            for i in range(1, CH):
                A = A.at[..., i, :].add(jnp.einsum('bhns,bhnsc->bhnc', A[..., i, :], A))
            inv = A + jnp.eye(CH, dtype=A.dtype)
            u = jnp.einsum('bhncs,bhnsd->bhncd', inv, v)
            w = jnp.einsum('bhncs,bhnsd->bhncd', inv, kb)
            mt = jnp.tril(jnp.ones((CH, CH), q.dtype))

            def step(S, xs):
                qi, ki, ui0, wi = xs
                attn = jnp.einsum('bhcd,bhsd->bhcs', qi, ki) * mt
                ui = ui0 - jnp.einsum('bhck,bhkv->bhcv', wi, S)
                oi = jnp.einsum('bhck,bhkv->bhcv', qi, S) + jnp.einsum('bhcs,bhsv->bhcv', attn, ui)
                S = S + jnp.einsum('bhcd,bhcv->bhdv', ki, ui)
                return (S, oi)
            mv = lambda t: jnp.moveaxis(t, 2, 0)
            S0 = jnp.zeros((B, Hh, dk, dv), q.dtype)
            S, o = jax.lax.scan(step, S0, (mv(q), mv(k), mv(u), mv(w)))
            o = jnp.moveaxis(o, 0, 2).reshape(B, Hh, L, dv)
            return (o, S)
        B, T, _ = hidden_states.shape
        q = jax.nn.silu(_dwconv_causal(hidden_states @ q_proj_w.T, q_conv_w)).reshape(B, T, H, DK)
        k = jax.nn.silu(_dwconv_causal(hidden_states @ k_proj_w.T, k_conv_w)).reshape(B, T, H, DK)
        v = jax.nn.silu(_dwconv_causal(hidden_states @ v_proj_w.T, v_conv_w)).reshape(B, T, H, DV)
        beta = jax.nn.sigmoid(hidden_states @ b_proj_w.T)
        bhl = lambda t: jnp.moveaxis(t, 2, 1)
        delta_out, _ = _delta_rule_chunkwise(bhl(q), bhl(k), bhl(v), jnp.moveaxis(beta, 2, 1))
        delta_out = jnp.moveaxis(delta_out, 1, 2)
        vflat = v.reshape(B, T, H * DV)
        firs = [_dwconv_causal(vflat, f).reshape(B, T, H, DV) for f in (fir_w3, fir_w7, fir_w15, fir_w31)]
        branches = jnp.stack(firs + [v, delta_out], 0)
        stats = jnp.moveaxis(jnp.mean(jnp.abs(branches), -1), 0, -1)
        gi = jnp.concatenate([hidden_states, stats.reshape(B, T, H * P)], -1)
        h1 = jax.nn.gelu(gi @ gate_w1.T + gate_b1, approximate=False)
        logits = (h1 @ gate_w2.T + gate_b2).reshape(B, T, H, P)
        logits = logits + alpha_stat * stats
        temp = jax.nn.softplus(gate_log_temp) + 0.0001
        probs = jax.nn.softmax(logits / temp[None, None, :, None], -1)
        probs = probs * (1.0 - FLOOR)
        probs = probs.at[..., -1].add(FLOOR)
        o = jnp.einsum('pbthd,bthp->bthd', branches, probs)
        o = o * jax.lax.rsqrt(jnp.mean(o * o, -1, keepdims=True) + 1e-05) * o_norm_w
        return o.reshape(B, T, H * DV) @ o_proj_w.T

    def _L1_ffn_ref(x, w1_w, w1_s, w2_w, w2_s, h1_w, h1_s, h2_w, h2_s, w3_w, w3_s):
        import jax, jax.numpy as jnp
        import numpy as np
        D_IN, D_HID = (128, 512)

        def _ternary(key, shape):
            return jax.random.randint(key, shape, -1, 2).astype(jnp.float32)

        def _tlin(x, w, s):
            return jnp.einsum('bsi,oi->bso', x, w) * s
        h = jax.nn.silu(_tlin(x, w1_w, w1_s)) * _tlin(x, w2_w, w2_s)
        h = jax.nn.gelu(_tlin(h, h1_w, h1_s), approximate=False)
        h = jax.nn.gelu(_tlin(h, h2_w, h2_s), approximate=False)
        return _tlin(h, w3_w, w3_s)
    x = L0_attn_a_x
    x = x + _L0_attn_a_ref(_layernorm(x, axis=-1), L0_attn_a_ln_g, L0_attn_a_ln_b, L0_attn_a_w_qkv, L0_attn_a_b_qkv, L0_attn_a_w_rel, L0_attn_a_w_out, L0_attn_a_b_out)
    x = x + _L0_ffn_ref(_layernorm(x, axis=-1), L0_ffn_router_w, L0_ffn_w13, L0_ffn_w2)
    x = x + _L0_attn_b_ref(_layernorm(x, axis=-1), L0_attn_b_rms_w, L0_attn_b_in_W, L0_attn_b_in_b, L0_attn_b_conv_w, L0_attn_b_conv_b, L0_attn_b_A_log, L0_attn_b_dbc_W, L0_attn_b_dbc_b, L0_attn_b_dup_W, L0_attn_b_dup_b, L0_attn_b_out_W, L0_attn_b_out_b)
    x = x + _L0_ffn_ref(_layernorm(x, axis=-1), L0_ffn_router_w, L0_ffn_w13, L0_ffn_w2)
    x = x + _L1_attn_a_ref(_layernorm(x, axis=-1), L1_attn_a_Wq, L1_attn_a_bq, L1_attn_a_Wk, L1_attn_a_bk, L1_attn_a_Wv, L1_attn_a_bv, L1_attn_a_Wg, L1_attn_a_bg, L1_attn_a_Wo, L1_attn_a_bo)
    x = x + _L1_ffn_ref(_layernorm(x, axis=-1), L1_ffn_w1_w, L1_ffn_w1_s, L1_ffn_w2_w, L1_ffn_w2_s, L1_ffn_h1_w, L1_ffn_h1_s, L1_ffn_h2_w, L1_ffn_h2_s, L1_ffn_w3_w, L1_ffn_w3_s)
    x = x + _L1_attn_b_ref(_layernorm(x, axis=-1), L1_attn_b_q_proj_w, L1_attn_b_k_proj_w, L1_attn_b_v_proj_w, L1_attn_b_b_proj_w, L1_attn_b_q_conv_w, L1_attn_b_k_conv_w, L1_attn_b_v_conv_w, L1_attn_b_fir_w3, L1_attn_b_fir_w7, L1_attn_b_fir_w15, L1_attn_b_fir_w31, L1_attn_b_gate_w1, L1_attn_b_gate_b1, L1_attn_b_gate_w2, L1_attn_b_gate_b2, L1_attn_b_gate_log_temp, L1_attn_b_alpha_stat, L1_attn_b_o_norm_w, L1_attn_b_o_proj_w)
    x = x + _L1_ffn_ref(_layernorm(x, axis=-1), L1_ffn_w1_w, L1_ffn_w1_s, L1_ffn_w2_w, L1_ffn_w2_s, L1_ffn_h1_w, L1_ffn_h1_s, L1_ffn_h2_w, L1_ffn_h2_s, L1_ffn_w3_w, L1_ffn_w3_s)
    return x

_drawn_inputs = setup_inputs


def setup_inputs(seed=0):
    import zlib

    import numpy as np

    out = dict(_drawn_inputs(seed))
    spreads = {'L0_attn_a_ln_g': (1.0, 0.2),
     'L0_attn_a_ln_b': (0.0, 0.1),
     'L0_attn_a_b_qkv': (0.0, 0.1),
     'L0_attn_a_b_out': (0.0, 0.1),
     'L0_attn_b_rms_w': (1.0, 0.2),
     'L1_attn_a_bq': (0.0, 0.1),
     'L1_attn_a_bk': (0.0, 0.1),
     'L1_attn_a_bv': (0.0, 0.1),
     'L1_attn_a_bg': (0.0, 0.1),
     'L1_attn_a_bo': (0.0, 0.1),
     'L1_attn_b_gate_b1': (0.0, 0.1),
     'L1_attn_b_gate_log_temp': (1.0, 0.2),
     'L1_attn_b_alpha_stat': (0.10000000149011612, 0.2),
     'L1_attn_b_o_norm_w': (1.0, 0.2)}
    factors = {}
    for name, (base, spread) in spreads.items():
        noise = np.random.default_rng([zlib.crc32(name.encode()), seed]).standard_normal(out[name].shape)
        drawn = base * np.exp(spread * noise) if base else spread * noise
        out[name] = jnp.asarray(drawn.astype(out[name].dtype))
    for name, factor in factors.items():
        out[name] = (out[name] * factor).astype(out[name].dtype)
    return out
```

```python
from contextlib import ExitStack
import math

import numpy as np

import concourse.bass as bass
from concourse import mybir

F32 = mybir.dt.float32
BF16 = mybir.dt.bfloat16
I32 = mybir.dt.int32
U32 = mybir.dt.uint32
ALU = mybir.AluOpType
ACT = mybir.ActivationFunctionType
AX_X = mybir.AxisListType.X

P = 128
B, T, D = 4, 1024, 128
TILES = B * T // P
TPB = T // P
BANK = 512
CHUNKS = B * T // BANK
TPC = BANK // P
LN_EPS = 1e-5


class Engine:

    def __init__(self, name, sem):
        self.name, self.sem, self.count = name, sem, 0
        self.steps, self.last, self.seen = [], None, {}

    def op(self, build):
        self.last = [build, None, 0]
        self.steps.append(self.last)

    def matmul(self, *args, **options):
        self.op(lambda e: e.matmul(*args, **options))

    def transpose(self, *args, **options):
        self.op(lambda e: e.transpose(*args, **options))

    def activation(self, *args, **options):
        self.op(lambda e: e.activation(*args, **options))

    def copy(self, *args, **options):
        self.op(lambda e: e.copy(*args, **options))

    def tensor_copy(self, *args, **options):
        self.op(lambda e: e.tensor_copy(*args, **options))

    def tensor_tensor(self, *args, **options):
        self.op(lambda e: e.tensor_tensor(*args, **options))

    def tensor_scalar(self, *args, **options):
        self.op(lambda e: e.tensor_scalar(*args, **options))

    def scalar_tensor_tensor(self, *args, **options):
        self.op(lambda e: e.scalar_tensor_tensor(*args, **options))

    def tensor_tensor_scan(self, *args, **options):
        self.op(lambda e: e.tensor_tensor_scan(*args, **options))

    def tensor_reduce(self, *args, **options):
        self.op(lambda e: e.tensor_reduce(*args, **options))

    def reciprocal(self, *args, **options):
        self.op(lambda e: e.reciprocal(*args, **options))

    def memset(self, *args, **options):
        self.op(lambda e: e.memset(*args, **options))

    def bn_stats(self, *args, **options):
        self.op(lambda e: e.bn_stats(*args, **options))

    def bn_aggr(self, *args, **options):
        self.op(lambda e: e.bn_aggr(*args, **options))

    def max(self, *args, **options):
        self.op(lambda e: e.max(*args, **options))

    def match_replace(self, *args, **options):
        self.op(lambda e: e.match_replace(*args, **options))

    def mark(self):
        if self.last[1] is None:
            self.count += 1
            self.last[1], self.last[2] = self.sem, 1
        return (self.name, self.sem, self.count)

    def wait(self, *marks):
        for name, sem, value in marks:
            if self.seen.get(name, 0) < value:
                self.seen[name] = value
                self.steps.append([None, sem, value])

    def settle(self):
        self.wait(self.mark())

    def dma(self, landing, out, in_):
        landing.count += 16
        self.steps.append([lambda e: e.dma_start(out, in_), landing.sem, 16])

    def gather(self, landing, out, table, rows):
        landing.count += 16
        self.steps.append([lambda e: e.indirect_dma_start(
            out, None, table, bass.IndirectOffsetOnAxis(rows, 0)), landing.sem, 16])

    def play(self, engine):
        for build, sem, value in self.steps:
            if build is None:
                engine.wait_ge(sem, value)
                continue
            made = build(engine)
            if sem is not None:
                made.then_inc(sem, value)


class Chained:

    def __init__(self, engine):
        self.engine = engine

    def tensor_tensor(self, *args):
        self.engine.tensor_tensor(*args)
        self.engine.settle()

    def tensor_scalar(self, *args):
        self.engine.tensor_scalar(*args)
        self.engine.settle()

    def scalar_tensor_tensor(self, *args):
        self.engine.scalar_tensor_tensor(*args)
        self.engine.settle()

    def tensor_reduce(self, *args):
        self.engine.tensor_reduce(*args)
        self.engine.settle()

    def tensor_copy(self, *args):
        self.engine.tensor_copy(*args)
        self.engine.settle()

    def reciprocal(self, *args):
        self.engine.reciprocal(*args)
        self.engine.settle()


class Landing:

    def __init__(self, name, sem):
        self.name, self.sem, self.count = name, sem, 0

    def landed(self):
        return (self.name, self.sem, self.count)


class Ring:

    def __init__(self, slots):
        self.slots, self.at = slots, 0
        self.readers = [() for _ in slots]

    def take(self):
        i = self.at % len(self.slots)
        self.at += 1
        return i, self.slots[i], self.readers[i]

    def release(self, i, *marks):
        self.readers[i] = marks


class Stage:

    def __init__(self, nc, net, name):
        self.nc, self.net, self.name, self.stack = nc, net, name, ExitStack()
        self.landings = []
        self.pe = Engine(name + "_pe", nc.alloc_semaphore(name + "_pe"))
        self.act = Engine(name + "_act", nc.alloc_semaphore(name + "_act"))
        self.dve = Engine(name + "_dve", nc.alloc_semaphore(name + "_dve"))
        self.pool = Engine(name + "_pool", nc.alloc_semaphore(name + "_pool"))
        self.sp = Engine(name + "_sp", None)
        for engine in (self.pe, self.act, self.dve, self.pool, self.sp):
            engine.wait(*net.done)

    def sbuf(self, name, shape, dtype=F32):
        return self.stack.enter_context(self.nc.sbuf_tensor(self.name + "_" + name, shape, dtype))

    def psum(self, name, shape, dtype=F32):
        return self.stack.enter_context(self.nc.psum_tensor(self.name + "_" + name, shape, dtype))

    def landing(self, name):
        self.landings.append(Landing(self.name + name, self.nc.alloc_semaphore(self.name + "_" + name)))
        return self.landings[-1]

    def close(self):
        self.net.done = [e.mark() for e in (self.pe, self.act, self.dve, self.pool) if e.last]
        self.net.done += [landing.landed() for landing in self.landings]
        with self.nc.Block() as block:
            @block.tensor
            def _(e):
                self.pe.play(e)

            @block.scalar
            def _(e):
                self.act.play(e)

            @block.vector
            def _(e):
                self.dve.play(e)

            @block.gpsimd
            def _(e):
                self.pool.play(e)

            @block.sync
            def _(e):
                self.sp.play(e)
        self.stack.close()


def layer_norm(s, net, xn, second_eps=None, twice=None):
    x = net.residual
    stats = s.sbuf("ln_stats", [P, TILES, 6])
    moments = s.sbuf("ln_moments", [P, TILES, 2])
    std = s.sbuf("ln_std", [P, TILES])
    inv = s.sbuf("ln_inv", [P, TILES])
    eps = s.sbuf("ln_eps", [P, 2])
    s.dve.memset(eps[:, 0:1], LN_EPS)
    s.dve.memset(eps[:, 1:2], second_eps or 0.0)
    for t in range(TILES):
        s.dve.bn_stats(stats[:, t, :], x[:, t, :])
    s.dve.settle()
    for t in range(TILES):
        s.dve.bn_aggr(moments[:, t, :], stats[:, t, :])
    var = moments[:, :, 1]
    s.act.wait(s.dve.mark())
    s.act.activation(std[:], var, ACT.Sqrt, bias=eps[:, 0:1])
    s.dve.wait(s.act.mark())
    s.dve.reciprocal(inv[:], std[:])
    s.dve.settle()
    if second_eps is not None:
        ratio = s.sbuf("ln_ratio", [P, TILES])
        factor = s.sbuf("ln_factor", [P, TILES])
        step = Chained(s.dve)
        step.tensor_tensor(ratio[:], var, inv[:], ALU.mult)
        step.tensor_tensor(std[:], ratio[:], inv[:], ALU.mult)
        s.act.wait(s.dve.mark())
        s.act.activation(ratio[:], std[:], ACT.Sqrt, bias=eps[:, 1:2])
        s.dve.wait(s.act.mark())
        step.reciprocal(factor[:], ratio[:])
        if twice is xn:
            step.tensor_tensor(inv[:], inv[:], factor[:], ALU.mult)
    marks = []
    for t in range(TILES):
        s.dve.tensor_scalar(xn[:, t, :], x[:, t, :], moments[:, t, 0:1], inv[:, t:t + 1],
                            ALU.subtract, ALU.mult)
        if t % TPC == TPC - 1:
            marks += [s.dve.mark()] * TPC
    if second_eps is not None and twice is not xn:
        for t in range(TILES):
            s.dve.wait(marks[t])
            s.dve.tensor_scalar(twice[:, t, :], xn[:, t, :], factor[:, t:t + 1], None, ALU.mult)
            marks[t] = s.dve.mark()
    return marks


def to_feature_major(s, net, ring, xn, marks, xT, gain=None, shift=None):
    done = []
    for c in range(CHUNKS):
        i, bank, readers = ring.take()
        s.pe.wait(*readers, marks[TPC * c + TPC - 1])
        for j in range(TPC):
            s.pe.transpose(bank[:, j * P:(j + 1) * P],
                                                               xn[:, TPC * c + j, :], net.ident[:])
        s.act.wait(s.pe.mark())
        out = xT[:, c * BANK:(c + 1) * BANK]
        if gain is None:
            s.act.copy(out, bank)
        elif shift is None:
            s.act.activation(out, bank, ACT.Copy, scale=gain)
        else:
            s.act.activation(out, bank, ACT.Identity, bias=shift,
                                                                scale=gain)
        done.append(s.act.mark())
        ring.release(i, s.act.mark())
    return done


def banks(psum, n, first=0):
    return [psum[:, i, :] for i in range(first, first + n)]


HEADS = 16
HD = D // HEADS
SPLITS = 3
TERMS = ((0, 0), (0, 1), (1, 0), (1, 1), (0, 2), (2, 0))
QROWS = HD * len(TERMS)
GROUP = 4
GROUPS = HEADS // GROUP
STACKS = 3


def split_parts(engine, value, rest, parts):
    step = Chained(engine)
    step.tensor_copy(parts[0], value)
    step.tensor_tensor(rest, value, parts[0], ALU.subtract)
    step.tensor_copy(parts[1], rest)
    step.tensor_tensor(parts[2], rest, parts[1], ALU.subtract)


class Heads:

    def __init__(self, s, scratch, with_v=True):
        self.s, self.scratch = s, scratch
        self.value = s.sbuf("hv", [P, 2, T])
        self.rest = s.sbuf("hr", [P, T])
        self.parts = s.sbuf("hp", [P, 2 * SPLITS, T], BF16)
        self.stored = [s.landing("parts%d" % i) for i in range(2)]
        self.free = ((), ())
        self.parts_free = [(), ()]

    def project(self, b, ring, weights, bias, scale, xT, ready):
        s = self.s
        for n in range(2):
            for half in range(T // BANK):
                i, bank, readers = ring.take()
                s.pe.wait(*readers, ready[b * (T // BANK) + half])
                s.pe.matmul(bank, weights[:, n * P:(n + 1) * P],
                            xT[:, b * T + half * BANK:b * T + (half + 1) * BANK], start=True, stop=True)
                s.act.wait(s.pe.mark(), *self.free[n])
                s.act.activation(self.value[:, n, half * BANK:(half + 1) * BANK], bank, ACT.Identity,
                                 bias=bias[:, n:n + 1], scale=scale if n == 0 else 1.0)
                ring.release(i, s.act.mark())
        s.pool.wait(s.act.mark())
        marks = []
        for n in range(2):
            s.pool.wait(*self.parts_free[n])
            parts = [self.parts[:, SPLITS * n + i, :] for i in range(SPLITS)]
            split_parts(s.pool, self.value[:, n, :], self.rest[:], parts)
            marks.append((s.pool.mark(),))
            s.sp.wait(s.pool.mark())
            s.sp.dma(self.stored[n], self.scratch[b, n].rearrange("s p t -> p s t"),
                     self.parts[:, SPLITS * n:SPLITS * (n + 1), :])
            self.parts_free[n] = (self.stored[n].landed(),)
        self.free = marks


def attention_stage(nc, net):
    s = Stage(nc, net, "attn")
    dram = net.dram
    pe, act, dve, pool, sp = s.pe, s.act, s.dve, s.pool, s.sp
    BROW = QROWS
    MROW = 2 * QROWS
    ROWS = MROW + 2
    scratch = nc.dram_tensor("attn_parts", (B, 2, SPLITS, P, T), BF16, kind="Internal").ap()
    phi_dram = nc.dram_tensor("attn_phi", (SPLITS, P, T), BF16, kind="Internal").ap()

    w_qkv = s.sbuf("w_qkv", [P, 3 * D])
    w_out = s.sbuf("w_out", [P, D])
    bias_qk = s.sbuf("bias_qk", [P, 2])
    bias_v = s.sbuf("bias_v", [1, D])
    bias_out = s.sbuf("bias_out", [1, D])
    gain = s.sbuf("gain", [P, 2])
    w_rel = s.sbuf("w_rel", [P, 2])
    ones = s.sbuf("ones", [1, P])
    loads = s.landing("loads")
    sp.dma(loads, w_qkv[:], dram["a_qkv"])
    sp.dma(loads, w_out[:], dram["a_out"])
    sp.dma(loads, bias_qk[:], dram["a_bqk"])
    sp.dma(loads, bias_v[:], dram["a_bv"])
    sp.dma(loads, bias_out[:], dram["a_bout"])
    sp.dma(loads, gain[:], dram["a_gain"])
    sp.dma(loads, w_rel[:], dram["a_rel"])
    select = s.sbuf("select", [P, 2, 32])
    sp.dma(loads, select[:], dram["head_select"])
    ident_bf = s.sbuf("ident_bf", [P, P], BF16)

    q_stack = s.sbuf("q_stack", [P, STACKS, GROUP, T], BF16)
    k_stack = s.sbuf("k_stack", [P, STACKS, GROUP, T], BF16)
    values = s.sbuf("values", [P, 2, TPB, HEADS, HD + 1])
    xT = s.sbuf("xT", [P, B * T])
    ps = s.psum("ps", [P, 8, BANK])
    key_ring = Ring(banks(ps, 3))
    score_ring = Ring(banks(ps, 3, 3))
    out_acc = ps[:, 6:8, :]
    scale = HD ** -0.5
    constants_in = s.landing("constants")
    for slot in range(STACKS):
        for h in range(GROUP):
            sp.dma(constants_in, k_stack[BROW:ROWS, slot, h, :], dram["psi"])

    weights_sb = s.sbuf("weights", [P, 2, GROUP, BANK])
    xn = weights_sb[:].rearrange("p a h (t d) -> p (a h t) d", d=P)
    marks = layer_norm(s, net, xn, LN_EPS, xn)
    act.wait(loads.landed())
    ready = to_feature_major(s, net, Ring(banks(ps, 8)), xn, marks, xT, gain[:, 0:1], gain[:, 1:2])
    after_ln = (ready[-1], pe.mark())
    pool.wait(*after_ln)
    dve.wait(*after_ln)

    tables = s.sbuf("tables", [P, 2, T])
    sp.wait(*after_ln)
    table_in = s.landing("tables")
    sp.dma(table_in, tables[:], dram["tables"])
    heads = Heads(s, scratch)
    dve.wait(table_in.landed(), loads.landed())
    step = Chained(dve)
    phi = tables[:, 1, :]
    step.tensor_scalar(tables[:, 0, :], tables[:, 0, :], w_rel[:, 0:1], None, ALU.mult)
    step.scalar_tensor_tensor(phi, phi, w_rel[:, 1:2], tables[:, 0, :], ALU.mult, ALU.add)
    phi_parts = [q_stack[:, 0, i, :] for i in range(SPLITS)]
    split_parts(dve, phi, tables[:, 0, :], phi_parts)
    sp.wait(dve.mark())
    phi_stored = s.landing("phi")
    sp.dma(phi_stored, phi_dram.rearrange("s p t -> p s t"), q_stack[:, 0, 0:SPLITS, :])
    step.tensor_scalar(bias_qk[:, 0:1], bias_qk[:, 0:1], scale, None, ALU.mult)
    dve.tensor_copy(ident_bf[:], net.ident[:])
    dve.memset(values[:, :, :, :, HD], 1.0)
    dve.memset(ones[:], 1.0)
    dve.memset(out_acc, 0.0)
    start = dve.mark()
    act.wait(start)
    pe.wait(start, loads.landed())

    value_free = [(), ()]

    def prepare(b):
        heads.project(b, key_ring, w_qkv, bias_qk, scale, xT, ready)
        act.wait(*value_free[b % 2])
        for c in range(T // BANK):
            i, bank, readers = key_ring.take()
            pe.wait(*readers)
            for j in range(TPC):
                cols = bank[:, j * P:(j + 1) * P]
                token = b * T + (TPC * c + j) * P
                pe.matmul(cols, xT[:, token:token + P], w_qkv[:, 2 * D:3 * D], start=True, stop=False)
                pe.matmul(cols, ones[:], bias_v[:], start=False, stop=True)
            act.wait(pe.mark())
            act.copy(values[:, b % 2, TPC * c:TPC * (c + 1), :, 0:HD],
                     bank.rearrange("p (j h d) -> p j h d", j=TPC, h=HEADS))
            key_ring.release(i, act.mark())
        return act.mark()

    stack_in = [s.landing("stack%d" % i) for i in range(STACKS)]
    stack_free = [() for _ in range(STACKS)]

    def assemble(g):
        b, first, slot = g // GROUPS, GROUP * (g % GROUPS), g % STACKS
        sp.wait(phi_stored.landed(), constants_in.landed(), *stack_free[slot])
        sp.wait(*heads.parts_free[0], *heads.parts_free[1])
        rows = slice(first * HD, (first + GROUP) * HD)
        for i, (qpart, kpart) in enumerate(TERMS):
            at = slice(HD * i, HD * (i + 1))
            bias_at = slice(BROW + HD * i, BROW + HD * (i + 1))
            for stack, where, source in ((q_stack, at, scratch[b, 0, qpart, rows, :]),
                                         (k_stack, at, scratch[b, 1, kpart, rows, :]),
                                         (q_stack, bias_at, phi_dram[qpart, rows, :])):
                sp.dma(stack_in[slot], stack[where, slot, :, :],
                       source.rearrange("(h d) t -> d h t", d=HD))

    peak_halves = s.sbuf("peak_halves", [P, STACKS, T // BANK, TPB * GROUP])
    peak = s.sbuf("peak", [P, STACKS, TPB * GROUP])
    peak_parts = s.sbuf("peak_parts", [P, STACKS, TPB, 2 * GROUP], BF16)
    peak_rows = s.sbuf("peak_rows", [2 * GROUP, STACKS, T], BF16)
    peaks_in = [s.landing("peaks%d" % i) for i in range(STACKS)]
    peak_free = [() for _ in range(STACKS)]

    def score(g, unit):
        half, h, t, slot = unit % 2, unit // 2 % GROUP, unit // (2 * GROUP), g % STACKS
        if unit == 0:
            pe.wait(stack_in[slot].landed())
            dve.wait(*peak_free[slot])
        i, bank, readers = score_ring.take()
        pe.wait(*readers)
        pe.matmul(bank, q_stack[0:MROW, slot, h, t * P:(t + 1) * P],
                  k_stack[0:MROW, slot, h, half * BANK:(half + 1) * BANK], start=True, stop=True)
        dve.wait(pe.mark())
        at = t * GROUP + h
        dve.tensor_reduce(peak_halves[:, slot, half, at:at + 1], bank, AX_X, ALU.max)
        score_ring.release(i, dve.mark())

    def peaks(g):
        slot = g % STACKS
        parts = peak_parts[:, slot].rearrange("p t (h s) -> p (t h) s", s=2)
        dve.settle()
        dve.tensor_tensor(peak[:, slot], peak_halves[:, slot, 0], peak_halves[:, slot, 1], ALU.max)
        dve.settle()
        dve.tensor_scalar(parts[:, :, 0], peak[:, slot], -1.0, None, ALU.mult)
        dve.settle()
        dve.scalar_tensor_tensor(parts[:, :, 1], peak[:, slot], -1.0, parts[:, :, 0], ALU.mult,
                                 ALU.subtract)
        pe.wait(dve.mark())
        for half in range(T // BANK):
            i, bank, readers = key_ring.take()
            pe.wait(*readers)
            for j in range(TPC):
                pe.matmul(bank[0:2 * GROUP, j * P:(j + 1) * P], peak_parts[:, slot, TPC * half + j, :],
                          ident_bf[:], start=True, stop=True)
            act.wait(pe.mark())
            act.copy(peak_rows[:, slot, half * BANK:(half + 1) * BANK], bank[0:2 * GROUP, :])
            key_ring.release(i, act.mark())
        sp.wait(act.mark())
        for h in range(GROUP):
            sp.dma(peaks_in[slot], q_stack[MROW:ROWS, slot, h, :],
                   peak_rows[2 * h:2 * h + 2, slot, :])
        peak_free[slot] = (pe.mark(), peaks_in[slot].landed())

    weight_ring = Ring([weights_sb[:, i] for i in range(2)])
    acc_free = [()]

    def exponentials(g, key_tile, half, between):
        slot = g % STACKS
        if key_tile == 0 and half == 0:
            pe.wait(peaks_in[slot].landed())
        w, weights, free = weight_ring.take()
        marks = []
        for h in range(GROUP):
            i, bank, readers = key_ring.take()
            pe.wait(*readers)
            pe.matmul(bank, k_stack[0:ROWS, slot, h, key_tile * P:(key_tile + 1) * P],
                      q_stack[0:ROWS, slot, h, half * BANK:(half + 1) * BANK], start=True, stop=True)
            act.wait(pe.mark(), *free)
            act.activation(weights[:, h, :], bank, ACT.Exp)
            key_ring.release(i, act.mark())
            last = act.mark()
            between(h)
        if key_tile == TPB - 1 and half == T // BANK - 1:
            stack_free[slot] = (pe.mark(),)
        return w, weights, last

    def weigh(g, key_tile, half, w, weights, mark):
        b, first = g // GROUPS, GROUP * (g % GROUPS)
        pe.wait(mark, *acc_free[0])
        for h in range(GROUP):
            pe.matmul(out_acc[32 * h:32 * h + HD + 1, half, :], values[:, b % 2, key_tile, first + h, :],
                      weights[:, h, :], start=key_tile == 0, stop=key_tile == TPB - 1)
        weight_ring.release(w, pe.mark())
        if key_tile == TPB - 1 and half == T // BANK - 1:
            act.wait(pe.mark())
            act.copy(sums[:, g % GROUPS, :], out_acc.rearrange("p c t -> p (c t)"))
            acc_free[0] = (act.mark(),)
            if g % GROUPS == GROUPS - 1:
                value_free[b % 2] = (pe.mark(),)
                sums_ready[0] = act.mark()

    sums = s.sbuf("sums", [P, GROUPS, T])
    sums_ready = [None]
    inverse = s.sbuf("inverse", [P, BANK])
    mixed = s.sbuf("mixed", [P, 2, BANK])
    mixed_free = [(), ()]

    def project_out(b, half):
        pe.wait(sums_ready[0])
        found = []
        for what in range(2):
            i, bank, readers = key_ring.take()
            pe.wait(*readers)
            for group in range(GROUPS):
                pe.matmul(bank[32 * group:32 * (group + 1), :], select[:, what, :],
                          sums[:, group, half * BANK:(half + 1) * BANK], start=True, stop=True)
            found.append((i, bank))
        dve.wait(pe.mark(), *mixed_free[half])
        dve.reciprocal(inverse[:], found[1][1])
        dve.settle()
        dve.tensor_tensor(mixed[:, half, :], found[0][1], inverse[:], ALU.mult)
        key_ring.release(found[0][0], dve.mark())
        key_ring.release(found[1][0], dve.mark())
        i, bank, readers = key_ring.take()
        pe.wait(dve.mark(), *readers)
        for j in range(TPC):
            cols = bank[:, j * P:(j + 1) * P]
            pe.matmul(cols, mixed[:, half, j * P:(j + 1) * P], w_out[:], start=True, stop=False)
            pe.matmul(cols, ones[:], bias_out[:], start=False, stop=True)
        mixed_free[half] = (pe.mark(),)
        dve.wait(pe.mark())
        tile = b * TPB + half * TPC
        x = net.residual[:, tile:tile + TPC, :].rearrange("p t d -> p (t d)")
        dve.tensor_tensor(x, bank, x, ALU.add)
        key_ring.release(i, dve.mark())

    units = GROUP * TPB * T // BANK
    total = B * GROUPS
    value_ready = [prepare(0)]
    assemble(0)
    assemble(1)
    for unit in range(units):
        score(0, unit)
    peaks(0)
    pending = []
    steps = [(k, half) for k in range(TPB) for half in range(T // BANK)]
    ahead = len(steps) - 3
    for g in range(total):
        b = g // GROUPS
        if g + 2 < total:
            assemble(g + 2)
        if g % GROUPS == 1 and b + 1 < B:
            value_ready.append(prepare(b + 1))
        done = 0
        for n, (key_tile, half) in enumerate(steps):
            def between(h):
                nonlocal done
                goal = min(units, (GROUP * n + h + 1) * units // (GROUP * ahead))
                while g + 1 < total and done < goal:
                    score(g + 1, done)
                    done += 1
            made = exponentials(g, key_tile, half, between)
            if pending:
                weigh(*pending.pop())
            if g % GROUPS == 0 and n == 0:
                pe.wait(value_ready[b])
            pending.append((g, key_tile, half) + made)
            if n in (3, 6) and g and g % GROUPS == 0:
                project_out(b - 1, n // 6)
            if g + 1 < total and n == ahead:
                peaks(g + 1)
    weigh(*pending.pop())
    project_out(B - 1, 0)
    project_out(B - 1, 1)
    s.close()


EXPERTS, HIDDEN_E = 8, 256
EB = HIDDEN_E // P


def moe_stage(nc, net, name):
    s = Stage(nc, net, name)
    xn = s.sbuf("xn", [P, TILES, P])
    xT = s.sbuf("xT", [P, B * T])
    probs = s.sbuf("probs", [P, TILES, EXPERTS])
    left = s.sbuf("left", [P, TILES, EXPERTS])
    key = s.sbuf("key", [P, TILES, EXPERTS])
    chosen = s.sbuf("chosen", [P, TILES, EXPERTS])
    weights = s.sbuf("weights", [P, TILES, EXPERTS])
    best = s.sbuf("best", [P, TILES])
    total = s.sbuf("total", [P, TILES])
    gate_sb = s.sbuf("gate", [P, 3, BANK])
    hidden = s.sbuf("hidden", [P, 4, BANK])
    w13 = s.sbuf("w13", [P, EXPERTS, 2 * HIDDEN_E])
    w2 = s.sbuf("w2", [P, EXPERTS, EB, P])
    loads = s.landing("loads")
    s.sp.dma(loads, w13[:], net.dram["w13"].rearrange("e d i -> d e i"))
    s.sp.dma(loads, w2[:], net.dram["w2"].rearrange("e (k i) d -> i e k d", i=P))
    ps = s.psum("ps", [P, 8, BANK])
    pe, act, dve = s.pe, s.act, s.dve
    ring = Ring(banks(ps, 2))
    marks = layer_norm(s, net, xn)
    ready = to_feature_major(s, net, ring, xn, marks, xT)

    logits = ps[:, 7, 0:TILES * EXPERTS].rearrange("p (t e) -> p t e", e=EXPERTS)
    for t in range(TILES):
        pe.wait(ready[t // TPC])
        pe.matmul(logits[:, t, :], xT[:, t * P:(t + 1) * P], net.router[:],
                                      start=True, stop=True)
    dve.wait(pe.mark())
    wide = lambda a: a[:].unsqueeze(2).broadcast_to([P, TILES, EXPERTS])

    step = Chained(dve)
    step.tensor_reduce(best[:], logits, AX_X, ALU.max)
    step.tensor_tensor(left[:], logits, wide(best), ALU.subtract)
    logits_read = dve.mark()
    act.wait(dve.mark())
    act.activation(key[:], left[:], ACT.Exp)
    dve.wait(act.mark())
    step.tensor_reduce(total[:], key[:], AX_X, ALU.add)
    step.reciprocal(best[:], total[:])
    step.tensor_tensor(probs[:], key[:], wide(best), ALU.mult)

    rank = net.expert_rank[:].unsqueeze(1).broadcast_to([P, TILES, EXPERTS])

    def take_best(source, into, top):
        step.tensor_reduce(top[:], source[:], AX_X, ALU.max)
        step.tensor_tensor(key[:], source[:], wide(top), ALU.is_equal)
        step.tensor_tensor(key[:], key[:], rank, ALU.mult)
        step.tensor_reduce(best[:], key[:], AX_X, ALU.max)
        step.tensor_tensor(into[:], key[:], wide(best), ALU.is_equal)
    second = s.sbuf("second", [P, TILES])
    take_best(probs, chosen, total)
    step.scalar_tensor_tensor(left[:], chosen[:], -2.0, probs[:], ALU.mult, ALU.add)
    take_best(left, weights, second)
    step.tensor_tensor(chosen[:], chosen[:], weights[:], ALU.add)
    step.tensor_tensor(chosen[:], chosen[:], probs[:], ALU.mult)
    step.scalar_tensor_tensor(best[:], total[:], 1e-6, second[:], ALU.add, ALU.add)
    step.reciprocal(total[:], best[:])
    step.tensor_tensor(weights[:], chosen[:], wide(total), ALU.mult)

    pairs = Ring([(ps[:, 2 * i, :], ps[:, 2 * i + 1, :]) for i in range(3)])
    for i in range(2):
        pairs.release(0, *ring.readers[0], *ring.readers[1])
    outs = Ring([ps[:, 6, :], ps[:, 7, :]])
    outs.release(1, logits_read)
    gates = Ring([gate_sb[:, i, :] for i in range(3)])
    hiddens = Ring([(hidden[:, EB * i:EB * i + EB, :]) for i in range(2)])

    def down(e_, c, hs, h_slot, h_marks):
        i, out, readers = outs.take()
        pe.wait(*readers, *h_marks)
        for j in range(TPC):
            for k in range(EB):
                pe.matmul(out[:, j * P:(j + 1) * P],
                                                   hs[:, k, j * P:(j + 1) * P],
                                                   w2[:, e_, k, :], start=k == 0, stop=k == EB - 1)
        hiddens.release(h_slot, pe.mark())
        dve.wait(pe.mark(), *added.get(c, ()))
        for j in range(TPC):
            t = TPC * c + j
            x = net.residual[:, t, :]
            dve.scalar_tensor_tensor(
                x, out[:, j * P:(j + 1) * P], weights[:, t, e_:e_ + 1], x, ALU.mult, ALU.add)
        outs.release(i, dve.mark())
        added[c] = (dve.mark(),)

    pe.wait(loads.landed())
    added = {}
    waiting = None
    for c in range(CHUNKS):
        tokens = slice(c * BANK, (c + 1) * BANK)
        for e_ in range(EXPERTS):
            h_slot, hs, h_readers = hiddens.take()
            h_marks = []
            for k in range(EB):
                i, (gate, up), readers = pairs.take()
                pe.wait(*readers)
                for out, base in ((gate, 0), (up, HIDDEN_E)):
                    w = w13[:, e_, base + k * P:base + (k + 1) * P]
                    pe.matmul(out, w, xT[:, tokens], start=True, stop=True)
                g, gate_s, g_readers = gates.take()
                act.wait(pe.mark(), *g_readers)
                act.activation(gate_s, gate, ACT.Silu)
                dve.wait(act.mark(), *h_readers)
                dve.op(lambda e, o=hs[:, k, :], a=gate_s, u=up: e.tensor_tensor(o, u, a, ALU.mult))
                gates.release(g, dve.mark())
                pairs.release(i, dve.mark())
                h_marks.append(dve.mark())
            if waiting:
                down(*waiting)
            waiting = (e_, c, hs, h_slot, h_marks)
    down(*waiting)
    s.close()


CH, STATES, TAPS = 256, 16, 4
CB = CH // P
RANK = CH // 16
PER = P // STATES
SUBS = 32 // PER
RMS_EPS = 1e-6


def mamba_stage(nc, net):
    s = Stage(nc, net, "mamba")
    dram = net.dram
    pe, act, dve, pool, sp = s.pe, s.act, s.dve, s.pool, s.sp
    loads = s.landing("loads")

    def load(name, shape, dtype=F32):
        buffer = s.sbuf(name, shape, dtype)
        sp.dma(loads, buffer[:], dram["m_" + name])
        return buffer
    w_in = load("w_in", [P, 2 * CH])
    b_in = load("b_in", [P, 2 * CB])
    conv_w = load("conv_w", [P, CB, TAPS])
    conv_b = load("conv_b", [P, CB])
    rates = load("rates", [P, CH // PER])
    w_delta = load("w_delta", [P, CB, RANK])
    w_b = load("w_b", [P, CB, P])
    w_c = load("w_c", [P, CB, P])
    b_delta = load("b_delta", [RANK, 1])
    b_bc = load("b_bc", [P, 2])
    w_up = load("w_up", [RANK, CH])
    b_up = load("b_up", [P, CB])
    w_out = load("w_out", [P, CB, P])
    b_out = load("b_out", [1, P])
    gain = load("gain", [P, 1])
    spread = load("spread", [3 * 32, SUBS, P], BF16)
    gather = load("gather", [P, SUBS, 32])
    ones = s.sbuf("ones", [1, P])
    xT = s.sbuf("xT", [P, B * T])
    padded = s.sbuf("padded", [P, CB, TAPS - 1 + T])
    x1 = s.sbuf("x1", [P, CB, T])
    gate = s.sbuf("gate", [P, 2, CB, T])
    low = s.sbuf("low", [RANK, T])
    temp = s.sbuf("temp", [P, 2, T])
    parts = s.sbuf("parts", [P, SPLITS, CB, 2, T], BF16)
    stack = s.sbuf("stack", [3 * 32, CB, 2, 4, T], BF16)
    b_rep = s.sbuf("b_rep", [P, 2, T])
    c_rep = s.sbuf("c_rep", [P, 2, T])
    driven = s.sbuf("driven", [P, 2, T])
    states = s.sbuf("states", [P, 3, T])
    out_c = s.sbuf("out_c", [P, 6, T])
    ps = s.psum("ps", [P, 8, BANK])
    pair = lambda i: ps[:, i:i + 2, :].rearrange("p a t -> p (a t)")

    xn = x1_view = out_c[:, 0:4, :].rearrange("p a (t d) -> p (a t) d", d=P)
    twice = gate[:].rearrange("p a b (t d) -> p (a b t) d", d=P)
    marks = layer_norm(s, net, xn, RMS_EPS, twice)
    act.wait(loads.landed())
    pe.wait(loads.landed())
    ready = to_feature_major(s, net, Ring(banks(ps, 8)), twice, marks, xT, gain[:, 0:1])
    x = net.residual[:].rearrange("p t d -> p (t d)")
    dve.tensor_tensor(x, x, xn.rearrange("p t d -> p (t d)"), ALU.add)
    dve.settle()
    act.wait(ready[-1], pe.mark())
    pool.wait(dve.mark())
    act.activation(rates[:], rates[:], ACT.Exp)
    act.settle()
    act.activation(rates[:], rates[:], ACT.Copy, scale=-1.0)
    dve.memset(padded[:, :, 0:TAPS - 1], 0.0)
    dve.memset(ones[:], 1.0)
    dve.wait(loads.landed(), ready[-1])
    act.wait(dve.mark())
    pe.wait(dve.mark(), act.mark())

    steps_ring = Ring([(pair(0)), (pair(2))])
    input_ring = Ring([pair(4)])
    summed = pair(6)
    driven_ring = Ring([driven[:, i, :] for i in range(2)])
    state_ring = Ring([states[:, i, :] for i in range(3)])
    product_ring = Ring([out_c[:, i, :] for i in range(6)])
    stack_in = [s.landing("stack%d" % i) for i in range(CB)]
    free = {}

    def project(slot, weights, source, rows=P):
        for half in range(T // BANK):
            cols = slice(half * BANK, (half + 1) * BANK)
            for k in range(len(source)):
                pe.matmul(slot[0:rows, cols], weights[k], source[k][:, cols],
                          start=k == 0, stop=k == len(source) - 1)

    def channels(b):
        tokens = slice(b * T, (b + 1) * T)
        pe.wait(*free.get("gate", ()))
        for m in range(CB):
            i, slot, readers = steps_ring.take()
            pe.wait(*readers)
            project(slot, [w_in[:, m * P:(m + 1) * P]], [xT[:, tokens]])
            act.wait(pe.mark(), *free.get("padded", ()))
            act.activation(padded[:, m, TAPS - 1:], slot, ACT.Identity, bias=b_in[:, m:m + 1])
            steps_ring.release(i, act.mark())
            i, slot, readers = steps_ring.take()
            pe.wait(*readers)
            project(slot, [w_in[:, CH + m * P:CH + (m + 1) * P]], [xT[:, tokens]])
            act.wait(pe.mark(), *free.get(("gate", b % 2), ()))
            act.activation(gate[:, b % 2, m, :], slot, ACT.Silu, bias=b_in[:, CB + m:CB + m + 1])
            steps_ring.release(i, act.mark())
        dve.wait(act.mark(), *free.get("x1", ()))
        for m in range(CB):
            dve.tensor_scalar(x1[:, m, :], padded[:, m, 0:T], conv_w[:, m, 0:1], conv_b[:, m:m + 1],
                              ALU.mult, ALU.add)
        for k in range(1, TAPS):
            dve.settle()
            for m in range(CB):
                dve.scalar_tensor_tensor(x1[:, m, :], padded[:, m, k:k + T], conv_w[:, m, k:k + 1],
                                         x1[:, m, :], ALU.mult, ALU.add)
        free["padded"] = (dve.mark(),)
        act.wait(dve.mark())
        act.activation(x1[:], x1[:], ACT.Silu)
        pe.wait(act.mark())
        source = [x1[:, k, :] for k in range(CB)]
        i, slot, readers = steps_ring.take()
        pe.wait(*readers)
        project(slot, [w_delta[:, k, :] for k in range(CB)], source, RANK)
        act.wait(pe.mark(), *free.get("low", ()))
        act.activation(low[:], slot[0:RANK, :], ACT.Identity, bias=b_delta[:, 0:1])
        steps_ring.release(i, act.mark())
        x1_marks = [pe.mark()]
        pe.wait(act.mark())
        for n, (weights, into) in enumerate(((w_b, b_rep), (w_c, c_rep))):
            i, slot, readers = steps_ring.take()
            pe.wait(*readers)
            project(slot, [weights[:, k, :] for k in range(CB)], source)
            act.wait(pe.mark(), *free.get(("rep", b % 2), ()))
            act.activation(into[:, b % 2, :], slot, ACT.Identity, bias=b_bc[:, n:n + 1])
            steps_ring.release(i, act.mark())
        free["bc", b % 2] = act.mark()
        free["x1"] = (pe.mark(),)

    def step_sizes(b, m):
        i, slot, readers = steps_ring.take()
        pe.wait(*readers)
        project(slot, [w_up[:, m * P:(m + 1) * P]], [low[:]])
        free["low"] = (pe.mark(),)
        delta, other = temp[:, 0, :], temp[:, 1, :]
        act.wait(pe.mark(), *free.get("temp", ()))
        act.activation(other, slot, ACT.Abs, bias=b_up[:, m:m + 1])
        dve.wait(act.mark())
        dve.tensor_scalar(delta, slot, b_up[:, m:m + 1], 0.0, ALU.add, ALU.max)
        steps_ring.release(i, dve.mark())
        act.settle()
        act.activation(other, other, ACT.Exp, scale=-1.0)
        act.settle()
        act.activation(other, other, ACT.Ln, bias=1.0)
        dve.wait(act.mark())
        dve.settle()
        dve.tensor_tensor(delta, delta, other, ALU.add)
        dve.settle()
        dve.tensor_tensor(other, delta, x1[:, m, :], ALU.mult)
        free["x1"] += (dve.mark(),)
        into = lambda k, what: parts[:, k, m, what, :]
        for what, value in ((0, delta), (1, other)):
            act.wait(dve.mark(), *free.get(("parts", m), ()))
            act.copy(into(0, what), value)
            dve.wait(act.mark())
            dve.tensor_tensor(value, value, into(0, what), ALU.subtract)
            act.wait(dve.mark())
            act.copy(into(1, what), value)
            dve.wait(act.mark())
            dve.tensor_tensor(into(2, what), value, into(1, what), ALU.subtract)
        free["temp"] = (dve.mark(), act.mark())
        free["parts ready", m] = (dve.mark(), act.mark())

    def restack(m):
        sp.wait(*free["parts ready", m], *free.get(("stack", m), ()))
        for k in range(SPLITS):
            for q in range(4):
                sp.dma(stack_in[m], stack[32 * k:32 * (k + 1), m, :, q, :],
                       parts[32 * q:32 * (q + 1), k, m, :, :])
        free["parts", m] = (stack_in[m].landed(),)
        free["stacked", m] = stack_in[m].landed()

    def scan(b, m, sub, q):
        group = (m * P + 32 * q + PER * sub) // PER
        i, slot, readers = steps_ring.take()
        pe.wait(free["stacked", m], *readers)
        project(slot, [spread[:, sub, :]], [stack[:, m, 0, q, :]])
        act.wait(pe.mark())
        act.activation(slot, slot, ACT.Exp, scale=rates[:, group:group + 1])
        decays = act.mark()
        j, inputs, readers = input_ring.take()
        pe.wait(*readers)
        project(inputs, [spread[:, sub, :]], [stack[:, m, 1, q, :]])
        d, drive, readers = driven_ring.take()
        dve.wait(pe.mark(), *readers, free["bc", b % 2])
        dve.tensor_tensor(drive, inputs, b_rep[:, b % 2, :], ALU.mult)
        input_ring.release(j, dve.mark())
        k, state, readers = state_ring.take()
        dve.wait(decays, *readers)
        dve.settle()
        dve.tensor_tensor_scan(state, slot, drive, 0.0, ALU.mult, ALU.add)
        steps_ring.release(i, dve.mark())
        driven_ring.release(d, dve.mark())
        n, product, readers = product_ring.take()
        pool.wait(dve.mark(), *readers, free["bc", b % 2])
        pool.tensor_tensor(product, state, c_rep[:, b % 2, :], ALU.mult)
        state_ring.release(k, pool.mark())
        return n, product, pool.mark(), sub, q

    def sum_states(items):
        pe.wait(*free.get("summed", ()))
        for half in range(T // BANK):
            for n, product, mark, sub, q in items:
                pe.wait(mark)
                pe.matmul(summed[32 * q:32 * (q + 1), half * BANK:(half + 1) * BANK], gather[:, sub, :],
                          product[:, half * BANK:(half + 1) * BANK], start=sub == 0,
                          stop=sub == SUBS - 1)
        for n, *_ in items:
            product_ring.release(n, pe.mark())

    def gated(b, m):
        dve.wait(pe.mark())
        g = gate[:, b % 2, m, :]
        dve.tensor_tensor(g, summed, g, ALU.mult)
        free["summed"] = (dve.mark(),)

    def project_out(b):
        i, slot, readers = steps_ring.take()
        pe.wait(*free["summed"], *readers)
        for t in range(TPB):
            for k in range(CB):
                pe.matmul(slot[:, t * P:(t + 1) * P], gate[:, b % 2, k, t * P:(t + 1) * P],
                          w_out[:, k, :], start=k == 0, stop=False)
            pe.matmul(slot[:, t * P:(t + 1) * P], ones[:], b_out[:], start=False, stop=True)
        free["gate", b % 2] = (pe.mark(),)
        dve.wait(pe.mark())
        xb = x[:, b * T:(b + 1) * T]
        dve.tensor_tensor(xb, xb, slot, ALU.add)
        steps_ring.release(i, dve.mark())

    channels(0)
    for m in range(CB):
        step_sizes(0, m)
        restack(m)
    waiting = None
    for b in range(B):
        for m in range(CB):
            for sub in range(SUBS):
                items = [scan(b, m, sub, q) for q in range(2)]
                if waiting:
                    sum_states(waiting[0])
                    if waiting[1] is not None:
                        gated(*waiting[1])
                        if waiting[1][1] == CB - 1:
                            project_out(waiting[1][0])
                items += [scan(b, m, sub, q) for q in range(2, 4)]
                if sub == SUBS - 1:
                    free["stack", m] = (pe.mark(),)
                waiting = (items, (b, m) if sub == SUBS - 1 else None)
                if b + 1 < B and m == 1:
                    if sub == 0:
                        channels(b + 1)
                    elif sub == 1:
                        step_sizes(b + 1, 0)
                    elif sub == 2:
                        step_sizes(b + 1, 1)
                        restack(0)
            if b + 1 < B and m == 1:
                restack(1)
        free["rep", b % 2] = (dve.mark(), pool.mark())
    sum_states(waiting[0])
    gated(*waiting[1])
    project_out(B - 1)
    s.close()


WIDE = 512
WB = WIDE // P


def ffn_stage(nc, net, name):
    s = Stage(nc, net, name)
    xn = s.sbuf("xn", [P, TILES, P])
    xT = s.sbuf("xT", [P, B * T])
    gate_sb = s.sbuf("gate", [P, 2, BANK])
    layers = s.sbuf("layers", [P, 6, WB, BANK])
    ps = s.psum("ps", [P, 8, BANK])
    pe, act, dve = s.pe, s.act, s.dve
    ring = Ring(banks(ps, 8))
    marks = layer_norm(s, net, xn)
    ready = to_feature_major(s, net, ring, xn, marks, xT)
    gates = Ring([gate_sb[:, i, :] for i in range(2)])
    buffers = [Ring([layers[:, 2 * n + i] for i in range(2)]) for n in range(3)]
    w = net.ffn

    def first(c):
        slot, out, readers = buffers[0].take()
        tokens = slice(c * BANK, (c + 1) * BANK)
        for m in range(WB):
            i, a, ra = ring.take()
            j, b, rb = ring.take()
            pe.wait(*ra, *rb, ready[c])
            cols = slice(m * P, (m + 1) * P)
            pe.matmul(a, w.w1[:, cols], xT[:, tokens], start=True, stop=True)
            pe.matmul(b, w.w2[:, cols], xT[:, tokens], start=True, stop=True)
            g, gate, rg = gates.take()
            act.wait(pe.mark(), *rg)
            act.activation(gate, a, ACT.Silu, scale=w.s1[:, m:m + 1])
            ring.release(i, act.mark())
            dve.wait(act.mark(), *readers)
            dve.scalar_tensor_tensor(
                out[:, m, :], b, w.s2[:, m:m + 1], gate, ALU.mult, ALU.mult)
            gates.release(g, dve.mark())
            ring.release(j, dve.mark())
        return slot, out, dve.mark()

    def middle(n, weights, scale, src_slot, src, src_mark):
        slot, out, readers = buffers[n].take()
        pe.wait(src_mark)
        for m in range(WB):
            i, a, ra = ring.take()
            pe.wait(*ra)
            for k in range(WB):
                pe.matmul(a, weights[:, k, m * P:(m + 1) * P], src[:, k, :],
                                                        start=k == 0, stop=k == WB - 1)
            act.wait(pe.mark(), *readers)
            act.activation(out[:, m, :], a, ACT.Gelu, scale=scale[:, m:m + 1])
            ring.release(i, act.mark())
        buffers[n - 1].release(src_slot, pe.mark())
        return slot, out, act.mark()

    def last(c, src_slot, src, src_mark):
        i, a, ra = ring.take()
        pe.wait(src_mark, *ra)
        for j in range(TPC):
            for k in range(WB):
                pe.matmul(a[:, j * P:(j + 1) * P], src[:, k, j * P:(j + 1) * P],
                                                   w.w3[:, k, :], start=k == 0, stop=k == WB - 1)
        buffers[2].release(src_slot, pe.mark())
        dve.wait(pe.mark())
        x = net.residual[:, TPC * c:TPC * (c + 1), :].rearrange("p t d -> p (t d)")
        dve.tensor_tensor(x, a, x, ALU.add)
        ring.release(i, dve.mark())

    state = {}
    for step in range(CHUNKS + 3):
        if step < CHUNKS:
            state[0, step] = first(step)
        if 0 <= step - 1 < CHUNKS:
            state[1, step - 1] = middle(1, w.h1, w.h1s, *state[0, step - 1])
        if 0 <= step - 2 < CHUNKS:
            state[2, step - 2] = middle(2, w.h2, w.h2s, *state[1, step - 2])
        if 0 <= step - 3 < CHUNKS:
            last(step - 3, *state[2, step - 3])
    s.close()


BLOCK, PICKED = 32, 8
BLOCKS = T // BLOCK
SELECTED = BLOCK * PICKED
MASKED = -1e9


def sparse_stage(nc, net):
    s = Stage(nc, net, "sparse")
    dram = net.dram
    pe, act, dve, pool, sp = s.pe, s.act, s.dve, s.pool, s.sp
    FILL = 66
    ROWS = FILL + 4
    scale = HD ** -0.5
    HALVES = T // BANK
    SLOTS = 2
    scratch = nc.dram_tensor("sp_parts", (B, 2, SPLITS, P, T), BF16, kind="Internal").ap()
    picked_parts = nc.dram_tensor("sp_picked_parts", (B, SPLITS, P, SELECTED), BF16, kind="Internal").ap()
    tables = [nc.dram_tensor("sp_table%d" % b, (HEADS * BLOCKS, 2 * HD * BLOCK), F32, kind="Internal").ap()
              for b in range(B)]
    picked = nc.dram_tensor("sp_picked", (B, HEADS * PICKED, 2 * HD * BLOCK), F32, kind="Internal").ap()

    loads = s.landing("loads")

    def load(name, shape, dtype=F32, source=None):
        buffer = s.sbuf(name, shape, dtype)
        sp.dma(loads, buffer[:], dram["s_" + name] if source is None else source)
        return buffer
    w_qkv = load("w_qkv", [P, 3 * D])
    w_out = load("w_out", [P, D])
    w_gate = load("w_gate", [P, 3, P])
    b_gate = load("b_gate", [P, 3])
    b_qkv = load("b_qkv", [P, 3])
    b_v = load("b_v", [1, D])
    b_out = load("b_out", [1, D])
    select = load("select", [P, 2, 32], F32, dram["head_select"])
    own = load("own", [P, HEADS])
    block_ones = load("block_ones", [P, P])
    peak_spread = load("peak_spread", [2 * HEADS, GROUPS, P], BF16)
    row_base = load("row_base", [P, 1])
    mask_q = load("mask_q", [P, 2, P], BF16)
    mask_k = load("mask_k", [P, 2, P], BF16)
    ident_bf = s.sbuf("ident_bf", [P, P], BF16)
    ones = s.sbuf("ones", [1, P])

    q_stack = s.sbuf("q_stack", [P, SLOTS, GROUP, T], BF16)
    k_stack = s.sbuf("k_stack", [P, SLOTS, GROUP, T], BF16)
    p_stack = s.sbuf("p_stack", [P, SLOTS, GROUP, SELECTED], BF16)
    values = s.sbuf("values", [P, 2, TPB, HEADS, HD + 1])
    p_values = s.sbuf("p_values", [P, 2, SELECTED // P, HEADS, HD + 1])
    xT = s.sbuf("xT", [P, B * T])
    compressed = s.sbuf("compressed", [P, 2, T])
    sums = s.sbuf("sums", [P, 2, GROUPS, T])
    weights_sb = s.sbuf("weights", [P, 2, GROUP, BANK])
    v_value = s.sbuf("v_value", [P, T])
    means = s.sbuf("means", [P, 2, BLOCKS])
    mean_rows = s.sbuf("mean_rows", [P, 2, HEADS, BLOCKS])
    mean_values = s.sbuf("mean_values", [P, GROUPS, 32])
    block_peak = s.sbuf("block_peak", [P, TPB, HEADS])
    block_peak_parts = s.sbuf("block_peak_parts", [P, TPB, HEADS, 2], BF16)
    block_peak_rows = s.sbuf("block_peak_rows", [2 * HEADS, T], BF16)
    powers = s.sbuf("powers", [P, BANK])
    inverse = s.sbuf("inverse", [P, BANK])
    probs = s.sbuf("probs", [P, BANK])
    block_sums = s.sbuf("block_sums", [P, HALVES, GROUPS])
    block_score = s.sbuf("block_score", [P, GROUPS])
    score_rows = s.sbuf("score_rows", [GROUPS, GROUP, BLOCKS])
    top = s.sbuf("top", [GROUPS, GROUP, PICKED])
    top_at = s.sbuf("top_at", [GROUPS, GROUP, PICKED], U32)
    row_at = s.sbuf("row_at", [P, 2], U32)
    gathered = s.sbuf("gathered", [P, 2 * HD * BLOCK])
    chosen = s.sbuf("chosen", [P, 2, SELECTED])
    chosen_rest = s.sbuf("chosen_rest", [P, SELECTED])
    chosen_parts = s.sbuf("chosen_parts", [P, SPLITS, SELECTED], BF16)

    ps = s.psum("ps", [P, 8, BANK])
    ring = Ring(banks(ps, 3))
    score_ring = Ring(banks(ps, 2, 3))
    acc_ring = Ring(banks(ps, 3, 5))
    xn = weights_sb[:].rearrange("p a h (t d) -> p (a h t) d", d=P)
    marks = layer_norm(s, net, xn)
    ready = to_feature_major(s, net, Ring(banks(ps, 8)), xn, marks, xT)
    heads = Heads(s, scratch)

    dve.wait(loads.landed(), ready[-1], pe.mark())
    dve.tensor_scalar(b_qkv[:, 0:1], b_qkv[:, 0:1], scale, None, ALU.mult)
    dve.tensor_copy(ident_bf[:], net.ident[:])
    dve.memset(ones[:], 1.0)
    dve.memset(values[:, :, :, :, HD], 1.0)
    dve.memset(p_values[:, :, :, :, HD], 1.0)
    for bank in acc_ring.slots:
        dve.memset(bank, 0.0)
    start = dve.mark()
    for engine in (act, pe, pool, sp):
        engine.wait(start, loads.landed(), ready[-1])
    constants_in = s.landing("constants")
    for slot in range(SLOTS):
        for h in range(GROUP):
            sp.dma(constants_in, q_stack[QROWS:FILL, slot, h, :], dram["s_fill"][0:FILL - QROWS, :])
            sp.dma(constants_in, k_stack[QROWS:ROWS, slot, h, :], dram["s_fill_window"])
            sp.dma(constants_in, p_stack[QROWS:ROWS, slot, h, :], dram["s_fill_picked"][:, 0:SELECTED])

    table_in, sums_in, gather_in = s.landing("table"), s.landing("rows"), s.landing("gather")
    picked_in, chosen_in, parts_in = s.landing("picked"), s.landing("chosen"), s.landing("parts")
    done = {}

    def pause():
        pass

    def prepare(b):
        n = b % 2
        tokens = lambda half: slice(b * T + half * BANK, b * T + (half + 1) * BANK)
        columns = lambda half: slice(half * BANK, (half + 1) * BANK)
        q_value, k_value = heads.value[:, 0, :], heads.value[:, 1, :]

        def project_qk():
            act.wait(*done.get("means", ()), *done.get("q read", ()))
            heads.free = tuple(tuple(f) + done.get("table", ()) + done.get("q read", ()) for f in heads.free)
            heads.project(b, ring, w_qkv, b_qkv, scale, xT, ready)

        def project_v():
            for half in range(HALVES):
                i, bank, readers = ring.take()
                pe.wait(*readers)
                pe.matmul(bank, w_qkv[:, 2 * D:3 * D], xT[:, tokens(half)], start=True, stop=True)
                act.wait(pe.mark(), *done.get("table", ()), *done.get("means", ()))
                act.activation(v_value[:, columns(half)], bank, ACT.Identity, bias=b_qkv[:, 2:3])
                ring.release(i, act.mark())
            done["v"] = act.mark()

        def lay_values():
            act.wait(*done.get(("values", n), ()))
            for c in range(HALVES):
                i, bank, readers = ring.take()
                pe.wait(*readers)
                for j in range(TPC):
                    cols = bank[:, j * P:(j + 1) * P]
                    token = b * T + (TPC * c + j) * P
                    pe.matmul(cols, xT[:, token:token + P], w_qkv[:, 2 * D:3 * D], start=True, stop=False)
                    pe.matmul(cols, ones[:], b_v[:], start=False, stop=True)
                act.wait(pe.mark())
                act.copy(values[:, n, TPC * c:TPC * (c + 1), :, 0:HD],
                         bank.rearrange("p (j h d) -> p j h d", j=TPC, h=HEADS))
                ring.release(i, act.mark())
            done["values ready", b] = act.mark()

        def store_table():
            sp.wait(done["v"])
            rows = tables[b].rearrange("(h k) (w d t) -> w h d k t", h=HEADS, w=2, d=HD)
            for h in range(HEADS):
                at = slice(h * HD, (h + 1) * HD)
                for w, value in enumerate((k_value, v_value)):
                    sp.dma(table_in, rows[w, h], value[at].rearrange("p (k t) -> p k t", t=BLOCK))
            done["table"] = (table_in.landed(),)

        def block_means():
            dve.wait(done["v"], *done.get("mean use", ()))
            for w, value in enumerate((k_value, v_value[:])):
                dve.tensor_reduce(means[:, w, :], value.rearrange("p (k t) -> p k t", t=BLOCK), AX_X,
                                  ALU.add)
            dve.settle()
            dve.tensor_scalar(means[:], means[:], 1.0 / BLOCK, None, ALU.mult)
            dve.settle()
            for w in range(2):
                dve.tensor_tensor(mean_rows[:, w], means[:, w, :].unsqueeze(1).broadcast_to(
                    [P, HEADS, BLOCKS]), own[:].unsqueeze(2).broadcast_to([P, HEADS, BLOCKS]), ALU.mult)
            done["means"] = (dve.mark(),)
            i, bank, readers = ring.take()
            pe.wait(dve.mark(), *readers)
            for g in range(GROUPS):
                pe.transpose(bank[:, g * P:(g + 1) * P],
                             mean_rows[:, 1, GROUP * g:GROUP * (g + 1), :].rearrange("p h k -> p (h k)"),
                             net.ident[:])
            act.wait(pe.mark())
            for g in range(GROUPS):
                act.copy(mean_values[:, g, :], bank[:, g * P + 32 * g:g * P + 32 * (g + 1)])
            ring.release(i, act.mark())

        def block_peaks(t):
            def run():
                i, bank, readers = ring.take()
                pe.wait(*readers)
                pe.matmul(bank, q_value[:, t * P:(t + 1) * P],
                          mean_rows[:, 0].rearrange("p h k -> p (h k)"), start=True, stop=True)
                dve.wait(pe.mark())
                dve.tensor_reduce(block_peak[:, t, :], bank.rearrange("p (h k) -> p h k", k=BLOCKS), AX_X,
                                  ALU.max)
                ring.release(i, dve.mark())
            return run

        def block_peak_turn():
            dve.settle()
            dve.tensor_scalar(block_peak_parts[:, :, :, 0], block_peak[:], -1.0, None, ALU.mult)
            dve.settle()
            dve.scalar_tensor_tensor(block_peak_parts[:, :, :, 1], block_peak[:], -1.0,
                                     block_peak_parts[:, :, :, 0], ALU.mult, ALU.subtract)
            for half in range(HALVES):
                i, bank, readers = ring.take()
                pe.wait(dve.mark(), *readers)
                for j in range(TPC):
                    pe.matmul(bank[0:2 * HEADS, j * P:(j + 1) * P],
                              block_peak_parts[:, TPC * half + j].rearrange("p h s -> p (h s)"),
                              ident_bf[:], start=True, stop=True)
                act.wait(pe.mark())
                act.copy(block_peak_rows[:, columns(half)], bank[0:2 * HEADS, :])
                ring.release(i, act.mark())
            done["peak rows"] = act.mark()

        def block_powers(g, half):
            def run():
                i, bank, readers = ring.take()
                pe.wait(done["peak rows"], *readers)
                pe.matmul(bank, mean_rows[:, 0, GROUP * g:GROUP * (g + 1), :].rearrange("p h k -> p (h k)"),
                          q_value[:, columns(half)], start=True, stop=False)
                pe.matmul(bank, peak_spread[:, g, :], block_peak_rows[:, columns(half)], start=False,
                          stop=True)
                act.wait(pe.mark(), *done.get("powers", ()))
                act.activation(powers[:], bank, ACT.Exp)
                done["powers ready"] = act.mark()
                ring.release(i, act.mark())
            return run

        def block_probs(g, half):
            def run():
                i, bank, readers = ring.take()
                pe.wait(done["powers ready"], *readers)
                pe.matmul(bank, block_ones[:], powers[:], start=True, stop=True)
                dve.wait(pe.mark(), *done.get("probs", ()))
                dve.reciprocal(inverse[:], bank)
                ring.release(i, dve.mark())
                dve.settle()
                dve.scalar_tensor_tensor(probs[:], powers[:], 1.0, inverse[:], ALU.mult, ALU.mult,
                                         accum_out=block_sums[:, half, g:g + 1])
                done["powers"] = (dve.mark(), pe.mark())
                done["probs ready"] = dve.mark()
            return run

        def block_output(g, half):
            def run():
                i, bank, readers = ring.take()
                pe.wait(done["probs ready"], *readers)
                where = slice(32 * g, 32 * (g + 1))
                pe.matmul(bank[where, :], mean_values[:, g, :], probs[:], start=True, stop=True)
                done["probs"] = (pe.mark(),)
                act.wait(pe.mark(), *done.get(("compressed", n), ()))
                act.copy(compressed[where, n, columns(half)], bank[where, :])
                ring.release(i, act.mark())
                if g == GROUPS - 1 and half == HALVES - 1:
                    done["compressed ready", b] = act.mark()
                    done["q read"] = (pe.mark(),)
                    done["mean use"] = (pe.mark(),)
            return run

        def lay_scores():
            dve.settle()
            dve.tensor_tensor(block_score[:], block_sums[:, 0, :], block_sums[:, 1, :], ALU.add)
            i, bank, readers = ring.take()
            pe.wait(dve.mark(), *readers)
            pe.transpose(bank[0:GROUPS, 0:P], block_score[:], net.ident[:])
            dve.wait(pe.mark())
            dve.tensor_copy(score_rows[:].rearrange("g h k -> g (h k)"), bank[0:GROUPS, 0:P])
            ring.release(i, dve.mark())

        def rank():
            dve.settle()
            for h in range(GROUP):
                dve.max(top[:, h, :], score_rows[:, h, :])
            dve.settle()
            dve.wait(*done.get("top_at", ()))
            for h in range(GROUP):
                dve.op(lambda e, h=h: e.max_index(top_at[:, h, :], top[:, h, :], score_rows[:, h, :]))
            pool.wait(dve.mark())
            for g in range(GROUPS):
                pool.dma(sums_in, row_at[32 * g:32 * (g + 1), 0:1],
                         top_at[g:g + 1].rearrange("g h k -> g (h k)"))
            done["top_at"] = (sums_in.landed(),)

        def fetch():
            dve.wait(sums_in.landed())
            dve.tensor_scalar(row_at[:, 1:2], row_at[:, 0:1], row_base[:, 0:1], None, ALU.add)
            pool.wait(dve.mark(), table_in.landed(), *done.get("gathered", ()))
            pool.gather(gather_in, gathered[:], tables[b], row_at[:, 1:2])
            sp.wait(gather_in.landed())
            sp.dma(picked_in, picked[b], gathered[:])
            done["gathered"] = (picked_in.landed(),)
            sp.wait(picked_in.landed(), *done.get("chosen", ()))
            blocks = picked[b].rearrange("(h j) (w d t) -> w h d j t", h=HEADS, w=2, d=HD)
            for w in range(2):
                for h in range(HEADS):
                    sp.dma(chosen_in, chosen[h * HD:(h + 1) * HD, w, :].rearrange(
                        "p (j t) -> p j t", t=BLOCK), blocks[w, h])

        def split_chosen():
            dve.wait(chosen_in.landed(), *done.get("chosen parts", ()))
            split_parts(dve, chosen[:, 0, :], chosen_rest[:], [chosen_parts[:, i, :] for i in range(SPLITS)])
            sp.wait(dve.mark())
            sp.dma(parts_in, picked_parts[b].rearrange("s p t -> p s t"), chosen_parts[:])
            done["chosen parts"] = (parts_in.landed(),)
            i, bank, readers = ring.take()
            pe.wait(chosen_in.landed(), *readers)
            for j in range(SELECTED // P):
                pe.transpose(bank[:, j * P:(j + 1) * P], chosen[:, 1, j * P:(j + 1) * P], net.ident[:])
            act.wait(pe.mark(), *done.get(("p_values", n), ()))
            act.copy(p_values[:, n, :, :, 0:HD],
                     bank[:, 0:SELECTED].rearrange("p (j h d) -> p j h d", j=SELECTED // P, h=HEADS))
            ring.release(i, act.mark())
            done["p_values ready", b] = act.mark()
            done["chosen"] = (pe.mark(), dve.mark())

        steps = [project_qk, project_v, store_table, lay_values, block_means]
        steps += [block_peaks(t) for t in range(TPB)] + [block_peak_turn]
        for g in range(GROUPS):
            for half in range(HALVES):
                steps += [block_powers(g, half), block_probs(g, half), block_output(g, half)]
        return steps + [lay_scores, rank] + [pause] * 4 + [fetch] + [pause] * 8 + [split_chosen]

    stack_in = [s.landing("stack%d" % i) for i in range(SLOTS)]
    stack_free = [() for _ in range(SLOTS)]

    def assemble(g):
        b, first, slot = g // GROUPS, GROUP * (g % GROUPS), g % SLOTS
        sp.wait(constants_in.landed(), parts_in.landed(), *stack_free[slot])
        sp.wait(*heads.parts_free[0], *heads.parts_free[1])
        rows = slice(first * HD, (first + GROUP) * HD)
        for i, (qpart, kpart) in enumerate(TERMS):
            at = slice(HD * i, HD * (i + 1))
            for stack, source in ((q_stack, scratch[b, 0, qpart, rows, :]),
                                  (k_stack, scratch[b, 1, kpart, rows, :]),
                                  (p_stack, picked_parts[b, kpart, rows, :])):
                sp.dma(stack_in[slot], stack[at, slot, :, :], source.rearrange("(h d) t -> d h t", d=HD))

    peak = s.sbuf("peak", [P, SLOTS, TPB, GROUP, 2])
    peak_parts = s.sbuf("peak_parts", [P, SLOTS, TPB, GROUP, 2, 2], BF16)
    peak_rows = s.sbuf("peak_rows", [4 * GROUP, SLOTS, T], BF16)
    peaks_in = [s.landing("peaks%d" % i) for i in range(SLOTS)]
    peak_free = [() for _ in range(SLOTS)]

    def score(g, unit):
        slot, kind = g % SLOTS, unit % 2
        h0, t = 2 * (unit // 2 % 2), unit // 4
        if unit == 0:
            pe.wait(stack_in[slot].landed())
            dve.wait(*peak_free[slot])
        i, bank, readers = score_ring.take()
        pe.wait(*readers)
        width = SELECTED if kind == 0 or t else P
        for n in range(2):
            out = bank[:, n * SELECTED:n * SELECTED + width]
            queries = q_stack[0:FILL, slot, h0 + n, t * P:(t + 1) * P]
            if kind == 0:
                pe.matmul(out, queries, p_stack[0:FILL, slot, h0 + n, :], start=True, stop=True)
            else:
                keys = k_stack[0:FILL, slot, h0 + n, (t + 1) * P - width:(t + 1) * P]
                pe.matmul(out, queries, keys, start=True, stop=False)
                pe.matmul(out, ident_bf[:], mask_q[:, 2 - width // P:, :].rearrange("p a k -> p (a k)"),
                          start=False, stop=True)
        dve.wait(pe.mark())
        dve.tensor_reduce(peak[:, slot, t, h0:h0 + 2, kind],
                          bank.rearrange("p (n k) -> p n k", n=2)[:, :, 0:width], AX_X, ALU.max)
        score_ring.release(i, dve.mark())

    def peaks(g):
        slot = g % SLOTS
        dve.settle()
        dve.tensor_scalar(peak_parts[:, slot, :, :, :, 0], peak[:, slot], -1.0, None, ALU.mult)
        dve.settle()
        flat = lambda a: a.rearrange("p t h k -> p (t h k)")
        dve.scalar_tensor_tensor(flat(peak_parts[:, slot, :, :, :, 1]), flat(peak[:, slot]), -1.0,
                                 flat(peak_parts[:, slot, :, :, :, 0]), ALU.mult, ALU.subtract)
        for half in range(HALVES):
            i, bank, readers = ring.take()
            pe.wait(dve.mark(), *readers)
            for j in range(TPC):
                pe.matmul(bank[0:4 * GROUP, j * P:(j + 1) * P],
                          peak_parts[:, slot, TPC * half + j].rearrange("p h k s -> p (h k s)"),
                          ident_bf[:], start=True, stop=True)
            act.wait(pe.mark())
            act.copy(peak_rows[:, slot, half * BANK:(half + 1) * BANK], bank[0:4 * GROUP, :])
            ring.release(i, act.mark())
        sp.wait(act.mark())
        for h in range(GROUP):
            sp.dma(peaks_in[slot], q_stack[FILL:ROWS, slot, h, :],
                   peak_rows[4 * h:4 * h + 4, slot, :])
        peak_free[slot] = (pe.mark(), peaks_in[slot].landed())

    weight_ring = Ring([weights_sb[:, i] for i in range(2)])
    acc = {}
    sums_ready = {}

    def accumulate(kind, half):
        if (kind, half) not in acc:
            i, bank, readers = acc_ring.take()
            pe.wait(*readers)
            acc[kind, half] = (i, bank)
        return acc[kind, half][1]

    def picked_weights(g, tile, half, between):
        slot = g % SLOTS
        w, weights, free = weight_ring.take()
        for h in range(GROUP):
            i, bank, readers = ring.take()
            pe.wait(*readers)
            pe.matmul(bank, p_stack[0:ROWS, slot, h, tile * P:(tile + 1) * P],
                      q_stack[0:ROWS, slot, h, half * BANK:(half + 1) * BANK], start=True, stop=True)
            act.wait(pe.mark(), *free)
            act.activation(weights[:, h, :], bank, ACT.Exp)
            mark = act.mark()
            ring.release(i, mark)
            between()

        def weigh():
            b, first = g // GROUPS, GROUP * (g % GROUPS)
            pe.wait(mark, done["p_values ready", b])
            into = accumulate(0, half)
            for h in range(GROUP):
                pe.matmul(into[32 * h:32 * h + HD + 1, :], p_values[:, b % 2, tile, first + h, :],
                          weights[:, h, :], start=tile == 0, stop=tile == 1)
            weight_ring.release(w, pe.mark())
            if tile:
                store(g, 0, half)
        return weigh

    def window_weights(g, tile, between):
        slot = g % SLOTS
        w, weights, free = weight_ring.take()
        width = 2 * P if tile < TPB - 1 else P
        for h0 in range(0, GROUP, 2):
            i, bank, readers = ring.take()
            pe.wait(*readers)
            for n in range(2):
                out = bank[:, n * 2 * P:n * 2 * P + width]
                pe.matmul(out, k_stack[0:ROWS, slot, h0 + n, tile * P:(tile + 1) * P],
                          q_stack[0:ROWS, slot, h0 + n, tile * P:tile * P + width], start=True, stop=False)
                pe.matmul(out, ident_bf[:], mask_k[:, 0:width // P, :].rearrange("p a q -> p (a q)"),
                          start=False, stop=True)
            act.wait(pe.mark(), *free)
            act.activation(weights[:, h0:h0 + 2, 0:width],
                           bank.rearrange("p (n q) -> p n q", n=2)[:, :, 0:width], ACT.Exp)
            mark = act.mark()
            ring.release(i, mark)
            between()
        if tile == TPB - 1:
            stack_free[slot] = (pe.mark(),)

        def weigh():
            b, first = g // GROUPS, GROUP * (g % GROUPS)
            pe.wait(mark, done["values ready", b])
            spans = [(tile, width // P)] if tile % TPC != TPC - 1 else [(tile + j, 1) for j in range(width // P)]
            for first_tile, count in spans:
                half, col = first_tile // TPC, first_tile % TPC * P
                into = accumulate(1, half)
                begins = first_tile % TPC == 0 and (tile == 0 or first_tile == tile + 1)
                for h in range(GROUP):
                    pe.matmul(into[32 * h:32 * h + HD + 1, col:col + count * P],
                              values[:, b % 2, tile, first + h, :],
                              weights[:, h, (first_tile - tile) * P:(first_tile - tile + count) * P],
                              start=begins, stop=tile == TPB - 1, skip_group_check=True)
            weight_ring.release(w, pe.mark())
            if tile % TPC == TPC - 1:
                store(g, 1, tile // TPC)
        return weigh

    def store(g, kind, half):
        i, bank = acc.pop((kind, half))
        act.wait(pe.mark(), *done.get(("sums", kind), ()))
        act.copy(sums[:, kind, g % GROUPS, half * BANK:(half + 1) * BANK], bank)
        acc_ring.release(i, act.mark())
        if g % GROUPS == GROUPS - 1 and half == HALVES - 1:
            sums_ready[g // GROUPS, kind] = act.mark()
            done[("p_values", "values")[kind], g // GROUPS % 2] = (pe.mark(),)

    mixed = s.sbuf("mixed", [P, 2, BANK])
    term = s.sbuf("term", [P, BANK])
    gates = s.sbuf("gates", [P, BANK])
    mixed_free = [(), ()]

    def project_out(b, half):
        at = slice(half * BANK, (half + 1) * BANK)

        def gate(kind):
            i, bank, readers = ring.take()
            pe.wait(*readers)
            pe.matmul(bank, w_gate[:, kind, :], xT[:, b * T + half * BANK:b * T + (half + 1) * BANK],
                      start=True, stop=True)
            act.wait(pe.mark(), *done.get("gates", ()))
            act.activation(gates[:], bank, ACT.Sigmoid, bias=b_gate[:, kind:kind + 1])
            done["gate"] = act.mark()
            ring.release(i, act.mark())

        def first():
            gate(0)
            dve.wait(done["gate"], done["compressed ready", b], *mixed_free[half])
            dve.tensor_tensor(mixed[:, half, :], compressed[:, b % 2, at], gates[:], ALU.mult)
            done["compressed", b % 2] = done["gates"] = (dve.mark(),)
            gate(1)

        def normalise(kind):
            def run():
                pe.wait(sums_ready[b, kind])
                found = []
                for what in range(2):
                    j, rows, readers = ring.take()
                    pe.wait(*readers)
                    for group in range(GROUPS):
                        pe.matmul(rows[32 * group:32 * (group + 1), :], select[:, what, :],
                                  sums[:, kind, group, at], start=True, stop=True)
                    found.append((j, rows))
                dve.wait(pe.mark(), done["gate"])
                step = Chained(dve)
                step.reciprocal(term[:], found[1][1])
                ring.release(found[1][0], dve.mark())
                step.tensor_tensor(term[:], found[0][1], term[:], ALU.mult)
                ring.release(found[0][0], dve.mark())
                step.tensor_tensor(term[:], term[:], gates[:], ALU.mult)
                step.tensor_tensor(mixed[:, half, :], mixed[:, half, :], term[:], ALU.add)
                done["mixed"] = dve.mark()
                done["gates"] = (dve.mark(),)
                if half == 1:
                    done["sums", kind] = (pe.mark(),)
                if kind == 0:
                    gate(2)
            return run

        def last():
            i, bank, readers = ring.take()
            pe.wait(done["mixed"], *readers)
            for j in range(TPC):
                cols = bank[:, j * P:(j + 1) * P]
                pe.matmul(cols, mixed[:, half, j * P:(j + 1) * P], w_out[:], start=True, stop=False)
                pe.matmul(cols, ones[:], b_out[:], start=False, stop=True)
            mixed_free[half] = (pe.mark(),)
            dve.wait(pe.mark())
            tile = b * TPB + half * TPC
            x = net.residual[:, tile:tile + TPC, :].rearrange("p t d -> p (t d)")
            dve.tensor_tensor(x, bank, x, ALU.add)
            ring.release(i, dve.mark())
        return [first, normalise(0), normalise(1), last]

    units, total = 4 * TPB, B * GROUPS
    for step in prepare(0):
        step()
    assemble(0)
    for unit in range(units):
        score(0, unit)
    peaks(0)
    steps = [(0, tile, half) for half in range(HALVES) for tile in range(2)]
    steps += [(1, tile, 0) for tile in range(TPB)]
    pieces = GROUP * 4 + GROUP // 2 * TPB
    begin, end = 8, pieces - 4
    work, ending, pending = [], [], []
    for g in range(total):
        b = g // GROUPS
        if g % GROUPS == GROUPS - 1:
            for step in work:
                step()
            work = []
        if g + 1 < total:
            assemble(g + 1)
        piece = counted = 0

        def between():
            nonlocal piece, counted
            piece += 1
            if ending:
                ending.pop(0)()
            elif work:
                left = (GROUPS - 1 - g % GROUPS) * pieces - piece
                for _ in range(-(-len(work) // max(left, 1))):
                    work.pop(0)()
            while g + 1 < total and counted < min(units, (piece - begin) * units // (end - begin)):
                score(g + 1, counted)
                counted += 1
        pe.wait(peaks_in[g % SLOTS].landed())
        for n, (kind, tile, half) in enumerate(steps):
            made = window_weights(g, tile, between) if kind else picked_weights(g, tile, half, between)
            if pending:
                pending.pop()()
            pending.append(made)
            if n == 0 and g % GROUPS == 0:
                ending = project_out(b - 1, 0) + project_out(b - 1, 1) if g else []
                work = prepare(b + 1) if b + 1 < B else []
            if n == 2:
                assert not ending
            if g + 1 < total and n == len(steps) - 2:
                peaks(g + 1)
    pending.pop()()
    for step in project_out(B - 1, 0) + project_out(B - 1, 1):
        step()
    s.close()


KH, KD, KC = 4, 32, 32
CPT = P // KC
CPB = T // KC
PAIRS = TPB // 2
FIR_TAPS = (3, 7, 15, 31)
HISTORY = max(FIR_TAPS) - 1
BRANCHES = len(FIR_TAPS) + 2
GATED = KH * BRANCHES
GATE_WIDE = 256
GB = GATE_WIDE // P
LEVELS = 5
FLOOR = 0.05
RATE, RATE2, RATE3 = 0.9,3,1.2
ON_POOL = -1
L2_EPS, O_EPS = 1e-12, 1e-5


def delta_stage(nc, net):
    s = Stage(nc, net, "delta")
    dram = net.dram
    pe, act, dve, pool, sp = s.pe, s.act, s.dve, s.pool, s.sp
    loads = s.landing("loads")

    def load(name, shape):
        buffer = s.sbuf(name, shape)
        sp.dma(loads, buffer[:], dram["d_" + name])
        return buffer
    w_qkv = load("w_qkv", [P, 3, P])
    w_beta = load("w_beta", [P, P])
    conv_w = load("conv_w", [P, 3, TAPS])
    fir_w = load("fir_w", [P, sum(FIR_TAPS)])
    w_gate = load("w_gate", [P, GATE_WIDE])
    w_stats = load("w_stats", [P, GATE_WIDE])
    b_gate = load("b_gate", [P, GB])
    w_logit = load("w_logit", [P, GB, GATED])
    w_alpha = load("w_alpha", [P, GATED])
    log_temp = load("log_temp", [P, GATED])
    o_gain = load("o_gain", [P, 1])
    w_out = load("w_out", [P, P])
    block_ones = load("block_ones", [P, P])
    eye = load("eye", [P, KC])
    masks = load("masks", [P, LEVELS + 2, KC])
    stat_select = load("stat_select", [P, BRANCHES, P])
    stat_one = load("stat_one", [P, 1])
    xT = s.sbuf("xT", [P, B * T])
    raw = s.sbuf("raw", [P, 3, TAPS - 1 + T])
    qk = s.sbuf("qk", [P, 2, T])
    v_all = s.sbuf("v", [P, 3, HISTORY + T])
    beta = s.sbuf("beta", [P, T])
    norm = raw[:, 0:2, TAPS - 1:]
    kbq = s.sbuf("kbq", [P, 2, CPB, KC])
    keep = s.sbuf("keep", [P, 2, CPB, 2, 2, KC])
    state = s.sbuf("state", [P, 2, CPB, KC])
    at_all = s.sbuf("at", [P, 2, KH, 2, KC])
    n_all = s.sbuf("n", [P, 2, 2, KH, 2, KC])
    t_all = s.sbuf("t", [P, 2, KH, 2, KC])
    kat_all = s.sbuf("kat", [P, 2, KH, 2, 2, KC])
    vk_all = s.sbuf("vk", [P, 2, 2, KH, 2, KC])
    uw_all = s.sbuf("uw", [P, 2, 2, KH, 2, KC])
    branch_all = s.sbuf("branch", [P, 2, BRANCHES - 1, T])
    absolute = s.sbuf("absolute", [P, 2, BANK])
    stats = s.sbuf("stats", [P, BANK])
    hidden = s.sbuf("hidden", [P, GB, BANK])
    logits = s.sbuf("logits", [P, TPC, KH, BRANCHES])
    small = s.sbuf("small", [P, 2, TPC * KH])
    product = s.sbuf("product", [P, BRANCHES, P])
    o = s.sbuf("o", [P, TPC, P])
    o_sq = s.sbuf("o_sq", [P, TPC, P])
    oT = s.sbuf("oT", [P, BANK])
    temper = s.sbuf("temper", [P, 2, GATED])
    eps = s.sbuf("eps", [P, 2])
    ps = s.psum("ps", [P, 8, BANK])
    cross = Ring([ps[:, 0:CPT, 0:8 * KC].rearrange(
        "p a (m t n) -> p a m t n", m=2, t=2)])
    diag = Ring([ps[:, 4, 0:256], ps[:, 5, 0:256]])
    wide = Ring(banks(ps, 2, 6))

    xn = branch_all[:, 0, 0:4, :].rearrange("p a (t d) -> p (a t) d", d=P)
    marks = layer_norm(s, net, xn)
    ready = to_feature_major(s, net, Ring(banks(ps, 8)), xn, marks, xT)
    act.wait(loads.landed(), ready[-1])
    dve.wait(loads.landed(), pe.mark())
    pe.wait(loads.landed(), ready[-1])
    pos, soft = temper[:, 0, :], temper[:, 1, :]
    act.activation(soft, log_temp[:], ACT.Abs)
    act.settle()
    act.activation(soft, soft, ACT.Exp, scale=-1.0)
    act.settle()
    act.activation(soft, soft, ACT.Ln, bias=1.0)
    dve.tensor_scalar(pos, log_temp[:], 0.0, None, ALU.max)
    dve.wait(act.mark())
    dve.settle()
    dve.scalar_tensor_tensor(soft, pos, 1e-4, soft, ALU.add, ALU.add)
    dve.settle()
    dve.reciprocal(pos, soft)
    act.activation(w_out[:], w_out[:], ACT.Copy, scale=o_gain[:, 0:1])
    dve.memset(raw[:, :, 0:TAPS - 1], 0.0)
    dve.memset(v_all[:, :, 0:HISTORY], 0.0)
    dve.memset(state[:, :, 0, :], 0.0)
    dve.memset(eps[:, 0:1], L2_EPS)
    dve.memset(eps[:, 1:2], O_EPS)
    for e in (pe, act, dve, pool):
        e.wait(dve.mark(), act.mark(), loads.landed())
    inv_temp = pos
    free = {}

    def project(weights, b, half, stop=True):
        i, bank, readers = wide.take()
        pe.wait(*readers)
        t0 = b * T + half * BANK
        pe.matmul(bank, weights, xT[:, t0:t0 + BANK], start=True, stop=stop)
        return i, bank

    def prepare(b):
        act.wait(*free.get("raw", ()))
        for n in range(3):
            for half in range(2):
                i, bank = project(w_qkv[:, n, :], b, half)
                act.wait(pe.mark())
                t0 = TAPS - 1 + half * BANK
                act.copy(raw[:, n, t0:t0 + BANK], bank)
                wide.release(i, act.mark())
            yield
        act.wait(*free.get("beta", ()))
        for half in range(2):
            i, bank = project(w_beta[:], b, half)
            act.wait(pe.mark())
            act.activation(beta[:, half * BANK:(half + 1) * BANK], bank, ACT.Sigmoid)
            wide.release(i, act.mark())
        yield
        v = v_all[:, b % 3, HISTORY:]
        outs = (qk[:, 0, :], qk[:, 1, :], v)
        dve.wait(act.mark(), *free.get("qk", ()), *free.get(("v", b % 3), ()))
        for n in (1, 0, 2):
            dve.tensor_scalar(outs[n], raw[:, n, 0:T], conv_w[:, n, 0:1], None, ALU.mult)
        for k in range(1, TAPS):
            dve.settle()
            for n in (1, 0, 2):
                dve.scalar_tensor_tensor(outs[n], raw[:, n, k:k + T], conv_w[:, n, k:k + 1], outs[n],
                                         ALU.mult, ALU.add)
            yield
        act.wait(dve.mark())
        for n in (1, 0, 2):
            act.activation(outs[n], outs[n], ACT.Silu)
        act.settle()
        silu = act.mark()
        for n in (1, 0):
            act.activation(norm[:, n, :], outs[n], ACT.Square)
        yield
        for n in (1, 0):
            for half in range(2):
                cols = slice(half * BANK, (half + 1) * BANK)
                i, bank, readers = wide.take()
                pe.wait(act.mark(), *readers)
                pe.matmul(bank, block_ones[:], norm[:, n, cols], start=True, stop=True)
                act.wait(pe.mark())
                act.activation(norm[:, n, cols], bank, ACT.Sqrt, bias=eps[:, 0:1])
                wide.release(i, act.mark())
            dve.wait(act.mark())
            dve.reciprocal(norm[:, n, :], norm[:, n, :])
            yield
        pool.wait(dve.mark())
        chunked = lambda a: a.rearrange("p (c t) -> p c t", t=KC)
        pool.wait(*free.get("kbq", ()))
        pool.tensor_tensor(qk[:, 1, :], qk[:, 1, :], norm[:, 1, :], ALU.mult)
        dve.wait(pool.mark(), *free.get("kbq", ()))
        dve.tensor_tensor(kbq[:, 0], chunked(qk[:, 1, :]), chunked(beta[:]), ALU.mult)
        pool.tensor_tensor(kbq[:, 1], chunked(qk[:, 0, :]), chunked(norm[:, 0, :]), ALU.mult)
        dve.wait(silu)
        dve.settle()
        dve.tensor_tensor(beta[:], v, beta[:], ALU.mult)
        free["raw"] = (dve.mark(), pool.mark())
        free["prepared"] = (dve.mark(), pool.mark(), silu)
        yield

    def blocks(slot, left, right):
        for tile in range(2):
            for h in range(KH):
                for c in range(CPT):
                    rows = slice(KC * c, KC * (c + 1))
                    pe.matmul(slot[rows, h, tile, :], left[rows, h, tile, :], right[rows, h, tile, :],
                              start=True, stop=True)

    def pair_of_tiles(b, pair, way):
        at, kat, t1 = at_all[:, way], kat_all[:, way], t_all[:, way]
        n, nT = n_all[:, way, 0], n_all[:, way, 1]
        vk, uw = vk_all[:, way], uw_all[:, way]
        busy = free.get(("way", way), ())
        pe.wait(*free["prepared"])
        first = pair * 2 * CPT
        for tile in range(2):
            i, bank, readers = wide.take()
            pe.wait(*readers)
            t0 = (2 * pair + tile) * P
            cols = slice(t0, t0 + P)
            kb = kbq[:, 0, first + tile * CPT:first + (tile + 1) * CPT, :]
            for m, source in enumerate((qk[:, 1, cols], beta[:, cols], kb.rearrange("p c t -> p (c t)"))):
                pe.transpose(bank[:, m * P:(m + 1) * P], source, net.ident[:])
            act.wait(pe.mark(), *busy)
            heads = lambda m: bank[:, m * P:(m + 1) * P].rearrange("p (h d) -> p h d", h=KH)
            act.copy(kat[:, :, tile, 0, :], heads(0))
            act.copy(vk[:, tile, :, 0, :], heads(1))
            act.copy(vk[:, tile, :, 1, :], heads(2))
            wide.release(i, act.mark())
        tokens = act.mark()
        i, slot, readers = cross.take()
        slot = slot[:, :, 0]
        pe.wait(*readers)
        for tile in range(2):
            for c in range(CPT):
                at_chunk = first + tile * CPT + c
                out = slice(KC * c, KC * (c + 1))
                for h in range(KH):
                    rows = slice(KC * h, KC * (h + 1))
                    pe.matmul(slot[out, h, tile, :], qk[rows, 1, at_chunk * KC:(at_chunk + 1) * KC],
                              kbq[rows, :, at_chunk, :], start=True, stop=True)
        dve.wait(pe.mark(), *busy)
        mask = lambda k: masks[:, k, :].unsqueeze(1).unsqueeze(1).broadcast_to([P, KH, 2, KC])
        dve.tensor_tensor(at, slot[:, :, :, 0:KC], mask(0), ALU.mult)
        dve.tensor_tensor(kat[:, :, :, 1, :], slot[:, :, :, KC:], mask(1), ALU.mult)
        cross.release(i, dve.mark())
        kat_mark = dve.mark()
        dve.settle()
        dve.tensor_tensor(t1, at, mask(2), ALU.mult)
        dve.settle()
        identity = eye[:].unsqueeze(1).unsqueeze(1).broadcast_to([P, KH, 2, KC])
        dve.tensor_tensor(nT, t1, identity, ALU.add)
        dve.settle()
        flat = lambda a: a.rearrange("p h t n -> p (h t n)")
        dve.op(lambda e, o_=flat(n), i_=flat(nT): e.transpose(o_, i_))
        ready = dve.mark()
        yield
        for level in range(1, LEVELS):
            i, slot, readers = diag.take()
            pe.wait(ready, *readers)
            grid = slot.rearrange("p (h t n) -> p h t n", h=KH, t=2)
            blocks(grid, at, n)
            dve.wait(pe.mark())
            dve.tensor_tensor(t1, grid, mask(2 + level), ALU.mult)
            ready = dve.mark()
            diag.release(i, ready)
            yield
            i, slot, readers = diag.take()
            pe.wait(ready, *readers)
            grid = slot.rearrange("p (h t n) -> p h t n", h=KH, t=2)
            if level < LEVELS - 1:
                blocks(grid, nT, t1)
                dve.wait(pe.mark())
                dve.tensor_tensor(n, n, grid, ALU.add)
                diag.release(i, dve.mark())
                dve.settle()
                dve.op(lambda e, o_=flat(nT), i_=flat(n): e.transpose(o_, i_))
            else:
                blocks(grid, t1, nT)
                dve.wait(pe.mark())
                dve.tensor_tensor(nT, nT, grid, ALU.add)
                diag.release(i, dve.mark())
            ready = dve.mark()
            yield
        for tile in range(2):
            i, slot, readers = diag.take()
            pe.wait(ready, tokens, *readers)
            for h in range(KH):
                for c in range(CPT):
                    rows = slice(KC * c, KC * (c + 1))
                    pe.matmul(slot[rows, 2 * KC * h:2 * KC * (h + 1)], nT[rows, h, tile, :],
                              vk[rows, tile, h, :, :], start=True, stop=True)
            act.wait(pe.mark(), *busy)
            act.copy(uw[:, tile].rearrange("p h a n -> p (h a n)"), slot)
            diag.release(i, act.mark())
        ready = act.mark()
        yield
        i, slot, readers = cross.take()
        pe.wait(ready, kat_mark, *readers)
        with_w, with_u = slot[:, :, 0], slot[:, :, 1]
        for tile in range(2):
            for h in range(KH):
                out = slice(KC * h, KC * (h + 1))
                for product_of in range(3):
                    for c in range(CPT):
                        rows = slice(KC * c, KC * (c + 1))
                        u, w = uw[rows, tile, h, 0, :], uw[rows, tile, h, 1, :]
                        if product_of == 0:
                            pe.matmul(with_w[out, c, tile, :], w, kat[rows, h, tile, :, :],
                                      start=True, stop=True)
                        elif product_of == 1:
                            pe.matmul(with_u[out, c, tile, 0:KC], kat[rows, h, tile, 0, :], u,
                                      start=True, stop=True)
                        else:
                            pe.matmul(with_u[out, c, tile, KC:], u, kat[rows, h, tile, 1, :],
                                      start=True, stop=True)
        by_chunk = lambda a: a.rearrange("p (t c) n -> p c t n", t=2)
        mine = keep[:, b % 2, first:first + 2 * CPT]
        dve.wait(pe.mark(), *free.get(("keep", b % 2), ()))
        dve.tensor_tensor(by_chunk(mine[:, :, 0, 0, :]), identity, with_w[:, :, :, 0:KC],
                          ALU.subtract)
        dve.tensor_tensor(by_chunk(mine[:, :, 0, 1, :]), by_chunk(kbq[:, 1, first:first + 2 * CPT, :]),
                          with_w[:, :, :, KC:], ALU.subtract)
        act.wait(dve.mark())
        by_two = lambda a: a.rearrange("p (t c) a n -> p c t (a n)", t=2)
        act.copy(by_two(mine[:, :, 1]), with_u)
        cross.release(i, act.mark())
        free["way", way] = (pe.mark(),)
        free["kept", b % 2] = (dve.mark(), act.mark())
        for name in ("qk", "kbq", "beta"):
            free[name] = (pe.mark(), dve.mark())
        yield

    def filters(b):
        v, branch = v_all[:, b % 3, :], branch_all[:, b % 2]
        for e in (dve, pool):
            e.wait(*free["prepared"], *free.get(("branch", b % 2), ()))
        for k in range(max(FIR_TAPS)):
            for n, count in enumerate(FIR_TAPS):
                if k >= count:
                    continue
                e = pool if n == ON_POOL else dve
                first = HISTORY + k - count + 1
                shifted = v[:, first:first + T]
                tap = sum(FIR_TAPS[:n]) + k
                weight = fir_w[:, tap:tap + 1]
                if k == 0:
                    e.tensor_scalar(branch[:, n, :], shifted, weight, None, ALU.mult)
                else:
                    e.settle()
                    e.scalar_tensor_tensor(branch[:, n, :], shifted, weight, branch[:, n, :],
                                           ALU.mult, ALU.add)
                if e is dve:
                    yield
        free["filtered", b % 2] = (dve.mark(), pool.mark())

    def finish(b):
        kept, branch = keep[:, b % 2], branch_all[:, b % 2]
        S = state[:, b % 2]
        pe.wait(*free["kept", b % 2], free["zero"])
        dve.wait(*free["kept", b % 2], *free.get(("state", b % 2), ()))
        for c in range(CPB - 1):
            i, bank, readers = wide.take()
            slot = bank[:, 0:KC]
            pe.wait(*readers)
            if c:
                pe.wait(stepped)
            for h in range(KH):
                rows = slice(KC * h, KC * (h + 1))
                pe.matmul(slot[rows, :], kept[rows, c, 0, 0, :], S[rows, c, :], start=True, stop=True)
            dve.wait(pe.mark())
            dve.tensor_tensor(S[:, c + 1, :], slot, kept[:, c, 1, 0, :], ALU.add)
            stepped = dve.mark()
            wide.release(i, stepped)
            yield
        v = v_all[:, b % 3, HISTORY:]
        for half in range(2):
            cols = slice(half * BANK, (half + 1) * BANK)
            c0 = half * CPB // 2
            i, bank, readers = wide.take()
            dve.wait(*free.get(("branch", b % 2), ()))
            pe.wait(stepped, *free["filtered", b % 2], *readers)
            for c in range(CPB // 2):
                for h in range(KH):
                    rows = slice(KC * h, KC * (h + 1))
                    pe.matmul(bank[rows, KC * c:KC * (c + 1)], S[rows, c0 + c, :],
                              kept[rows, c0 + c, 0, 1, :], start=True, stop=True)
            dve.wait(pe.mark())
            dve.tensor_tensor(branch[:, 4, cols].rearrange("p (c t) -> p c t", t=KC),
                              bank.rearrange("p (c t) -> p c t", t=KC),
                              kept[:, c0:c0 + CPB // 2, 1, 1, :], ALU.add)
            ruled = dve.mark()
            wide.release(i, ruled)
            if half:
                free["keep", b % 2] = free["state", b % 2] = (pe.mark(), dve.mark())
            source = lambda p, at=cols: v[:, at] if p == 4 else branch[:, min(p, 4), at]
            yield
            j, sums, readers = wide.take()
            pe.wait(*readers)
            for p in range(BRANCHES):
                act.wait(ruled, *free["filtered", b % 2], *free.get(("absolute", p % 2), ()))
                act.activation(absolute[:, p % 2, :], source(p), ACT.Abs)
                pe.wait(act.mark())
                pe.matmul(sums, stat_select[:, p, :], absolute[:, p % 2, :], start=p == 0,
                          stop=p == BRANCHES - 1)
                free["absolute", p % 2] = (pe.mark(),)
            act.wait(pe.mark(), *free.get("stats", ()))
            act.activation(stats[:], sums, ACT.Identity, bias=stat_one[:, 0:1])
            ready = act.mark()
            wide.release(j, ready)
            yield
            for m in range(GB):
                i, bank = project(w_gate[:, m * P:(m + 1) * P], b, half, stop=False)
                pe.wait(ready)
                pe.matmul(bank, w_stats[:, m * P:(m + 1) * P], stats[:], start=False, stop=True)
                act.wait(pe.mark(), *free.get("hidden", ()))
                act.activation(hidden[:, m, :], bank, ACT.Gelu, bias=b_gate[:, m:m + 1])
                wide.release(i, act.mark())
            ready = act.mark()
            yield
            i, bank, readers = wide.take()
            pe.wait(ready, *readers)
            for t in range(TPC):
                tok = slice(t * P, (t + 1) * P)
                out = bank[:, t * GATED:(t + 1) * GATED]
                for m in range(GB):
                    pe.matmul(out, hidden[:, m, tok], w_logit[:, m, :], start=m == 0, stop=False)
                pe.matmul(out, stats[:, tok], w_alpha[:], start=False, stop=True)
            free["stats"] = free["hidden"] = (pe.mark(),)
            grid = lambda a: a.rearrange("p (t h) -> p t h", h=KH)
            most, total = grid(small[:, 0, :]), grid(small[:, 1, :])
            over = lambda a: a.unsqueeze(3).broadcast_to([P, TPC, KH, BRANCHES])
            dve.wait(pe.mark(), *free.get("logits", ()))
            step = Chained(dve)
            lg = logits[:].rearrange("p t h n -> p t (h n)")
            step.tensor_tensor(lg, bank[:, 0:TPC * GATED].rearrange("p (t g) -> p t g", g=GATED),
                               inv_temp.unsqueeze(1).broadcast_to([P, TPC, GATED]), ALU.mult)
            wide.release(i, dve.mark())
            step.tensor_reduce(most, logits[:], AX_X, ALU.max)
            step.tensor_tensor(logits[:], logits[:], over(most), ALU.subtract)
            act.wait(dve.mark())
            act.activation(logits[:], logits[:], ACT.Exp)
            ready = act.mark()
            yield
            dve.wait(ready)
            step.tensor_reduce(total, logits[:], AX_X, ALU.add)
            step.reciprocal(most, total)
            step.tensor_scalar(most, most, 1.0 - FLOOR, None, ALU.mult)
            step.tensor_tensor(logits[:], logits[:], over(most), ALU.mult)
            step.tensor_scalar(logits[:, :, :, BRANCHES - 1], logits[:, :, :, BRANCHES - 1], FLOOR,
                               None, ALU.add)
            yield
            for t in range(TPC):
                tok = slice(half * BANK + t * P, half * BANK + (t + 1) * P)
                dve.wait(*free.get("product", ()))
                for part in range(2):
                    i, bank, readers = wide.take()
                    pe.wait(*readers)
                    for p in range(3):
                        n = 3 * part + p
                        pe.transpose(bank[:, p * P:(p + 1) * P],
                                     source(n, tok), net.ident[:])
                    dve.wait(pe.mark())
                    for p in range(3):
                        n = 3 * part + p
                        weight = logits[:, t, :, n:n + 1].broadcast_to([P, KH, KD])
                        dve.tensor_tensor(product[:, n, :].rearrange("p (h d) -> p h d", h=KH),
                                          bank[:, p * P:(p + 1) * P].rearrange("p (h d) -> p h d", h=KH),
                                          weight, ALU.mult)
                    wide.release(i, dve.mark())
                dve.settle()
                dve.wait(*free.get("o", ()))
                dve.tensor_reduce(o[:, t, :], product[:].rearrange("p n d -> p d n"), AX_X, ALU.add)
                dve.settle()
                yield
            free["logits"] = ()
            if half:
                free["branch", b % 2] = free["v", b % 3] = (pe.mark(), act.mark())
            act.wait(dve.mark())
            act.activation(o_sq[:], o[:], ACT.Square)
            ready = act.mark()
            yield
            dve.wait(ready)
            heads = lambda a: a.rearrange("p t (h d) -> p (t h) d", d=KD)
            flat = small[:, 1, :]
            dve.tensor_reduce(flat, heads(o_sq[:]), AX_X, ALU.add)
            act.wait(dve.mark())
            act.activation(flat, flat, ACT.Sqrt, scale=1.0 / KD, bias=eps[:, 1:2])
            ready = act.mark()
            yield
            dve.wait(ready)
            step.reciprocal(small[:, 0, :], flat)
            step.tensor_tensor(heads(o[:]), heads(o[:]),
                               small[:, 0, :].unsqueeze(2).broadcast_to([P, TPC * KH, KD]), ALU.mult)
            ready = dve.mark()
            yield
            i, bank, readers = wide.take()
            pe.wait(ready, *readers)
            for t in range(TPC):
                pe.transpose(bank[:, t * P:(t + 1) * P], o[:, t, :], net.ident[:])
            act.wait(pe.mark(), *free.get("oT", ()))
            free["o"] = (pe.mark(),)
            act.copy(oT[:], bank)
            ready = act.mark()
            wide.release(i, ready)
            yield
            i, bank, readers = wide.take()
            pe.wait(ready, *readers)
            for t in range(TPC):
                pe.matmul(bank[:, t * P:(t + 1) * P], oT[:, t * P:(t + 1) * P], w_out[:],
                          start=True, stop=True)
            free["oT"] = (pe.mark(),)
            dve.wait(pe.mark())
            first = b * TPB + half * TPC
            x = net.residual[:, first:first + TPC, :].rearrange("p t d -> p (t d)")
            dve.tensor_tensor(x, x, bank, ALU.add)
            wide.release(i, dve.mark())
            yield

    free["zero"] = dve.mark()

    def pairs_of_tiles(b):
        for pair in range(0, PAIRS, 2):
            both = [pair_of_tiles(b, pair + way, way) for way in range(2)]
            while both:
                for one in list(both):
                    if next(one, free) is free:
                        both.remove(one)
                    yield

    def interleave(work, *others):
        due = [0.0 for _ in others]
        for _ in work:
            for n, (other, rate) in enumerate(others):
                due[n] += rate
                while due[n] >= 1:
                    due[n] -= 1
                    next(other, None)

    interleave(prepare(0))
    ending = iter(())
    for b in range(B):
        filtering = filters(b)
        interleave(pairs_of_tiles(b), (filtering, RATE3), (ending, RATE))
        for _ in filtering:
            pass
        if b + 1 < B:
            interleave(prepare(b + 1), (ending, RATE2))
        for _ in ending:
            pass
        ending = finish(b)
    for _ in ending:
        pass
    s.close()


class Net:
    pass


def load_stage(nc, net, stack, dram):
    def sbuf(name, shape, dtype=F32):
        return stack.enter_context(nc.sbuf_tensor(name, shape, dtype))

    s = Stage(nc, net, "load")
    loads = s.landing("loads")

    def load(name, shape, source, dtype=F32):
        buffer = sbuf("w_" + name, shape, dtype)
        s.sp.dma(loads, buffer[:], source)
        return buffer
    net.residual = sbuf("residual", [P, TILES, P])
    s.sp.dma(loads, net.residual[:], dram["x"].rearrange("b (t p) d -> p (b t) d", p=P))
    net.ident = load("ident", [P, P], dram["ident"])
    net.expert_rank = load("expert_rank", [P, EXPERTS], dram["expert_rank"])
    net.router = load("router", [P, EXPERTS], dram["router"])
    net.dram = dram
    s.act.wait(loads.landed())
    s.dve.wait(loads.landed())
    s.pe.wait(loads.landed())
    s.close()


class Weights:
    pass


def ffn_weights(nc, net, stack, name):
    s = Stage(nc, net, name + "w")
    loads = s.landing("loads")
    w = net.ffn = Weights()
    dram = net.dram

    def load(what, shape, source):
        buffer = stack.enter_context(nc.sbuf_tensor("%s_w_%s" % (name, what), shape, F32))
        s.sp.dma(loads, buffer[:], source)
        return buffer
    w.w1 = load("f1", [P, WIDE], dram["w1"])
    w.w2 = load("f2", [P, WIDE], dram["w2w"])
    w.h1 = load("h1", [P, WB, WIDE], dram["h1"].rearrange("(k i) o -> i k o", i=P))
    w.h2 = load("h2", [P, WB, WIDE], dram["h2"].rearrange("(k i) o -> i k o", i=P))
    w.w3 = load("w3", [P, WB, P], dram["w3"].rearrange("(k i) o -> i k o", i=P))
    for n in ("s1", "s2", "h1s", "h2s"):
        buffer = load(n, [P, WB], dram[n])
        if n == "s1":
            w.s1 = buffer
        elif n == "s2":
            w.s2 = buffer
        elif n == "h1s":
            w.h1s = buffer
        else:
            w.h2s = buffer
    s3 = s.sbuf("s3", [P, P])
    s.sp.dma(loads, s3[:], dram["s3"].partition_broadcast(P))
    s.dve.wait(loads.landed())
    wide = s3[:].unsqueeze(1).broadcast_to([P, WB, P])
    s.dve.tensor_tensor(w.w3[:], w.w3[:], wide, ALU.mult)
    s.pe.wait(s.dve.mark())
    s.close()


def store_stage(nc, net):
    s = Stage(nc, net, "store")
    stored = s.landing("stored")
    s.sp.dma(stored, net.dram["out"].rearrange("b (t p) d -> p (b t) d", p=P), net.residual[:])
    s.sp.wait(stored.landed())
    s.close()


def build_network(nc, dram, stages="012345678"):
    net = Net()
    net.done = []
    with ExitStack() as stack:
        load_stage(nc, net, stack, dram)
        if "0" in stages:
            attention_stage(nc, net)
        if "1" in stages:
            moe_stage(nc, net, "moe0")
        if "2" in stages:
            mamba_stage(nc, net)
        if "3" in stages:
            moe_stage(nc, net, "moe1")
        if "4" in stages:
            sparse_stage(nc, net)
        if "5" in stages:
            with ExitStack() as ffn_stack:
                ffn_weights(nc, net, ffn_stack, "ffn0")
                ffn_stage(nc, net, "ffn0")
        if "6" in stages:
            delta_stage(nc, net)
        if "7" in stages:
            with ExitStack() as ffn_stack:
                ffn_weights(nc, net, ffn_stack, "ffn1")
                ffn_stage(nc, net, "ffn1")
        store_stage(nc, net)


def layouts(given):
    def flipped(name):
        return np.ascontiguousarray(np.asarray(given[name]).T)

    def columns(name, n=P):
        return np.ascontiguousarray(np.asarray(given[name]).reshape(-1, n).T)
    a = {
        "x": given["L0_attn_a_x"],
        "router": flipped("L0_ffn_router_w"), "w13": given["L0_ffn_w13"], "w2": given["L0_ffn_w2"],
        "w1": flipped("L1_ffn_w1_w"), "w2w": flipped("L1_ffn_w2_w"), "h1": flipped("L1_ffn_h1_w"),
        "h2": flipped("L1_ffn_h2_w"), "w3": flipped("L1_ffn_w3_w"),
        "s1": columns("L1_ffn_w1_s"), "s2": columns("L1_ffn_w2_s"), "h1s": columns("L1_ffn_h1_s"),
        "h2s": columns("L1_ffn_h2_s"), "s3": given["L1_ffn_w3_s"],
    }
    w_qkv = np.asarray(given["L0_attn_a_w_qkv"])
    b_qkv = np.asarray(given["L0_attn_a_b_qkv"])
    w_rel = np.asarray(given["L0_attn_a_w_rel"])
    a.update({
        "a_qkv": w_qkv, "a_out": given["L0_attn_a_w_out"],
        "a_bqk": b_qkv[:2 * D].reshape(2, D).T, "a_bv": b_qkv[2 * D:].reshape(1, D),
        "a_bout": np.asarray(given["L0_attn_a_b_out"]).reshape(1, D),
        "a_gain": np.stack([given["L0_attn_a_ln_g"], given["L0_attn_a_ln_b"]], 1),
        "a_rel": np.stack([np.repeat(w_rel[0::2], 2, 0).T.reshape(-1),
                           np.repeat(w_rel[1::2], 2, 0).T.reshape(-1)], 1),
    })
    def mamba(name):
        return np.asarray(given["L0_attn_b_" + name])
    dbc, dbc_b = mamba("dbc_W"), mamba("dbc_b")
    blocks = lambda w: w.reshape(CB, P, -1).transpose(1, 0, 2)
    a.update({
        "m_w_in": mamba("in_W"), "m_b_in": mamba("in_b").reshape(2 * CB, P).T,
        "m_conv_w": blocks(mamba("conv_w")), "m_conv_b": mamba("conv_b").reshape(CB, P).T,
        "m_rates": mamba("A_log").reshape(CH // PER, P).T,
        "m_w_delta": blocks(dbc[:, :RANK]),
        "m_w_b": blocks(np.tile(dbc[:, RANK:RANK + STATES], (1, PER))),
        "m_w_c": blocks(np.tile(dbc[:, RANK + STATES:], (1, PER))),
        "m_b_delta": dbc_b[:RANK].reshape(RANK, 1),
        "m_b_bc": np.stack([np.tile(dbc_b[RANK:RANK + STATES], PER),
                            np.tile(dbc_b[RANK + STATES:], PER)], 1),
        "m_w_up": mamba("dup_W"), "m_b_up": mamba("dup_b").reshape(CB, P).T,
        "m_w_out": blocks(mamba("out_W")), "m_b_out": mamba("out_b").reshape(1, P),
        "m_gain": mamba("rms_w").reshape(P, 1),
    })
    def sparse(name):
        return np.asarray(given["L1_attn_a_" + name])
    w_gate = sparse("Wg")
    a.update({
        "s_w_qkv": np.concatenate([sparse("Wq"), sparse("Wk"), sparse("Wv")], 1),
        "s_w_out": sparse("Wo"), "s_w_gate": np.repeat(w_gate[:, :, None], P, 2),
        "s_b_gate": np.tile(sparse("bg"), (P, 1)),
        "s_b_qkv": np.stack([sparse("bq"), sparse("bk"), sparse("bv")], 1),
        "s_b_v": sparse("bv").reshape(1, D), "s_b_out": sparse("bo").reshape(1, D),
    })
    def delta(name):
        return np.asarray(given["L1_attn_b_" + name])
    f = np.float32
    w1, w2 = delta("gate_w1").T, delta("gate_w2").T
    w_stats = np.zeros((P, GATE_WIDE), f)
    w_stats[:GATED] = w1[P:]
    w_alpha = np.zeros((P, GATED), f)
    w_alpha[np.arange(GATED), np.arange(GATED)] = np.tile(delta("alpha_stat"), KH)
    w_alpha[GATED] = delta("gate_b2")
    a.update({
        "d_w_qkv": np.stack([delta(n + "_proj_w").T for n in "qkv"], 1),
        "d_w_beta": np.repeat(delta("b_proj_w"), KD, 0).T,
        "d_conv_w": np.stack([delta(n + "_conv_w") for n in "qkv"], 1),
        "d_fir_w": np.concatenate([delta("fir_w%d" % n) for n in FIR_TAPS], 1),
        "d_w_gate": w1[:P], "d_w_stats": w_stats, "d_b_gate": delta("gate_b1").reshape(GB, P).T,
        "d_w_logit": w2.reshape(GB, P, GATED).transpose(1, 0, 2), "d_w_alpha": w_alpha,
        "d_log_temp": np.tile(np.repeat(delta("gate_log_temp"), BRANCHES), (P, 1)),
        "d_o_gain": np.tile(delta("o_norm_w"), KH).reshape(P, 1), "d_w_out": delta("o_proj_w").T,
    })
    a.update(constants())
    return a


FILL_ROWS = 66 + 4 - QROWS


def constants():
    f = np.float32
    c = {"ident": np.eye(P, dtype=f),
         "expert_rank": np.tile(np.arange(EXPERTS, 0, -1, dtype=f), (P, 1))}
    freq = np.exp(np.arange(0, HD, 2) * (-math.log(10000.0) / HD))
    angle = freq[:, None] * np.arange(T)
    sin, cos = np.sin(angle), np.cos(angle)
    by_sine = np.stack([sin, -cos], 1).reshape(HD, T)
    by_cosine = np.stack([cos, sin], 1).reshape(HD, T)
    c["tables"] = np.stack([np.tile(by_sine, (HEADS, 1)), np.tile(by_cosine, (HEADS, 1))], 1).astype(f)
    psi = np.stack([cos, sin], 1).reshape(HD, T).astype(f)
    bf = mybir.dt.np(BF16)
    parts = []
    rest = psi
    for _ in range(SPLITS):
        parts.append(rest.astype(bf))
        rest = rest - parts[-1].astype(f)
    c["psi"] = np.concatenate([parts[k] for _, k in TERMS] + [np.ones((2, T), bf)])
    select = np.zeros((P, 2, 32), f)
    for h in range(GROUP):
        for d in range(HD):
            select[32 * h + d, 0, HD * h + d] = 1
            select[32 * h + HD, 1, HD * h + d] = 1
    c["head_select"] = select
    c["s_own"] = np.repeat(np.eye(HEADS, dtype=f), HD, 0)
    c["s_block_ones"] = np.kron(np.eye(P // 32), np.ones((32, 32))).astype(f)
    spread_peaks = np.zeros((2 * HEADS, GROUPS, P), f)
    for h in range(HEADS):
        spread_peaks[2 * h:2 * h + 2, h // GROUP, 32 * (h % GROUP):32 * (h % GROUP + 1)] = 1
    c["s_peak_spread"] = spread_peaks.astype(bf)
    c["s_row_base"] = (np.arange(P) // PICKED * BLOCKS).astype(f).reshape(P, 1)
    i = np.arange(P)
    own_tile = np.where(i[None, :] <= i[:, None], 0.0, MASKED)
    before = np.where(i[None, :] > i[:, None], 0.0, MASKED)
    c["s_mask_q"] = np.stack([before, own_tile], 1).astype(bf)
    c["s_mask_k"] = np.stack([own_tile.T, before.T], 1).astype(bf)
    fill = np.zeros((FILL_ROWS, T), f)
    c["s_fill"] = fill.astype(bf)
    for name, at in (("s_fill_picked", FILL_ROWS - 4), ("s_fill_window", FILL_ROWS - 2)):
        rows = fill.copy()
        rows[at:at + 2] = 1
        c[name] = rows.astype(bf)
    spread = np.zeros((SPLITS, 32, SUBS, P), f)
    gather = np.zeros((P, SUBS, 32), f)
    for sub in range(SUBS):
        for ch in range(PER):
            spread[:, PER * sub + ch, sub, STATES * ch:STATES * (ch + 1)] = 1
            gather[STATES * ch:STATES * (ch + 1), sub, PER * sub + ch] = 1
    c["m_spread"] = spread.reshape(SPLITS * 32, SUBS, P).astype(bf)
    c["m_gather"] = gather
    c["d_block_ones"] = c["s_block_ones"]
    c["d_eye"] = np.tile(np.eye(KC), (CPT, 1)).astype(f)
    row, col = np.indices((KC, KC))
    masks = [-(col > row).astype(f), (col >= row).astype(f), ((row ^ col) == 1) & (col > row)]
    for n in range(1, LEVELS):
        masks.append((row >> n == (col >> n) + 1) & (row >> (n + 1) == col >> (n + 1)))
    c["d_masks"] = np.tile(np.stack(masks, 1).astype(f), (CPT, 1, 1))
    select = np.zeros((P, BRANCHES, P), f)
    for h in range(KH):
        for n in range(BRANCHES):
            select[KD * h:KD * (h + 1), n, BRANCHES * h + n] = 1.0 / KD
    c["d_stat_select"] = select
    c["d_stat_one"] = (np.arange(P) == GATED).astype(f).reshape(P, 1)
    return c


def kernel(**inputs):
    import concourse.bacc as bacc
    from concourse.bass_utils import run_bass_kernel_spmd

    nc = bacc.Bacc("TRN2", target_bir_lowering=False, num_devices=1)
    arrays = {f"in_{name}": np.ascontiguousarray(a) for name, a in layouts(inputs).items()}
    dram = {name[3:]: nc.dram_tensor(name, a.shape, mybir.dt.from_np(a.dtype), kind="ExternalInput").ap()
            for name, a in arrays.items()}
    dram["out"] = nc.dram_tensor("out", (B, T, D), F32, kind="ExternalOutput").ap()
    build_network(nc, dram)
    result = run_bass_kernel_spmd(nc, [arrays], core_ids=[0])
    return result.results[0]["out"]
```

```python
from contextlib import ExitStack
import math

import numpy as np

import concourse.bass as bass
from concourse import mybir

F32 = mybir.dt.float32
BF16 = mybir.dt.bfloat16
F16 = mybir.dt.float16
I32 = mybir.dt.int32
U32 = mybir.dt.uint32
ALU = mybir.AluOpType
ACT = mybir.ActivationFunctionType
AX_X = mybir.AxisListType.X

P = 128
B, T, D = 4, 1024, 128
TILES = B * T // P
TPB = T // P
BANK = 512
CHUNKS = B * T // BANK
TPC = BANK // P
LN_EPS = 1e-5
W_SCALE = 64.0


class Engine:

    def __init__(self, name, sem):
        self.name, self.sem, self.count = name, sem, 0
        self.steps, self.last, self.seen = [], None, {}

    def op(self, build):
        self.last = [build, None, 0]
        self.steps.append(self.last)

    def matmul(self, *args, **options):
        self.op(lambda e: e.matmul(*args, **options))

    def transpose(self, *args, **options):
        self.op(lambda e: e.transpose(*args, **options))

    def activation(self, *args, **options):
        self.op(lambda e: e.activation(*args, **options))

    def copy(self, *args, **options):
        self.op(lambda e: e.copy(*args, **options))

    def tensor_copy(self, *args, **options):
        self.op(lambda e: e.tensor_copy(*args, **options))

    def tensor_tensor(self, *args, **options):
        self.op(lambda e: e.tensor_tensor(*args, **options))

    def tensor_scalar(self, *args, **options):
        self.op(lambda e: e.tensor_scalar(*args, **options))

    def scalar_tensor_tensor(self, *args, **options):
        self.op(lambda e: e.scalar_tensor_tensor(*args, **options))

    def tensor_tensor_scan(self, *args, **options):
        self.op(lambda e: e.tensor_tensor_scan(*args, **options))

    def tensor_reduce(self, *args, **options):
        self.op(lambda e: e.tensor_reduce(*args, **options))

    def reciprocal(self, *args, **options):
        self.op(lambda e: e.reciprocal(*args, **options))

    def memset(self, *args, **options):
        self.op(lambda e: e.memset(*args, **options))

    def bn_stats(self, *args, **options):
        self.op(lambda e: e.bn_stats(*args, **options))

    def bn_aggr(self, *args, **options):
        self.op(lambda e: e.bn_aggr(*args, **options))

    def max(self, *args, **options):
        self.op(lambda e: e.max(*args, **options))

    def match_replace(self, *args, **options):
        self.op(lambda e: e.match_replace(*args, **options))

    def mark(self):
        if self.last[1] is None:
            self.count += 1
            self.last[1], self.last[2] = self.sem, 1
        return (self.name, self.sem, self.count)

    def wait(self, *marks):
        for name, sem, value in marks:
            if self.seen.get(name, 0) < value:
                self.seen[name] = value
                self.steps.append([None, sem, value])

    def settle(self):
        self.wait(self.mark())

    def dma(self, landing, out, in_):
        landing.count += 16
        self.steps.append([lambda e: e.dma_start(out, in_), landing.sem, 16])

    def gather(self, landing, out, table, rows):
        landing.count += 16
        self.steps.append([lambda e: e.indirect_dma_start(
            out, None, table, bass.IndirectOffsetOnAxis(rows, 0)), landing.sem, 16])

    def play(self, engine):
        for build, sem, value in self.steps:
            if build is None:
                engine.wait_ge(sem, value)
                continue
            made = build(engine)
            if sem is not None:
                made.then_inc(sem, value)


class Chained:

    def __init__(self, engine):
        self.engine = engine

    def tensor_tensor(self, *args):
        self.engine.tensor_tensor(*args)
        self.engine.settle()

    def tensor_scalar(self, *args):
        self.engine.tensor_scalar(*args)
        self.engine.settle()

    def scalar_tensor_tensor(self, *args):
        self.engine.scalar_tensor_tensor(*args)
        self.engine.settle()

    def tensor_reduce(self, *args):
        self.engine.tensor_reduce(*args)
        self.engine.settle()

    def tensor_copy(self, *args):
        self.engine.tensor_copy(*args)
        self.engine.settle()

    def reciprocal(self, *args):
        self.engine.reciprocal(*args)
        self.engine.settle()


class Landing:

    def __init__(self, name, sem):
        self.name, self.sem, self.count = name, sem, 0

    def landed(self):
        return (self.name, self.sem, self.count)


class Ring:

    def __init__(self, slots):
        self.slots, self.at = slots, 0
        self.readers = [() for _ in slots]

    def take(self):
        i = self.at % len(self.slots)
        self.at += 1
        return i, self.slots[i], self.readers[i]

    def release(self, i, *marks):
        self.readers[i] = marks


class Stage:

    def __init__(self, nc, net, name):
        self.nc, self.net, self.name, self.stack = nc, net, name, ExitStack()
        self.landings = []
        self.pe = Engine(name + "_pe", nc.alloc_semaphore(name + "_pe"))
        self.act = Engine(name + "_act", nc.alloc_semaphore(name + "_act"))
        self.dve = Engine(name + "_dve", nc.alloc_semaphore(name + "_dve"))
        self.pool = Engine(name + "_pool", nc.alloc_semaphore(name + "_pool"))
        self.sp = Engine(name + "_sp", None)
        for engine in (self.pe, self.act, self.dve, self.pool, self.sp):
            engine.wait(*net.done)

    def sbuf(self, name, shape, dtype=F32):
        return self.stack.enter_context(self.nc.sbuf_tensor(self.name + "_" + name, shape, dtype))

    def psum(self, name, shape, dtype=F32):
        return self.stack.enter_context(self.nc.psum_tensor(self.name + "_" + name, shape, dtype))

    def landing(self, name):
        self.landings.append(Landing(self.name + name, self.nc.alloc_semaphore(self.name + "_" + name)))
        return self.landings[-1]

    def close(self):
        self.net.done = [e.mark() for e in (self.pe, self.act, self.dve, self.pool) if e.last]
        self.net.done += [landing.landed() for landing in self.landings]
        with self.nc.Block() as block:
            @block.tensor
            def _(e):
                self.pe.play(e)

            @block.scalar
            def _(e):
                self.act.play(e)

            @block.vector
            def _(e):
                self.dve.play(e)

            @block.gpsimd
            def _(e):
                self.pool.play(e)

            @block.sync
            def _(e):
                self.sp.play(e)
        self.stack.close()


def layer_norm(s, net, xn, second_eps=None, twice=None):
    x = net.residual
    stats = s.sbuf("ln_stats", [P, TILES, 6])
    moments = s.sbuf("ln_moments", [P, TILES, 2])
    std = s.sbuf("ln_std", [P, TILES])
    inv = s.sbuf("ln_inv", [P, TILES])
    eps = s.sbuf("ln_eps", [P, 2])
    s.dve.memset(eps[:, 0:1], LN_EPS)
    s.dve.memset(eps[:, 1:2], second_eps or 0.0)
    if second_eps is not None:
        ratio = s.sbuf("ln_ratio", [P, TILES])
        factor = s.sbuf("ln_factor", [P, TILES])
    marks = []
    groups = [slice(b * TPB, (b + 1) * TPB) for b in range(B)]

    def statistics(group):
        for t in range(group.start, group.stop):
            s.dve.bn_stats(stats[:, t, :], x[:, t, :])
        s.dve.settle()
        for t in range(group.start, group.stop):
            s.dve.bn_aggr(moments[:, t, :], stats[:, t, :])
        s.act.wait(s.dve.mark())
        s.act.activation(std[:, group], moments[:, group, 1], ACT.Sqrt, bias=eps[:, 0:1])
        return s.act.mark()
    root = statistics(groups[0])
    for b, group in enumerate(groups):
        ahead = statistics(groups[b + 1]) if b + 1 < B else None
        s.dve.wait(root)
        step = Chained(s.dve)
        step.reciprocal(inv[:, group], std[:, group])
        if second_eps is not None:
            step.tensor_tensor(ratio[:, group], moments[:, group, 1], inv[:, group], ALU.mult)
            step.tensor_tensor(std[:, group], ratio[:, group], inv[:, group], ALU.mult)
            s.act.wait(s.dve.mark())
            s.act.activation(ratio[:, group], std[:, group], ACT.Sqrt, bias=eps[:, 1:2])
            s.dve.wait(s.act.mark())
            step.reciprocal(factor[:, group], ratio[:, group])
            if twice is xn:
                step.tensor_tensor(inv[:, group], inv[:, group], factor[:, group], ALU.mult)
        for t in range(group.start, group.stop):
            s.dve.tensor_scalar(xn[:, t, :], x[:, t, :], moments[:, t, 0:1], inv[:, t:t + 1],
                                ALU.subtract, ALU.mult)
            if t % TPC == TPC - 1:
                marks += [s.dve.mark()] * TPC
        if second_eps is not None and twice is not xn:
            s.dve.settle()
            for t in range(group.start, group.stop):
                s.dve.tensor_scalar(twice[:, t, :], xn[:, t, :], factor[:, t:t + 1], None, ALU.mult)
                marks[t] = s.dve.mark()
        root = ahead
    return marks


def to_feature_major(s, net, ring, xn, marks, xT, gain=None, shift=None):
    done = []
    for c in range(CHUNKS):
        i, bank, readers = ring.take()
        s.pe.wait(*readers, marks[TPC * c + TPC - 1])
        for j in range(TPC):
            s.pe.transpose(bank[:, j * P:(j + 1) * P], xn[:, TPC * c + j, :], net.ident[:])
        s.act.wait(s.pe.mark())
        out = xT[:, c * BANK:(c + 1) * BANK]
        if gain is None:
            s.act.copy(out, bank)
        elif shift is None:
            s.act.activation(out, bank, ACT.Copy, scale=gain)
        else:
            s.act.activation(out, bank, ACT.Identity, bias=shift, scale=gain)
        done.append(s.act.mark())
        ring.release(i, s.act.mark())
    return done



def high_half(s, value, halves, ready, scale=1.0, engine=None):
    engine = engine or s.dve
    high, low = halves
    s.act.wait(*ready)
    s.act.activation(high, value, ACT.Copy, scale=scale)
    done = s.act.mark()

    def low_half():
        engine.wait(done, *ready)
        if scale == 1.0:
            engine.tensor_tensor(low, value, high, ALU.subtract)
        else:
            engine.scalar_tensor_tensor(low, value, scale, high, ALU.mult, ALU.subtract)
        return (done, engine.mark())
    return low_half


def split_halves(s, value, halves, ready, scale=1.0):
    return high_half(s, value, halves, ready, scale)()


def product_of_halves(pe, out, left, right, first=True, last=True):
    pairs = ((left[0], right[0]), (left[0], right[1]), (left[1], right[0]))
    for i, (a, b) in enumerate(pairs):
        pe.matmul(out, a, b, start=first and i == 0, stop=last and i == 2)


def banks(psum, n, first=0):
    return [psum[:, i, :] for i in range(first, first + n)]


HEADS = 16
HD = D // HEADS
SPLITS = 3
TERMS = ((0, 0), (0, 1), (1, 0), (1, 1), (0, 2), (2, 0))
QROWS = HD * len(TERMS)
GROUP = 4
GROUPS = HEADS // GROUP
STACKS = 3


def split_parts(engine, value, rest, parts):
    step = Chained(engine)
    step.tensor_copy(parts[0], value)
    step.tensor_tensor(rest, value, parts[0], ALU.subtract)
    step.tensor_copy(parts[1], rest)
    step.tensor_tensor(parts[2], rest, parts[1], ALU.subtract)


class Heads:

    def __init__(self, s, scratch, with_v=True):
        self.s, self.scratch = s, scratch
        self.value = s.sbuf("hv", [P, 2, T])
        self.rest = s.sbuf("hr", [P, T])
        self.parts = s.sbuf("hp", [P, 2 * SPLITS, T], BF16)
        self.stored = [s.landing("parts%d" % i) for i in range(2)]
        self.free = ((), ())
        self.parts_free = [(), ()]

    def project(self, b, ring, weights, bias, scale, xT, ready):
        s = self.s
        for n in range(2):
            for half in range(T // BANK):
                i, bank, readers = ring.take()
                s.pe.wait(*readers, ready[b * (T // BANK) + half])
                s.pe.matmul(bank, weights[:, n * P:(n + 1) * P],
                            xT[:, b * T + half * BANK:b * T + (half + 1) * BANK], start=True, stop=True)
                s.act.wait(s.pe.mark(), *self.free[n])
                s.act.activation(self.value[:, n, half * BANK:(half + 1) * BANK], bank, ACT.Identity,
                                 bias=bias[:, n:n + 1], scale=scale if n == 0 else 1.0)
                ring.release(i, s.act.mark())
        s.pool.wait(s.act.mark())
        marks = []
        for n in range(2):
            s.pool.wait(*self.parts_free[n])
            parts = [self.parts[:, SPLITS * n + i, :] for i in range(SPLITS)]
            split_parts(s.pool, self.value[:, n, :], self.rest[:], parts)
            marks.append((s.pool.mark(),))
            s.sp.wait(s.pool.mark())
            s.sp.dma(self.stored[n], self.scratch[b, n].rearrange("s p t -> p s t"),
                     self.parts[:, SPLITS * n:SPLITS * (n + 1), :])
            self.parts_free[n] = (self.stored[n].landed(),)
        self.free = marks


def attention_stage(nc, net):
    s = Stage(nc, net, "attn")
    dram = net.dram
    pe, act, dve, pool, sp = s.pe, s.act, s.dve, s.pool, s.sp
    BROW = QROWS
    MROW = 2 * QROWS
    ROWS = MROW + 2
    scratch = nc.dram_tensor("attn_parts", (B, 2, SPLITS, P, T), BF16, kind="Internal").ap()
    phi_dram = nc.dram_tensor("attn_phi", (SPLITS, P, T), BF16, kind="Internal").ap()

    w_qkv = s.sbuf("w_qkv", [P, 3 * D])
    w_out = s.sbuf("w_out", [P, D])
    bias_qk = s.sbuf("bias_qk", [P, 2])
    bias_v = s.sbuf("bias_v", [1, D])
    bias_out = s.sbuf("bias_out", [1, D])
    gain = s.sbuf("gain", [P, 2])
    w_rel = s.sbuf("w_rel", [P, 2])
    ones = s.sbuf("ones", [1, P])
    loads = s.landing("loads")
    sp.dma(loads, w_qkv[:], dram["a_qkv"])
    sp.dma(loads, w_out[:], dram["a_out"])
    sp.dma(loads, bias_qk[:], dram["a_bqk"])
    sp.dma(loads, bias_v[:], dram["a_bv"])
    sp.dma(loads, bias_out[:], dram["a_bout"])
    sp.dma(loads, gain[:], dram["a_gain"])
    sp.dma(loads, w_rel[:], dram["a_rel"])
    select = s.sbuf("select", [P, 2, 32])
    sp.dma(loads, select[:], dram["head_select"])
    ident_bf = s.sbuf("ident_bf", [P, P], BF16)

    q_stack = s.sbuf("q_stack", [P, STACKS, GROUP, T], BF16)
    k_stack = s.sbuf("k_stack", [P, STACKS, GROUP, T], BF16)
    values = s.sbuf("values", [P, 2, TPB, HEADS, HD + 1])
    xT = s.sbuf("xT", [P, B * T])
    ps = s.psum("ps", [P, 8, BANK])
    key_ring = Ring(banks(ps, 3))
    score_ring = Ring(banks(ps, 3, 3))
    out_acc = ps[:, 6:8, :]
    scale = HD ** -0.5
    constants_in = s.landing("constants")
    for slot in range(STACKS):
        for h in range(GROUP):
            sp.dma(constants_in, k_stack[BROW:ROWS, slot, h, :], dram["psi"])

    weights_sb = s.sbuf("weights", [P, 2, GROUP, BANK])
    xn = weights_sb[:].rearrange("p a h (t d) -> p (a h t) d", d=P)
    marks = layer_norm(s, net, xn, LN_EPS, xn)
    act.wait(loads.landed())
    ready = to_feature_major(s, net, Ring(banks(ps, 8)), xn, marks, xT, gain[:, 0:1], gain[:, 1:2])
    after_ln = (ready[-1], pe.mark())
    pool.wait(*after_ln)
    dve.wait(*after_ln)

    tables = s.sbuf("tables", [P, 2, T])
    sp.wait(*after_ln)
    table_in = s.landing("tables")
    sp.dma(table_in, tables[:], dram["tables"])
    heads = Heads(s, scratch)
    dve.wait(table_in.landed(), loads.landed())
    step = Chained(dve)
    phi = tables[:, 1, :]
    step.tensor_scalar(tables[:, 0, :], tables[:, 0, :], w_rel[:, 0:1], None, ALU.mult)
    step.scalar_tensor_tensor(phi, phi, w_rel[:, 1:2], tables[:, 0, :], ALU.mult, ALU.add)
    phi_parts = [q_stack[:, 0, i, :] for i in range(SPLITS)]
    split_parts(dve, phi, tables[:, 0, :], phi_parts)
    sp.wait(dve.mark())
    phi_stored = s.landing("phi")
    sp.dma(phi_stored, phi_dram.rearrange("s p t -> p s t"), q_stack[:, 0, 0:SPLITS, :])
    step.tensor_scalar(bias_qk[:, 0:1], bias_qk[:, 0:1], scale, None, ALU.mult)
    dve.tensor_copy(ident_bf[:], net.ident[:])
    dve.memset(values[:, :, :, :, HD], 1.0)
    dve.memset(ones[:], 1.0)
    dve.memset(out_acc, 0.0)
    start = dve.mark()
    act.wait(start)
    pe.wait(start, loads.landed())

    value_free = [(), ()]

    def prepare(b):
        heads.project(b, key_ring, w_qkv, bias_qk, scale, xT, ready)
        act.wait(*value_free[b % 2])
        for c in range(T // BANK):
            i, bank, readers = key_ring.take()
            pe.wait(*readers)
            for j in range(TPC):
                cols = bank[:, j * P:(j + 1) * P]
                token = b * T + (TPC * c + j) * P
                pe.matmul(cols, xT[:, token:token + P], w_qkv[:, 2 * D:3 * D], start=True, stop=False)
                pe.matmul(cols, ones[:], bias_v[:], start=False, stop=True)
            act.wait(pe.mark())
            act.copy(values[:, b % 2, TPC * c:TPC * (c + 1), :, 0:HD],
                     bank.rearrange("p (j h d) -> p j h d", j=TPC, h=HEADS))
            key_ring.release(i, act.mark())
        return act.mark()

    stack_in = [s.landing("stack%d" % i) for i in range(STACKS)]
    stack_free = [() for _ in range(STACKS)]

    def assemble(g):
        b, first, slot = g // GROUPS, GROUP * (g % GROUPS), g % STACKS
        sp.wait(phi_stored.landed(), constants_in.landed(), *stack_free[slot])
        sp.wait(*heads.parts_free[0], *heads.parts_free[1])
        rows = slice(first * HD, (first + GROUP) * HD)
        for i, (qpart, kpart) in enumerate(TERMS):
            at = slice(HD * i, HD * (i + 1))
            bias_at = slice(BROW + HD * i, BROW + HD * (i + 1))
            for stack, where, source in ((q_stack, at, scratch[b, 0, qpart, rows, :]),
                                         (k_stack, at, scratch[b, 1, kpart, rows, :]),
                                         (q_stack, bias_at, phi_dram[qpart, rows, :])):
                sp.dma(stack_in[slot], stack[where, slot, :, :],
                       source.rearrange("(h d) t -> d h t", d=HD))

    peak_halves = s.sbuf("peak_halves", [P, STACKS, T // BANK, TPB * GROUP])
    peak = s.sbuf("peak", [P, STACKS, TPB * GROUP])
    peak_parts = s.sbuf("peak_parts", [P, STACKS, TPB, 2 * GROUP], BF16)
    peak_rows = s.sbuf("peak_rows", [2 * GROUP, STACKS, T], BF16)
    peaks_in = [s.landing("peaks%d" % i) for i in range(STACKS)]
    peak_free = [() for _ in range(STACKS)]

    def score(g, unit):
        half, h, t, slot = unit % 2, unit // 2 % GROUP, unit // (2 * GROUP), g % STACKS
        if unit == 0:
            pe.wait(stack_in[slot].landed())
            dve.wait(*peak_free[slot])
        i, bank, readers = score_ring.take()
        pe.wait(*readers)
        pe.matmul(bank, q_stack[0:MROW, slot, h, t * P:(t + 1) * P],
                  k_stack[0:MROW, slot, h, half * BANK:(half + 1) * BANK], start=True, stop=True)
        dve.wait(pe.mark())
        at = t * GROUP + h
        dve.tensor_reduce(peak_halves[:, slot, half, at:at + 1], bank, AX_X, ALU.max)
        score_ring.release(i, dve.mark())

    def peaks(g):
        slot = g % STACKS
        parts = peak_parts[:, slot].rearrange("p t (h s) -> p (t h) s", s=2)
        dve.settle()
        dve.tensor_tensor(peak[:, slot], peak_halves[:, slot, 0], peak_halves[:, slot, 1], ALU.max)
        dve.settle()
        dve.tensor_scalar(parts[:, :, 0], peak[:, slot], -1.0, None, ALU.mult)
        dve.settle()
        dve.scalar_tensor_tensor(parts[:, :, 1], peak[:, slot], -1.0, parts[:, :, 0], ALU.mult,
                                 ALU.subtract)
        pe.wait(dve.mark())
        for half in range(T // BANK):
            i, bank, readers = key_ring.take()
            pe.wait(*readers)
            for j in range(TPC):
                pe.matmul(bank[0:2 * GROUP, j * P:(j + 1) * P], peak_parts[:, slot, TPC * half + j, :],
                          ident_bf[:], start=True, stop=True)
            act.wait(pe.mark())
            act.copy(peak_rows[:, slot, half * BANK:(half + 1) * BANK], bank[0:2 * GROUP, :])
            key_ring.release(i, act.mark())
        sp.wait(act.mark())
        for h in range(GROUP):
            sp.dma(peaks_in[slot], q_stack[MROW:ROWS, slot, h, :],
                   peak_rows[2 * h:2 * h + 2, slot, :])
        peak_free[slot] = (pe.mark(), peaks_in[slot].landed())

    weight_ring = Ring([weights_sb[:, i] for i in range(2)])
    acc_free = [()]

    def exponentials(g, key_tile, half, between):
        slot = g % STACKS
        if key_tile == 0 and half == 0:
            pe.wait(peaks_in[slot].landed())
        w, weights, free = weight_ring.take()
        marks = []
        for h in range(GROUP):
            i, bank, readers = key_ring.take()
            pe.wait(*readers)
            pe.matmul(bank, k_stack[0:ROWS, slot, h, key_tile * P:(key_tile + 1) * P],
                      q_stack[0:ROWS, slot, h, half * BANK:(half + 1) * BANK], start=True, stop=True)
            act.wait(pe.mark(), *free)
            act.activation(weights[:, h, :], bank, ACT.Exp)
            key_ring.release(i, act.mark())
            last = act.mark()
            between(h)
        if key_tile == TPB - 1 and half == T // BANK - 1:
            stack_free[slot] = (pe.mark(),)
        return w, weights, last

    def weigh(g, key_tile, half, w, weights, mark):
        b, first = g // GROUPS, GROUP * (g % GROUPS)
        pe.wait(mark, *acc_free[0])
        for h in range(GROUP):
            pe.matmul(out_acc[32 * h:32 * h + HD + 1, half, :], values[:, b % 2, key_tile, first + h, :],
                      weights[:, h, :], start=key_tile == 0, stop=key_tile == TPB - 1)
        weight_ring.release(w, pe.mark())
        if key_tile == TPB - 1 and half == T // BANK - 1:
            act.wait(pe.mark())
            act.copy(sums[:, g % GROUPS, :], out_acc.rearrange("p c t -> p (c t)"))
            acc_free[0] = (act.mark(),)
            if g % GROUPS == GROUPS - 1:
                value_free[b % 2] = (pe.mark(),)
                sums_ready[0] = act.mark()

    sums = s.sbuf("sums", [P, GROUPS, T])
    sums_ready = [None]
    inverse = s.sbuf("inverse", [P, BANK])
    mixed = s.sbuf("mixed", [P, 2, BANK])
    mixed_free = [(), ()]
    mixed_ready = [None, None]

    def normalise(half):
        pe.wait(sums_ready[0])
        found = []
        for what in range(2):
            i, bank, readers = key_ring.take()
            pe.wait(*readers)
            for group in range(GROUPS):
                pe.matmul(bank[32 * group:32 * (group + 1), :], select[:, what, :],
                          sums[:, group, half * BANK:(half + 1) * BANK], start=True, stop=True)
            found.append((i, bank))
        dve.wait(pe.mark(), *mixed_free[half])
        dve.reciprocal(inverse[:], found[1][1])
        dve.settle()
        dve.tensor_tensor(mixed[:, half, :], found[0][1], inverse[:], ALU.mult)
        key_ring.release(found[0][0], dve.mark())
        key_ring.release(found[1][0], dve.mark())
        mixed_ready[half] = dve.mark()

    def project_out(b, half):
        i, bank, readers = key_ring.take()
        pe.wait(mixed_ready[half], *readers)
        for j in range(TPC):
            cols = bank[:, j * P:(j + 1) * P]
            pe.matmul(cols, mixed[:, half, j * P:(j + 1) * P], w_out[:], start=True, stop=False)
            pe.matmul(cols, ones[:], bias_out[:], start=False, stop=True)
        mixed_free[half] = (pe.mark(),)
        dve.wait(pe.mark())
        tile = b * TPB + half * TPC
        x = net.residual[:, tile:tile + TPC, :].rearrange("p t d -> p (t d)")
        dve.tensor_tensor(x, bank, x, ALU.add)
        key_ring.release(i, dve.mark())

    units = GROUP * TPB * T // BANK
    total = B * GROUPS
    value_ready = [prepare(0)]
    assemble(0)
    assemble(1)
    for unit in range(units):
        score(0, unit)
    peaks(0)
    pending = []
    steps = [(k, half) for k in range(TPB) for half in range(T // BANK)]
    ahead = len(steps) - 3
    for g in range(total):
        b = g // GROUPS
        if g + 2 < total:
            assemble(g + 2)
        if g % GROUPS == 1 and b + 1 < B:
            value_ready.append(prepare(b + 1))
        done = 0
        for n, (key_tile, half) in enumerate(steps):
            def between(h):
                nonlocal done
                goal = min(units, (GROUP * n + h + 1) * units // (GROUP * ahead))
                while g + 1 < total and done < goal:
                    score(g + 1, done)
                    done += 1
            made = exponentials(g, key_tile, half, between)
            if pending:
                weigh(*pending.pop())
            if g % GROUPS == 0 and n == 0:
                pe.wait(value_ready[b])
            pending.append((g, key_tile, half) + made)
            if n in (3, 6) and g and g % GROUPS == 0:
                normalise(n // 6)
            if n in (5, 8) and g and g % GROUPS == 0:
                project_out(b - 1, n // 8)
            if g + 1 < total and n == ahead:
                peaks(g + 1)
    weigh(*pending.pop())
    normalise(0)
    normalise(1)
    project_out(B - 1, 0)
    project_out(B - 1, 1)
    s.close()


EXPERTS, HIDDEN_E = 8, 256
EB = HIDDEN_E // P


def moe_stage(nc, net, name):
    s = Stage(nc, net, name)
    xn = s.sbuf("xn", [P, TILES, P])
    xT = s.sbuf("xT", [P, B * T])
    probs = s.sbuf("probs", [P, TILES, EXPERTS])
    left = s.sbuf("left", [P, TILES, EXPERTS])
    key = s.sbuf("key", [P, TILES, EXPERTS])
    chosen = s.sbuf("chosen", [P, TILES, EXPERTS])
    weights = s.sbuf("weights", [P, TILES, EXPERTS])
    best = s.sbuf("best", [P, TILES])
    total = s.sbuf("total", [P, TILES])
    gate_sb = s.sbuf("gate", [P, 3, BANK])
    exact_sb = s.sbuf("exact", [P, 3, BANK])
    hidden = s.sbuf("hidden", [P, 2, EB, 2, BANK], F16)
    xT_halves = s.sbuf("xT_halves", [P, 2, B * T], F16)
    w13_halves = s.sbuf("w13_halves", [P, 2, EXPERTS, 2 * HIDDEN_E], F16)
    w2_halves = s.sbuf("w2_halves", [P, 2, EXPERTS, EB, P], F16)
    w13 = s.sbuf("w13", [P, EXPERTS, 2 * HIDDEN_E])
    w2 = s.sbuf("w2", [P, EXPERTS, EB, P])
    loads = s.landing("loads")
    s.sp.dma(loads, w13[:], net.dram["w13"].rearrange("e d i -> d e i"))
    s.sp.dma(loads, w2[:], net.dram["w2"].rearrange("e (k i) d -> i e k d", i=P))
    ps = s.psum("ps", [P, 8, BANK])
    pe, act, dve = s.pe, s.act, s.dve
    ring = Ring(banks(ps, 2))
    marks = layer_norm(s, net, xn)
    halves = lambda a: (a[:, 0], a[:, 1])
    ready = to_feature_major(s, net, ring, xn, marks, xT)

    tokens_ready = [split_halves(s, xT[:, c * BANK:(c + 1) * BANK],
                                 halves(xT_halves[:, :, c * BANK:(c + 1) * BANK]), (ready[c],))
                    for c in range(CHUNKS)]

    act.wait(loads.landed())
    ready_weights = []

    def split_expert(e_):
        done = ()
        for w, both in ((w13, w13_halves), (w2, w2_halves)):
            act.activation(w[:, e_], w[:, e_], ACT.Copy, scale=W_SCALE)
            act.settle()
            done += high_half(s, w[:, e_], halves(both[:, :, e_]), (act.mark(),), engine=s.pool)()
        ready_weights.append(done)
    for e_ in range(2):
        split_expert(e_)

    logits = ps[:, 7, 0:TILES * EXPERTS].rearrange("p (t e) -> p t e", e=EXPERTS)
    for t in range(TILES):
        pe.wait(ready[t // TPC])
        pe.matmul(logits[:, t, :], xT[:, t * P:(t + 1) * P], net.router[:], start=True, stop=True)
    dve.wait(pe.mark())
    wide = lambda a: a[:].unsqueeze(2).broadcast_to([P, TILES, EXPERTS])

    step = Chained(dve)
    step.tensor_reduce(best[:], logits, AX_X, ALU.max)
    step.tensor_tensor(left[:], logits, wide(best), ALU.subtract)
    logits_read = dve.mark()
    act.wait(dve.mark())
    act.activation(key[:], left[:], ACT.Exp)
    dve.wait(act.mark())
    step.tensor_reduce(total[:], key[:], AX_X, ALU.add)
    step.reciprocal(best[:], total[:])
    step.tensor_tensor(probs[:], key[:], wide(best), ALU.mult)

    rank = net.expert_rank[:].unsqueeze(1).broadcast_to([P, TILES, EXPERTS])

    def take_best(source, into, top):
        step.tensor_reduce(top[:], source[:], AX_X, ALU.max)
        step.tensor_tensor(key[:], source[:], wide(top), ALU.is_equal)
        step.tensor_tensor(key[:], key[:], rank, ALU.mult)
        step.tensor_reduce(best[:], key[:], AX_X, ALU.max)
        step.tensor_tensor(into[:], key[:], wide(best), ALU.is_equal)
    second = s.sbuf("second", [P, TILES])
    take_best(probs, chosen, total)
    step.scalar_tensor_tensor(left[:], chosen[:], -2.0, probs[:], ALU.mult, ALU.add)
    take_best(left, weights, second)
    step.tensor_tensor(chosen[:], chosen[:], weights[:], ALU.add)
    step.tensor_tensor(chosen[:], chosen[:], probs[:], ALU.mult)
    step.scalar_tensor_tensor(best[:], total[:], 1e-6, second[:], ALU.add, ALU.add)
    step.reciprocal(total[:], best[:])
    step.tensor_tensor(weights[:], chosen[:], wide(total), ALU.mult)
    step.tensor_scalar(weights[:], weights[:], 1.0 / W_SCALE, None, ALU.mult)

    pairs = Ring([(ps[:, 2 * i, :], ps[:, 2 * i + 1, :]) for i in range(3)])
    for i in range(2):
        pairs.release(0, *ring.readers[0], *ring.readers[1])
    outs = Ring([ps[:, 6, :], ps[:, 7, :]])
    outs.release(1, logits_read)
    gates = Ring([gate_sb[:, i, :] for i in range(3)])
    hiddens = Ring([hidden[:, i] for i in range(2)])
    exacts = Ring([exact_sb[:, i, :] for i in range(3)])

    def down(e_, c, hs, h_slot, h_marks):
        i, out, readers = outs.take()
        pe.wait(*readers, *h_marks)
        for j in range(TPC):
            for k in range(EB):
                product_of_halves(pe, out[:, j * P:(j + 1) * P],
                                  halves(hs[:, k, :, j * P:(j + 1) * P]),
                                  halves(w2_halves[:, :, e_, k, :]), k == 0, k == EB - 1)
        hiddens.release(h_slot, pe.mark())
        dve.wait(pe.mark(), *added.get(c, ()))
        for j in range(TPC):
            t = TPC * c + j
            x = net.residual[:, t, :]
            dve.scalar_tensor_tensor(
                x, out[:, j * P:(j + 1) * P], weights[:, t, e_:e_ + 1], x, ALU.mult, ALU.add)
        outs.release(i, dve.mark())
        added[c] = (dve.mark(),)

    added = {}
    waiting = None
    for c in range(CHUNKS):
        tokens = slice(c * BANK, (c + 1) * BANK)
        for e_ in range(EXPERTS):
            pe.wait(*ready_weights[e_])
            if c == 0 and e_ + 2 < EXPERTS:
                split_expert(e_ + 2)
            h_slot, hs, h_readers = hiddens.take()
            h_marks = []
            for k in range(EB):
                i, (gate, up), readers = pairs.take()
                pe.wait(*readers, *tokens_ready[c])
                for out, base in ((gate, 0), (up, HIDDEN_E)):
                    product_of_halves(pe, out,
                                      halves(w13_halves[:, :, e_, base + k * P:base + (k + 1) * P]),
                                      halves(xT_halves[:, :, tokens]))
                g, gate_s, g_readers = gates.take()
                act.wait(pe.mark(), *g_readers)
                act.activation(gate_s, gate, ACT.Silu, scale=1.0 / W_SCALE)
                x_slot, exact, x_readers = exacts.take()
                dve.wait(act.mark(), *x_readers)
                dve.scalar_tensor_tensor(exact, up, 1.0 / W_SCALE, gate_s, ALU.mult, ALU.mult)
                gates.release(g, dve.mark())
                pairs.release(i, dve.mark())
                split = high_half(s, exact, halves(hs[:, k]), (dve.mark(), *h_readers),
                                  engine=s.pool)()
                exacts.release(x_slot, *split)
                h_marks += split
            if waiting:
                down(*waiting)
            waiting = (e_, c, hs, h_slot, h_marks)
    down(*waiting)
    s.close()


CH, STATES, TAPS = 256, 16, 4
CB = CH // P
RANK = CH // 16
PER = P // STATES
SUBS = 32 // PER
RMS_EPS = 1e-6


def mamba_stage(nc, net):
    s = Stage(nc, net, "mamba")
    dram = net.dram
    pe, act, dve, pool, sp = s.pe, s.act, s.dve, s.pool, s.sp
    loads = s.landing("loads")

    def load(name, shape, dtype=F32):
        buffer = s.sbuf(name, shape, dtype)
        sp.dma(loads, buffer[:], dram["m_" + name])
        return buffer
    w_in = load("w_in", [P, 2 * CH])
    b_in = load("b_in", [P, 2 * CB])
    conv_w = load("conv_w", [P, CB, TAPS])
    conv_b = load("conv_b", [P, CB])
    rates = load("rates", [P, CH // PER])
    w_delta = load("w_delta", [P, CB, RANK])
    w_b = load("w_b", [P, CB, P])
    w_c = load("w_c", [P, CB, P])
    b_delta = load("b_delta", [RANK, 1])
    b_bc = load("b_bc", [P, 2])
    w_up = load("w_up", [RANK, CH])
    b_up = load("b_up", [P, CB])
    w_out = load("w_out", [P, CB, P])
    b_out = load("b_out", [1, P])
    gain = load("gain", [P, 1])
    spread = load("spread", [3 * 32, SUBS, P], BF16)
    gather = load("gather", [P, SUBS, 32])
    ones = s.sbuf("ones", [1, P])
    xT = s.sbuf("xT", [P, B * T])
    padded = s.sbuf("padded", [P, CB, TAPS - 1 + T])
    x1 = s.sbuf("x1", [P, CB, T])
    gate = s.sbuf("gate", [P, 2, CB, T])
    low = s.sbuf("low", [RANK, T])
    temp = s.sbuf("temp", [P, 2, T])
    parts = s.sbuf("parts", [P, SPLITS, CB, 2, T], BF16)
    stack = s.sbuf("stack", [3 * 32, CB, 2, 4, T], BF16)
    b_rep = s.sbuf("b_rep", [P, 2, T])
    c_rep = s.sbuf("c_rep", [P, 2, T])
    driven = s.sbuf("driven", [P, 2, T])
    states = s.sbuf("states", [P, 3, T])
    out_c = s.sbuf("out_c", [P, 6, T])
    ps = s.psum("ps", [P, 8, BANK])
    pair = lambda i: ps[:, i:i + 2, :].rearrange("p a t -> p (a t)")

    xn = x1_view = out_c[:, 0:4, :].rearrange("p a (t d) -> p (a t) d", d=P)
    twice = gate[:].rearrange("p a b (t d) -> p (a b t) d", d=P)
    marks = layer_norm(s, net, xn, RMS_EPS, twice)
    act.wait(loads.landed())
    pe.wait(loads.landed())
    ready = to_feature_major(s, net, Ring(banks(ps, 8)), twice, marks, xT, gain[:, 0:1])
    x = net.residual[:].rearrange("p t d -> p (t d)")
    dve.tensor_tensor(x, x, xn.rearrange("p t d -> p (t d)"), ALU.add)
    dve.settle()
    act.wait(ready[-1], pe.mark())
    pool.wait(dve.mark())
    act.activation(rates[:], rates[:], ACT.Exp)
    act.settle()
    act.activation(rates[:], rates[:], ACT.Copy, scale=-1.0)
    dve.memset(padded[:, :, 0:TAPS - 1], 0.0)
    dve.memset(ones[:], 1.0)
    dve.wait(loads.landed(), ready[-1])
    act.wait(dve.mark())
    pe.wait(dve.mark(), act.mark())

    steps_ring = Ring([(pair(0)), (pair(2))])
    input_ring = Ring([pair(4)])
    summed = pair(6)
    driven_ring = Ring([driven[:, i, :] for i in range(2)])
    state_ring = Ring([states[:, i, :] for i in range(3)])
    product_ring = Ring([out_c[:, i, :] for i in range(6)])
    stack_in = [s.landing("stack%d" % i) for i in range(CB)]
    free = {}

    def project(slot, weights, source, rows=P):
        for half in range(T // BANK):
            cols = slice(half * BANK, (half + 1) * BANK)
            for k in range(len(source)):
                pe.matmul(slot[0:rows, cols], weights[k], source[k][:, cols],
                          start=k == 0, stop=k == len(source) - 1)

    def channels(b):
        tokens = slice(b * T, (b + 1) * T)
        filled = []
        for m in range(CB):
            i, slot, readers = steps_ring.take()
            pe.wait(*readers)
            project(slot, [w_in[:, m * P:(m + 1) * P]], [xT[:, tokens]])
            act.wait(pe.mark(), *free.get("padded", ()))
            act.activation(padded[:, m, TAPS - 1:], slot, ACT.Identity, bias=b_in[:, m:m + 1])
            filled.append(act.mark())
            steps_ring.release(i, act.mark())
            yield
        for m in range(CB):
            i, slot, readers = steps_ring.take()
            pe.wait(*readers)
            project(slot, [w_in[:, CH + m * P:CH + (m + 1) * P]], [xT[:, tokens]])
            act.wait(pe.mark(), *free.get(("gate", b % 2), ()))
            act.activation(gate[:, b % 2, m, :], slot, ACT.Silu, bias=b_in[:, CB + m:CB + m + 1])
            steps_ring.release(i, act.mark())
            yield
        dve.wait(*filled, *free.get("x1", ()))
        for m in range(CB):
            dve.tensor_scalar(x1[:, m, :], padded[:, m, 0:T], conv_w[:, m, 0:1], conv_b[:, m:m + 1],
                              ALU.mult, ALU.add)
        for k in range(1, TAPS):
            dve.settle()
            for m in range(CB):
                dve.scalar_tensor_tensor(x1[:, m, :], padded[:, m, k:k + T], conv_w[:, m, k:k + 1],
                                         x1[:, m, :], ALU.mult, ALU.add)
            ready = dve.mark()
            yield
        free["padded"] = (ready,)
        act.wait(ready)
        act.activation(x1[:], x1[:], ACT.Silu)
        silu = act.mark()
        yield
        source = [x1[:, k, :] for k in range(CB)]
        pe.wait(silu)
        act.wait(*free.get("low", ()), *free.get(("rep", b % 2), ()))
        for weights, into, bias in ((w_delta, low[:], b_delta[:, 0:1]),
                                    (w_b, b_rep[:, b % 2, :], b_bc[:, 0:1]),
                                    (w_c, c_rep[:, b % 2, :], b_bc[:, 1:2])):
            rows = RANK if weights is w_delta else P
            for half in range(T // BANK):
                cols = slice(half * BANK, (half + 1) * BANK)
                i, slot, readers = steps_ring.take()
                pe.wait(*readers)
                for k in range(CB):
                    pe.matmul(slot[0:rows, cols], weights[:, k, :], source[k][:, cols], start=k == 0,
                              stop=k == CB - 1)
                act.wait(pe.mark())
                act.activation(into[:, cols], slot[0:rows, cols], ACT.Identity, bias=bias)
                steps_ring.release(i, act.mark())
                if weights is w_delta:
                    free["low ready"] = act.mark()
                yield
        free["bc", b % 2] = act.mark()
        free["x1"] = (silu, pe.mark())

    def step_sizes(b, m):
        i, slot, readers = steps_ring.take()
        pe.wait(free["low ready"], *readers)
        project(slot, [w_up[:, m * P:(m + 1) * P]], [low[:]])
        free["low"] = (pe.mark(),)
        delta, other = temp[:, 0, :], temp[:, 1, :]
        act.wait(pe.mark(), *free.get("temp", ()))
        act.activation(other, slot, ACT.Abs, bias=b_up[:, m:m + 1])
        dve.wait(act.mark())
        dve.tensor_scalar(delta, slot, b_up[:, m:m + 1], 0.0, ALU.add, ALU.max)
        steps_ring.release(i, dve.mark())
        act.settle()
        act.activation(other, other, ACT.Exp, scale=-1.0)
        act.settle()
        act.activation(other, other, ACT.Ln, bias=1.0)
        ready = act.mark()
        yield
        dve.wait(ready)
        dve.settle()
        dve.tensor_tensor(delta, delta, other, ALU.add)
        dve.settle()
        summed_up = dve.mark()
        dve.tensor_tensor(other, delta, x1[:, m, :], ALU.mult)
        times_x1 = dve.mark()
        free["x1"] += (times_x1,)
        into = lambda k, what: parts[:, k, m, what, :]
        values = ((0, delta, summed_up), (1, other, times_x1))
        yield
        for k in range(2):
            copied = []
            for what, value, ready in values:
                act.wait(ready, *free.get(("parts", m), ()))
                act.copy(into(k, what), value)
                copied.append(act.mark())
            yield
            rest = []
            for (what, value, _), ready in zip(values, copied):
                dve.wait(ready)
                out = value if k == 0 else into(2, what)
                dve.tensor_tensor(out, value, into(k, what), ALU.subtract)
                rest.append((what, value, dve.mark()))
            values = rest
            yield
        free["temp"] = free["parts ready", m] = (values[-1][2], copied[-1])

    def restack(m):
        sp.wait(*free["parts ready", m], *free.get(("stack", m), ()))
        for k in range(SPLITS):
            for q in range(4):
                sp.dma(stack_in[m], stack[32 * k:32 * (k + 1), m, :, q, :],
                       parts[32 * q:32 * (q + 1), k, m, :, :])
        free["parts", m] = (stack_in[m].landed(),)
        free["stacked", m] = stack_in[m].landed()

    def scan(b, m, sub, q):
        group = (m * P + 32 * q + PER * sub) // PER
        i, slot, readers = steps_ring.take()
        pe.wait(free["stacked", m], *readers)
        project(slot, [spread[:, sub, :]], [stack[:, m, 0, q, :]])
        act.wait(pe.mark())
        act.activation(slot, slot, ACT.Exp, scale=rates[:, group:group + 1])
        decays = act.mark()
        j, inputs, readers = input_ring.take()
        pe.wait(*readers)
        project(inputs, [spread[:, sub, :]], [stack[:, m, 1, q, :]])
        d, drive, readers = driven_ring.take()
        dve.wait(pe.mark(), *readers, free["bc", b % 2])
        dve.tensor_tensor(drive, inputs, b_rep[:, b % 2, :], ALU.mult)
        input_ring.release(j, dve.mark())
        k, state, readers = state_ring.take()
        dve.wait(decays, *readers)
        dve.settle()
        dve.tensor_tensor_scan(state, slot, drive, 0.0, ALU.mult, ALU.add)
        steps_ring.release(i, dve.mark())
        driven_ring.release(d, dve.mark())
        n, product, readers = product_ring.take()
        pool.wait(dve.mark(), *readers, free["bc", b % 2])
        pool.tensor_tensor(product, state, c_rep[:, b % 2, :], ALU.mult)
        state_ring.release(k, pool.mark())
        return n, product, pool.mark(), sub, q

    def sum_states(items):
        pe.wait(*free.get("summed", ()))
        for half in range(T // BANK):
            for n, product, mark, sub, q in items:
                pe.wait(mark)
                pe.matmul(summed[32 * q:32 * (q + 1), half * BANK:(half + 1) * BANK], gather[:, sub, :],
                          product[:, half * BANK:(half + 1) * BANK], start=sub == 0,
                          stop=sub == SUBS - 1)
        for n, *_ in items:
            product_ring.release(n, pe.mark())

    def gated(b, m):
        dve.wait(pe.mark())
        g = gate[:, b % 2, m, :]
        dve.tensor_tensor(g, summed, g, ALU.mult)
        free["summed"] = (dve.mark(),)

    def project_out(b):
        slot = summed
        pe.wait(*free["summed"])
        for t in range(TPB):
            for k in range(CB):
                pe.matmul(slot[:, t * P:(t + 1) * P], gate[:, b % 2, k, t * P:(t + 1) * P],
                          w_out[:, k, :], start=k == 0, stop=False)
            pe.matmul(slot[:, t * P:(t + 1) * P], ones[:], b_out[:], start=False, stop=True)
        projected = pe.mark()
        free["gate", b % 2] = (projected,)
        yield
        dve.wait(projected)
        xb = x[:, b * T:(b + 1) * T]
        dve.tensor_tensor(xb, xb, slot, ALU.add)
        free["summed"] = (dve.mark(),)

    def all_of(*works):
        for work in works:
            yield from work

    for _ in all_of(channels(0), step_sizes(0, 0)):
        pass
    restack(0)
    for _ in step_sizes(0, 1):
        pass
    restack(1)
    scans = SUBS * 4
    waiting, ending = None, iter(())
    for b in range(B):
        nxt = b + 1 < B
        first = all_of(channels(b + 1), step_sizes(b + 1, 0)) if nxt else iter(())
        second = step_sizes(b + 1, 1) if nxt else iter(())
        for m in range(CB):
            for sub in range(SUBS):
                items = []
                for q in range(4):
                    items.append(scan(b, m, sub, q))
                    if q == 1 and waiting:
                        sum_states(waiting[0])
                        if waiting[1] is not None:
                            gated(*waiting[1])
                            if waiting[1][1] == CB - 1:
                                ending = project_out(waiting[1][0])
                                next(ending)
                    if q == 3:
                        next(ending, None)
                    at = m * scans + 4 * sub + q
                    if at >= 4:
                        next(first, None)
                    if nxt and at == scans + 9:
                        for _ in first:
                            pass
                        restack(0)
                    if at > scans + 9:
                        next(second, None)
                if sub == SUBS - 1:
                    free["stack", m] = (pe.mark(),)
                waiting = (items, (b, m) if sub == SUBS - 1 else None)
        if nxt:
            for _ in second:
                pass
            restack(1)
        free["rep", b % 2] = (dve.mark(), pool.mark())
    sum_states(waiting[0])
    gated(*waiting[1])
    for _ in project_out(B - 1):
        pass
    s.close()


WIDE = 512
WB = WIDE // P


class TernaryWeights:

    def __init__(self, s, dram):
        self.s = s
        scales = s.landing("scales")
        self.scale = {}
        for n in ("s1", "s2", "h1s", "h2s"):
            self.scale[n] = s.sbuf(n, [P, WB])
            s.sp.dma(scales, self.scale[n][:], dram[n])
        self.s3 = s.sbuf("s3", [P, 1, P])
        s.sp.dma(scales, self.s3[:, 0, :], dram["s3"].partition_broadcast(P))
        self.scales_in = scales.landed()
        self.parts = []
        for what, blocks, columns in (("w1", 1, WIDE), ("w2w", 1, WIDE), ("h1", WB, WIDE),
                                      ("h2", WB, WIDE), ("w3", WB, P)):
            exact = s.sbuf(what, [P, blocks, columns])
            both = s.sbuf(what + "_halves", [P, blocks, 2, columns], F16)
            landing = s.landing(what)
            s.sp.dma(landing, exact[:], dram[what].rearrange("(k i) o -> i k o", i=P))
            self.parts.append((what, exact, both, landing.landed()))
        self.w1, self.w2, self.h1, self.h2, self.w3 = [both for _, _, both, _ in self.parts]

    def split(self):
        s, done = self.s, {}
        s.act.wait(self.scales_in)
        s.dve.wait(self.scales_in)
        for what, exact, both, ready in self.parts:
            if what == "w3":
                s.dve.wait(ready)
                s.dve.tensor_tensor(exact[:], exact[:], self.s3[:].broadcast_to([P, WB, P]), ALU.mult)
                ready = s.dve.mark()
            done[what] = split_halves(s, exact[:], (both[:, :, 0, :], both[:, :, 1, :]), (ready,),
                                      W_SCALE if what == "w3" else 1.0)
        return done


def ffn_stage(nc, net, name):
    s = Stage(nc, net, name)
    xn = s.sbuf("xn", [P, TILES, P])
    xT = s.sbuf("xT", [P, B * T])
    xT_halves = s.sbuf("xT_halves", [P, 2, B * T], F16)
    gate_sb = s.sbuf("gate", [P, 2, BANK])
    exact_sb = s.sbuf("exact", [P, 3, BANK])
    layers = s.sbuf("layers", [P, 6, WB, 2, BANK], F16)
    ps = s.psum("ps", [P, 8, BANK])
    pe, act, dve = s.pe, s.act, s.dve
    w = TernaryWeights(s, net.dram)
    ring = Ring(banks(ps, 8))
    marks = layer_norm(s, net, xn)
    ready = [split_halves(s, xT[:, c * BANK:(c + 1) * BANK],
                          [xT_halves[:, i, c * BANK:(c + 1) * BANK] for i in range(2)], (mark,))
             for c, mark in enumerate(to_feature_major(s, net, ring, xn, marks, xT))]
    exacts = Ring([exact_sb[:, i, :] for i in range(3)])
    halves = lambda a: (a[:, 0, :], a[:, 1, :])
    gates = Ring([gate_sb[:, i, :] for i in range(2)])
    buffers = [Ring([layers[:, 2 * n + i] for i in range(2)]) for n in range(3)]
    weights_ready = w.split()

    def first(c):
        slot, out, readers = buffers[0].take()
        tokens = slice(c * BANK, (c + 1) * BANK)
        for m in range(WB):
            i, a, ra = ring.take()
            j, b, rb = ring.take()
            pe.wait(*ra, *rb, *ready[c], *weights_ready["w1"], *weights_ready["w2w"])
            cols = slice(m * P, (m + 1) * P)
            source = halves(xT_halves[:, :, tokens])
            product_of_halves(pe, a, halves(w.w1[:, 0, :, cols]), source)
            product_of_halves(pe, b, halves(w.w2[:, 0, :, cols]), source)
            g, gate, rg = gates.take()
            act.wait(pe.mark(), *rg)
            act.activation(gate, a, ACT.Silu, scale=w.scale["s1"][:, m:m + 1])
            ring.release(i, act.mark())
            e, exact, re = exacts.take()
            dve.wait(act.mark(), *readers, *re)
            dve.scalar_tensor_tensor(exact, b, w.scale["s2"][:, m:m + 1], gate, ALU.mult, ALU.mult)
            gates.release(g, dve.mark())
            ring.release(j, dve.mark())
            split = split_halves(s, exact, halves(out[:, m]), (dve.mark(), *readers))
            exacts.release(e, *split)
        return slot, out, split

    def middle(n, weights, scale, src_slot, src, src_mark):
        slot, out, readers = buffers[n].take()
        pe.wait(*src_mark, *weights_ready["h%d" % n])
        for m in range(WB):
            i, a, ra = ring.take()
            pe.wait(*ra)
            for k in range(WB):
                product_of_halves(pe, a, halves(weights[:, k, :, m * P:(m + 1) * P]), halves(src[:, k]),
                                  k == 0, k == WB - 1)
            e, exact, re = exacts.take()
            act.wait(pe.mark(), *re)
            act.activation(exact, a, ACT.Gelu, scale=scale[:, m:m + 1])
            ring.release(i, act.mark())
            split = split_halves(s, exact, halves(out[:, m]), (act.mark(), *readers))
            exacts.release(e, *split)
        buffers[n - 1].release(src_slot, pe.mark())
        return slot, out, split

    def last(c, src_slot, src, src_mark):
        i, a, ra = ring.take()
        pe.wait(*src_mark, *ra, *weights_ready["w3"])
        for j in range(TPC):
            for k in range(WB):
                product_of_halves(pe, a[:, j * P:(j + 1) * P], halves(src[:, k, :, j * P:(j + 1) * P]),
                                  halves(w.w3[:, k]), k == 0, k == WB - 1)
        buffers[2].release(src_slot, pe.mark())
        dve.wait(pe.mark())
        x = net.residual[:, TPC * c:TPC * (c + 1), :].rearrange("p t d -> p (t d)")
        dve.scalar_tensor_tensor(x, a, 1.0 / W_SCALE, x, ALU.mult, ALU.add)
        ring.release(i, dve.mark())

    state = {}
    for step in range(CHUNKS + 3):
        if step < CHUNKS:
            state[0, step] = first(step)
        if 0 <= step - 1 < CHUNKS:
            state[1, step - 1] = middle(1, w.h1, w.scale["h1s"], *state[0, step - 1])
        if 0 <= step - 2 < CHUNKS:
            state[2, step - 2] = middle(2, w.h2, w.scale["h2s"], *state[1, step - 2])
        if 0 <= step - 3 < CHUNKS:
            last(step - 3, *state[2, step - 3])
    s.close()


BLOCK, PICKED = 32, 8
BLOCKS = T // BLOCK
SELECTED = BLOCK * PICKED
MASKED = -1e9


def sparse_stage(nc, net):
    s = Stage(nc, net, "sparse")
    dram = net.dram
    pe, act, dve, pool, sp = s.pe, s.act, s.dve, s.pool, s.sp
    FILL = 66
    ROWS = FILL + 4
    scale = HD ** -0.5
    HALVES = T // BANK
    SLOTS = 2
    scratch = nc.dram_tensor("sp_parts", (B, 2, SPLITS, P, T), BF16, kind="Internal").ap()
    picked_parts = nc.dram_tensor("sp_picked_parts", (B, SPLITS, P, SELECTED), BF16, kind="Internal").ap()
    tables = [nc.dram_tensor("sp_table%d" % b, (HEADS * BLOCKS, 2 * HD * BLOCK), F32, kind="Internal").ap()
              for b in range(B)]
    picked = nc.dram_tensor("sp_picked", (B, HEADS * PICKED, 2 * HD * BLOCK), F32, kind="Internal").ap()

    loads = s.landing("loads")

    def load(name, shape, dtype=F32, source=None):
        buffer = s.sbuf(name, shape, dtype)
        sp.dma(loads, buffer[:], dram["s_" + name] if source is None else source)
        return buffer
    w_qkv = load("w_qkv", [P, 3 * D])
    w_out = load("w_out", [P, D])
    w_gate = load("w_gate", [P, 3, P])
    b_gate = load("b_gate", [P, 3])
    b_qkv = load("b_qkv", [P, 3])
    b_v = load("b_v", [1, D])
    b_out = load("b_out", [1, D])
    select = load("select", [P, 2, 32], F32, dram["head_select"])
    own = load("own", [P, HEADS])
    block_ones = load("block_ones", [P, P])
    peak_spread = load("peak_spread", [2 * HEADS, GROUPS, P], BF16)
    row_base = load("row_base", [P, 1])
    mask_q = load("mask_q", [P, 2, P], BF16)
    mask_k = load("mask_k", [P, 2, P], BF16)
    ident_bf = s.sbuf("ident_bf", [P, P], BF16)
    ones = s.sbuf("ones", [1, P])

    q_stack = s.sbuf("q_stack", [P, SLOTS, GROUP, T], BF16)
    k_stack = s.sbuf("k_stack", [P, SLOTS, GROUP, T], BF16)
    p_stack = s.sbuf("p_stack", [P, SLOTS, GROUP, SELECTED], BF16)
    values = s.sbuf("values", [P, 2, TPB, HEADS, HD + 1])
    p_values = s.sbuf("p_values", [P, 2, SELECTED // P, HEADS, HD + 1])
    xT = s.sbuf("xT", [P, B * T])
    compressed = s.sbuf("compressed", [P, 2, T])
    sums = s.sbuf("sums", [P, 2, GROUPS, T])
    weights_sb = s.sbuf("weights", [P, 2, GROUP, BANK])
    v_value = s.sbuf("v_value", [P, T])
    means = s.sbuf("means", [P, 2, BLOCKS])
    mean_rows = s.sbuf("mean_rows", [P, 2, HEADS, BLOCKS])
    mean_values = s.sbuf("mean_values", [P, GROUPS, 32])
    block_peak = s.sbuf("block_peak", [P, TPB, HEADS])
    block_peak_parts = s.sbuf("block_peak_parts", [P, TPB, HEADS, 2], BF16)
    block_peak_rows = s.sbuf("block_peak_rows", [2 * HEADS, T], BF16)
    powers_sb = s.sbuf("powers", [P, 2, BANK])
    inverse = s.sbuf("inverse", [P, BANK])
    probs_sb = s.sbuf("probs", [P, 2, BANK])
    block_sums = s.sbuf("block_sums", [P, HALVES, GROUPS])
    block_score = s.sbuf("block_score", [P, GROUPS])
    score_rows = s.sbuf("score_rows", [GROUPS, GROUP, BLOCKS])
    top = s.sbuf("top", [GROUPS, GROUP, PICKED])
    top_at = s.sbuf("top_at", [GROUPS, GROUP, PICKED], U32)
    row_at = s.sbuf("row_at", [P, 2], U32)
    gathered = s.sbuf("gathered", [P, 2 * HD * BLOCK])
    chosen = s.sbuf("chosen", [P, 2, SELECTED])
    chosen_rest = s.sbuf("chosen_rest", [P, SELECTED])
    chosen_parts = s.sbuf("chosen_parts", [P, SPLITS, SELECTED], BF16)

    ps = s.psum("ps", [P, 8, BANK])
    ring = Ring(banks(ps, 3))
    score_ring = Ring(banks(ps, 2, 3))
    acc_ring = Ring(banks(ps, 3, 5))
    xn = weights_sb[:].rearrange("p a h (t d) -> p (a h t) d", d=P)
    marks = layer_norm(s, net, xn)
    ready = to_feature_major(s, net, Ring(banks(ps, 8)), xn, marks, xT)
    heads = Heads(s, scratch)

    dve.wait(loads.landed(), ready[-1], pe.mark())
    dve.tensor_scalar(b_qkv[:, 0:1], b_qkv[:, 0:1], scale, None, ALU.mult)
    dve.tensor_copy(ident_bf[:], net.ident[:])
    dve.memset(ones[:], 1.0)
    dve.memset(values[:, :, :, :, HD], 1.0)
    dve.memset(p_values[:, :, :, :, HD], 1.0)
    for bank in acc_ring.slots:
        dve.memset(bank, 0.0)
    start = dve.mark()
    for engine in (act, pe, pool, sp):
        engine.wait(start, loads.landed(), ready[-1])
    constants_in = s.landing("constants")
    for slot in range(SLOTS):
        for h in range(GROUP):
            sp.dma(constants_in, q_stack[QROWS:FILL, slot, h, :], dram["s_fill"][0:FILL - QROWS, :])
            sp.dma(constants_in, k_stack[QROWS:ROWS, slot, h, :], dram["s_fill_window"])
            sp.dma(constants_in, p_stack[QROWS:ROWS, slot, h, :], dram["s_fill_picked"][:, 0:SELECTED])

    table_in, sums_in, gather_in = s.landing("table"), s.landing("rows"), s.landing("gather")
    picked_in, chosen_in, parts_in = s.landing("picked"), s.landing("chosen"), s.landing("parts")
    done = {}

    def pause():
        pass

    def prepare(b):
        n = b % 2
        tokens = lambda half: slice(b * T + half * BANK, b * T + (half + 1) * BANK)
        columns = lambda half: slice(half * BANK, (half + 1) * BANK)
        q_value, k_value = heads.value[:, 0, :], heads.value[:, 1, :]

        def project_qk():
            act.wait(*done.get("means", ()), *done.get("q read", ()))
            heads.free = tuple(tuple(f) + done.get("table", ()) + done.get("q read", ()) for f in heads.free)
            heads.project(b, ring, w_qkv, b_qkv, scale, xT, ready)

        def project_v():
            for half in range(HALVES):
                i, bank, readers = ring.take()
                pe.wait(*readers)
                pe.matmul(bank, w_qkv[:, 2 * D:3 * D], xT[:, tokens(half)], start=True, stop=True)
                act.wait(pe.mark(), *done.get("table", ()), *done.get("means", ()))
                act.activation(v_value[:, columns(half)], bank, ACT.Identity, bias=b_qkv[:, 2:3])
                ring.release(i, act.mark())
            done["v"] = act.mark()

        def lay_values():
            act.wait(*done.get(("values", n), ()))
            for c in range(HALVES):
                i, bank, readers = ring.take()
                pe.wait(*readers)
                for j in range(TPC):
                    cols = bank[:, j * P:(j + 1) * P]
                    token = b * T + (TPC * c + j) * P
                    pe.matmul(cols, xT[:, token:token + P], w_qkv[:, 2 * D:3 * D], start=True, stop=False)
                    pe.matmul(cols, ones[:], b_v[:], start=False, stop=True)
                act.wait(pe.mark())
                act.copy(values[:, n, TPC * c:TPC * (c + 1), :, 0:HD],
                         bank.rearrange("p (j h d) -> p j h d", j=TPC, h=HEADS))
                ring.release(i, act.mark())
            done["values ready", b] = act.mark()

        def store_table():
            sp.wait(done["v"])
            rows = tables[b].rearrange("(h k) (w d t) -> w h d k t", h=HEADS, w=2, d=HD)
            for h in range(HEADS):
                at = slice(h * HD, (h + 1) * HD)
                for w, value in enumerate((k_value, v_value)):
                    sp.dma(table_in, rows[w, h], value[at].rearrange("p (k t) -> p k t", t=BLOCK))
            done["table"] = (table_in.landed(),)

        def block_means():
            dve.wait(done["v"], *done.get("mean use", ()))
            for w, value in enumerate((k_value, v_value[:])):
                dve.tensor_reduce(means[:, w, :], value.rearrange("p (k t) -> p k t", t=BLOCK), AX_X,
                                  ALU.add)
            dve.settle()
            dve.tensor_scalar(means[:], means[:], 1.0 / BLOCK, None, ALU.mult)
            dve.settle()
            for w in range(2):
                dve.tensor_tensor(mean_rows[:, w], means[:, w, :].unsqueeze(1).broadcast_to(
                    [P, HEADS, BLOCKS]), own[:].unsqueeze(2).broadcast_to([P, HEADS, BLOCKS]), ALU.mult)
            done["means"] = (dve.mark(),)
            i, bank, readers = ring.take()
            pe.wait(dve.mark(), *readers)
            for g in range(GROUPS):
                pe.transpose(bank[:, g * P:(g + 1) * P],
                             mean_rows[:, 1, GROUP * g:GROUP * (g + 1), :].rearrange("p h k -> p (h k)"),
                             net.ident[:])
            act.wait(pe.mark())
            for g in range(GROUPS):
                act.copy(mean_values[:, g, :], bank[:, g * P + 32 * g:g * P + 32 * (g + 1)])
            ring.release(i, act.mark())

        def block_peaks(t):
            def run():
                i, bank, readers = ring.take()
                pe.wait(*readers)
                pe.matmul(bank, q_value[:, t * P:(t + 1) * P],
                          mean_rows[:, 0].rearrange("p h k -> p (h k)"), start=True, stop=True)
                dve.wait(pe.mark())
                dve.tensor_reduce(block_peak[:, t, :], bank.rearrange("p (h k) -> p h k", k=BLOCKS), AX_X,
                                  ALU.max)
                ring.release(i, dve.mark())
            return run

        def block_peak_turn():
            dve.settle()
            dve.tensor_scalar(block_peak_parts[:, :, :, 0], block_peak[:], -1.0, None, ALU.mult)
            dve.settle()
            dve.scalar_tensor_tensor(block_peak_parts[:, :, :, 1], block_peak[:], -1.0,
                                     block_peak_parts[:, :, :, 0], ALU.mult, ALU.subtract)
            for half in range(HALVES):
                i, bank, readers = ring.take()
                pe.wait(dve.mark(), *readers)
                for j in range(TPC):
                    pe.matmul(bank[0:2 * HEADS, j * P:(j + 1) * P],
                              block_peak_parts[:, TPC * half + j].rearrange("p h s -> p (h s)"),
                              ident_bf[:], start=True, stop=True)
                act.wait(pe.mark())
                act.copy(block_peak_rows[:, columns(half)], bank[0:2 * HEADS, :])
                ring.release(i, act.mark())
            done["peak rows"] = act.mark()

        def block_powers(g, half):
            def run():
                i, bank, readers = ring.take()
                pe.wait(done["peak rows"], *readers)
                pe.matmul(bank, mean_rows[:, 0, GROUP * g:GROUP * (g + 1), :].rearrange("p h k -> p (h k)"),
                          q_value[:, columns(half)], start=True, stop=False)
                pe.matmul(bank, peak_spread[:, g, :], block_peak_rows[:, columns(half)], start=False,
                          stop=True)
                act.wait(pe.mark(), *done.get(("powers", half), ()), *done.get("gates", ()))
                act.activation(powers_sb[:, half], bank, ACT.Exp)
                done["powers ready", half] = act.mark()
                ring.release(i, act.mark())
            return run

        def block_probs(g, half):
            def run():
                i, bank, readers = ring.take()
                pe.wait(done["powers ready", half], *readers)
                pe.matmul(bank, block_ones[:], powers_sb[:, half], start=True, stop=True)
                dve.wait(pe.mark(), *done.get(("probs", half), ()))
                dve.settle()
                dve.reciprocal(inverse[:], bank)
                ring.release(i, dve.mark())
                dve.settle()
                dve.scalar_tensor_tensor(probs_sb[:, half], powers_sb[:, half], 1.0, inverse[:], ALU.mult, ALU.mult,
                                         accum_out=block_sums[:, half, g:g + 1])
                done["powers", half] = (dve.mark(), pe.mark())
                done["probs ready", half] = dve.mark()
            return run

        def block_output(g, half):
            def run():
                i, bank, readers = ring.take()
                pe.wait(done["probs ready", half], *readers)
                where = slice(32 * g, 32 * (g + 1))
                pe.matmul(bank[where, :], mean_values[:, g, :], probs_sb[:, half], start=True, stop=True)
                done["probs", half] = (pe.mark(),)
                act.wait(pe.mark(), *done.get(("compressed", n), ()))
                act.copy(compressed[where, n, columns(half)], bank[where, :])
                ring.release(i, act.mark())
                if g == GROUPS - 1 and half == HALVES - 1:
                    done["compressed ready", b] = act.mark()
                    done["q read"] = (pe.mark(),)
                    done["mean use"] = (pe.mark(),)
            return run

        def lay_scores():
            dve.settle()
            dve.tensor_tensor(block_score[:], block_sums[:, 0, :], block_sums[:, 1, :], ALU.add)
            i, bank, readers = ring.take()
            pe.wait(dve.mark(), *readers)
            pe.transpose(bank[0:GROUPS, 0:P], block_score[:], net.ident[:])
            dve.wait(pe.mark())
            dve.tensor_copy(score_rows[:].rearrange("g h k -> g (h k)"), bank[0:GROUPS, 0:P])
            ring.release(i, dve.mark())

        def rank():
            dve.settle()
            for h in range(GROUP):
                dve.max(top[:, h, :], score_rows[:, h, :])
            dve.settle()
            dve.wait(*done.get("top_at", ()))
            for h in range(GROUP):
                dve.op(lambda e, h=h: e.max_index(top_at[:, h, :], top[:, h, :], score_rows[:, h, :]))
            pool.wait(dve.mark())
            for g in range(GROUPS):
                pool.dma(sums_in, row_at[32 * g:32 * (g + 1), 0:1],
                         top_at[g:g + 1].rearrange("g h k -> g (h k)"))
            done["top_at"] = (sums_in.landed(),)

        def fetch():
            dve.wait(sums_in.landed())
            dve.tensor_scalar(row_at[:, 1:2], row_at[:, 0:1], row_base[:, 0:1], None, ALU.add)
            pool.wait(dve.mark(), table_in.landed(), *done.get("gathered", ()))
            pool.gather(gather_in, gathered[:], tables[b], row_at[:, 1:2])
            sp.wait(gather_in.landed())
            sp.dma(picked_in, picked[b], gathered[:])
            done["gathered"] = (picked_in.landed(),)
            sp.wait(picked_in.landed(), *done.get("chosen", ()))
            blocks = picked[b].rearrange("(h j) (w d t) -> w h d j t", h=HEADS, w=2, d=HD)
            for w in range(2):
                for h in range(HEADS):
                    sp.dma(chosen_in, chosen[h * HD:(h + 1) * HD, w, :].rearrange(
                        "p (j t) -> p j t", t=BLOCK), blocks[w, h])

        def split_chosen():
            dve.wait(chosen_in.landed(), *done.get("chosen parts", ()))
            split_parts(dve, chosen[:, 0, :], chosen_rest[:], [chosen_parts[:, i, :] for i in range(SPLITS)])
            sp.wait(dve.mark())
            sp.dma(parts_in, picked_parts[b].rearrange("s p t -> p s t"), chosen_parts[:])
            done["chosen parts"] = (parts_in.landed(),)
            i, bank, readers = ring.take()
            pe.wait(chosen_in.landed(), *readers)
            for j in range(SELECTED // P):
                pe.transpose(bank[:, j * P:(j + 1) * P], chosen[:, 1, j * P:(j + 1) * P], net.ident[:])
            act.wait(pe.mark(), *done.get(("p_values", n), ()))
            act.copy(p_values[:, n, :, :, 0:HD],
                     bank[:, 0:SELECTED].rearrange("p (j h d) -> p j h d", j=SELECTED // P, h=HEADS))
            ring.release(i, act.mark())
            done["p_values ready", b] = act.mark()
            done["chosen"] = (pe.mark(), dve.mark())

        steps = [project_qk, project_v, store_table, lay_values, block_means]
        steps += [block_peaks(t) for t in range(TPB)] + [block_peak_turn]
        for g in range(GROUPS):
            for half in range(HALVES):
                steps += [block_powers(g, half)]
                if g or half:
                    steps += [block_output(*before)]
                steps += [block_probs(g, half)]
                before = (g, half)
        steps += [pause, block_output(*before)]
        return steps + [lay_scores, rank] + [pause] * 4 + [fetch] + [pause] * 24 + [split_chosen]

    stack_in = [s.landing("stack%d" % i) for i in range(SLOTS)]
    stack_free = [() for _ in range(SLOTS)]

    def assemble(g):
        b, first, slot = g // GROUPS, GROUP * (g % GROUPS), g % SLOTS
        sp.wait(constants_in.landed(), parts_in.landed(), *stack_free[slot])
        sp.wait(*heads.parts_free[0], *heads.parts_free[1])
        rows = slice(first * HD, (first + GROUP) * HD)
        for i, (qpart, kpart) in enumerate(TERMS):
            at = slice(HD * i, HD * (i + 1))
            for stack, source in ((q_stack, scratch[b, 0, qpart, rows, :]),
                                  (k_stack, scratch[b, 1, kpart, rows, :]),
                                  (p_stack, picked_parts[b, kpart, rows, :])):
                sp.dma(stack_in[slot], stack[at, slot, :, :], source.rearrange("(h d) t -> d h t", d=HD))

    peak = s.sbuf("peak", [P, SLOTS, TPB, GROUP, 2])
    peak_parts = s.sbuf("peak_parts", [P, SLOTS, TPB, GROUP, 2, 2], BF16)
    peak_rows = s.sbuf("peak_rows", [4 * GROUP, SLOTS, T], BF16)
    peaks_in = [s.landing("peaks%d" % i) for i in range(SLOTS)]
    peak_free = [() for _ in range(SLOTS)]

    def score(g, unit):
        slot, kind = g % SLOTS, unit % 2
        h0, t = 2 * (unit // 2 % 2), unit // 4
        if unit == 0:
            pe.wait(stack_in[slot].landed())
            dve.wait(*peak_free[slot])
        i, bank, readers = score_ring.take()
        pe.wait(*readers)
        width = SELECTED if kind == 0 or t else P
        for n in range(2):
            out = bank[:, n * SELECTED:n * SELECTED + width]
            queries = q_stack[0:FILL, slot, h0 + n, t * P:(t + 1) * P]
            if kind == 0:
                pe.matmul(out, queries, p_stack[0:FILL, slot, h0 + n, :], start=True, stop=True)
            else:
                keys = k_stack[0:FILL, slot, h0 + n, (t + 1) * P - width:(t + 1) * P]
                pe.matmul(out, queries, keys, start=True, stop=False)
                pe.matmul(out, ident_bf[:], mask_q[:, 2 - width // P:, :].rearrange("p a k -> p (a k)"),
                          start=False, stop=True)
        dve.wait(pe.mark())
        dve.tensor_reduce(peak[:, slot, t, h0:h0 + 2, kind],
                          bank.rearrange("p (n k) -> p n k", n=2)[:, :, 0:width], AX_X, ALU.max)
        score_ring.release(i, dve.mark())

    def peaks(g):
        slot = g % SLOTS
        dve.settle()
        dve.tensor_scalar(peak_parts[:, slot, :, :, :, 0], peak[:, slot], -1.0, None, ALU.mult)
        dve.settle()
        flat = lambda a: a.rearrange("p t h k -> p (t h k)")
        dve.scalar_tensor_tensor(flat(peak_parts[:, slot, :, :, :, 1]), flat(peak[:, slot]), -1.0,
                                 flat(peak_parts[:, slot, :, :, :, 0]), ALU.mult, ALU.subtract)
        for half in range(HALVES):
            i, bank, readers = ring.take()
            pe.wait(dve.mark(), *readers)
            for j in range(TPC):
                pe.matmul(bank[0:4 * GROUP, j * P:(j + 1) * P],
                          peak_parts[:, slot, TPC * half + j].rearrange("p h k s -> p (h k s)"),
                          ident_bf[:], start=True, stop=True)
            act.wait(pe.mark())
            act.copy(peak_rows[:, slot, half * BANK:(half + 1) * BANK], bank[0:4 * GROUP, :])
            ring.release(i, act.mark())
        sp.wait(act.mark())
        for h in range(GROUP):
            sp.dma(peaks_in[slot], q_stack[FILL:ROWS, slot, h, :],
                   peak_rows[4 * h:4 * h + 4, slot, :])
        peak_free[slot] = (pe.mark(), peaks_in[slot].landed())

    weight_ring = Ring([weights_sb[:, i] for i in range(2)])
    acc = {}
    sums_ready = {}

    def accumulate(kind, half):
        if (kind, half) not in acc:
            i, bank, readers = acc_ring.take()
            pe.wait(*readers)
            acc[kind, half] = (i, bank)
        return acc[kind, half][1]

    def picked_weights(g, tile, half, between):
        slot = g % SLOTS
        w, weights, free = weight_ring.take()
        for h in range(GROUP):
            i, bank, readers = ring.take()
            pe.wait(*readers)
            pe.matmul(bank, p_stack[0:ROWS, slot, h, tile * P:(tile + 1) * P],
                      q_stack[0:ROWS, slot, h, half * BANK:(half + 1) * BANK], start=True, stop=True)
            act.wait(pe.mark(), *free)
            act.activation(weights[:, h, :], bank, ACT.Exp)
            mark = act.mark()
            ring.release(i, mark)
            between()

        def weigh():
            b, first = g // GROUPS, GROUP * (g % GROUPS)
            pe.wait(mark, done["p_values ready", b])
            into = accumulate(0, half)
            for h in range(GROUP):
                pe.matmul(into[32 * h:32 * h + HD + 1, :], p_values[:, b % 2, tile, first + h, :],
                          weights[:, h, :], start=tile == 0, stop=tile == 1)
            weight_ring.release(w, pe.mark())
            if tile:
                store(g, 0, half)
        return weigh

    def window_weights(g, tile, between):
        slot = g % SLOTS
        w, weights, free = weight_ring.take()
        width = 2 * P if tile < TPB - 1 else P
        for h0 in range(0, GROUP, 2):
            i, bank, readers = ring.take()
            pe.wait(*readers)
            for n in range(2):
                out = bank[:, n * 2 * P:n * 2 * P + width]
                pe.matmul(out, k_stack[0:ROWS, slot, h0 + n, tile * P:(tile + 1) * P],
                          q_stack[0:ROWS, slot, h0 + n, tile * P:tile * P + width], start=True, stop=False)
                pe.matmul(out, ident_bf[:], mask_k[:, 0:width // P, :].rearrange("p a q -> p (a q)"),
                          start=False, stop=True)
            act.wait(pe.mark(), *free)
            act.activation(weights[:, h0:h0 + 2, 0:width],
                           bank.rearrange("p (n q) -> p n q", n=2)[:, :, 0:width], ACT.Exp)
            mark = act.mark()
            ring.release(i, mark)
            between()
        if tile == TPB - 1:
            stack_free[slot] = (pe.mark(),)

        def weigh():
            b, first = g // GROUPS, GROUP * (g % GROUPS)
            pe.wait(mark, done["values ready", b])
            spans = [(tile, width // P)] if tile % TPC != TPC - 1 else [(tile + j, 1) for j in range(width // P)]
            for first_tile, count in spans:
                half, col = first_tile // TPC, first_tile % TPC * P
                into = accumulate(1, half)
                begins = first_tile % TPC == 0 and (tile == 0 or first_tile == tile + 1)
                for h in range(GROUP):
                    pe.matmul(into[32 * h:32 * h + HD + 1, col:col + count * P],
                              values[:, b % 2, tile, first + h, :],
                              weights[:, h, (first_tile - tile) * P:(first_tile - tile + count) * P],
                              start=begins, stop=tile == TPB - 1, skip_group_check=True)
            weight_ring.release(w, pe.mark())
            if tile % TPC == TPC - 1:
                store(g, 1, tile // TPC)
        return weigh

    def store(g, kind, half):
        i, bank = acc.pop((kind, half))
        act.wait(pe.mark(), *done.get(("sums", kind), ()))
        act.copy(sums[:, kind, g % GROUPS, half * BANK:(half + 1) * BANK], bank)
        acc_ring.release(i, act.mark())
        if g % GROUPS == GROUPS - 1 and half == HALVES - 1:
            sums_ready[g // GROUPS, kind] = act.mark()
            done[("p_values", "values")[kind], g // GROUPS % 2] = (pe.mark(),)

    mixed = s.sbuf("mixed", [P, 2, BANK])
    term, gates = inverse, powers_sb[:, 0]
    mixed_free = [(), ()]

    def project_out(b, half):
        at = slice(half * BANK, (half + 1) * BANK)

        def gate(kind):
            i, bank, readers = ring.take()
            pe.wait(*readers)
            pe.matmul(bank, w_gate[:, kind, :], xT[:, b * T + half * BANK:b * T + (half + 1) * BANK],
                      start=True, stop=True)
            act.wait(pe.mark(), *done.get("gates", ()), *done.get(("powers", 0), ()))
            act.activation(gates, bank, ACT.Sigmoid, bias=b_gate[:, kind:kind + 1])
            done["gate"] = act.mark()
            ring.release(i, act.mark())

        def first():
            gate(0)
            dve.wait(done["gate"], done["compressed ready", b], *mixed_free[half])
            dve.tensor_tensor(mixed[:, half, :], compressed[:, b % 2, at], gates, ALU.mult)
            done["compressed", b % 2] = done["gates"] = (dve.mark(),)
            gate(1)

        def normalise(kind):
            def run():
                pe.wait(sums_ready[b, kind])
                found = []
                for what in range(2):
                    j, rows, readers = ring.take()
                    pe.wait(*readers)
                    for group in range(GROUPS):
                        pe.matmul(rows[32 * group:32 * (group + 1), :], select[:, what, :],
                                  sums[:, kind, group, at], start=True, stop=True)
                    found.append((j, rows))
                dve.wait(pe.mark(), done["gate"])
                step = Chained(dve)
                dve.settle()
                step.reciprocal(term[:], found[1][1])
                ring.release(found[1][0], dve.mark())
                step.tensor_tensor(term[:], found[0][1], term[:], ALU.mult)
                ring.release(found[0][0], dve.mark())
                step.tensor_tensor(term[:], term[:], gates, ALU.mult)
                step.tensor_tensor(mixed[:, half, :], mixed[:, half, :], term[:], ALU.add)
                done["mixed", half] = dve.mark()
                done["gates"] = (dve.mark(),)
                if half == 1:
                    done["sums", kind] = (pe.mark(),)
                if kind == 0:
                    gate(2)
            return run

        def last():
            i, bank, readers = ring.take()
            pe.wait(done["mixed", half], *readers)
            for j in range(TPC):
                cols = bank[:, j * P:(j + 1) * P]
                pe.matmul(cols, mixed[:, half, j * P:(j + 1) * P], w_out[:], start=True, stop=False)
                pe.matmul(cols, ones[:], b_out[:], start=False, stop=True)
            mixed_free[half] = (pe.mark(),)
            dve.wait(pe.mark())
            tile = b * TPB + half * TPC
            x = net.residual[:, tile:tile + TPC, :].rearrange("p t d -> p (t d)")
            dve.tensor_tensor(x, bank, x, ALU.add)
            ring.release(i, dve.mark())
        return [first, normalise(0), normalise(1)], last

    def end_of(b):
        (steps, last), (other_steps, other_last) = project_out(b, 0), project_out(b, 1)
        return steps + other_steps[:1] + [last] + other_steps[1:] + [other_last]

    units, total = 4 * TPB, B * GROUPS
    for step in prepare(0):
        step()
    assemble(0)
    for unit in range(units):
        score(0, unit)
    peaks(0)
    steps = [(0, tile, half) for half in range(HALVES) for tile in range(2)]
    steps += [(1, tile, 0) for tile in range(TPB)]
    pieces = GROUP * 4 + GROUP // 2 * TPB
    begin, end = 8, pieces - 4
    work, ending, pending = [], [], []
    bridge = 5
    for g in range(total):
        b = g // GROUPS
        if g % GROUPS == GROUPS - 1:
            for step in work:
                step()
            work = []
        if g + 1 < total:
            assemble(g + 1)
        piece = counted = 0

        def between():
            nonlocal piece, counted
            piece += 1
            if ending:
                ending.pop(0)()
            elif work:
                left = (GROUPS - 1 - g % GROUPS) * pieces - piece
                for _ in range(-(-len(work) // max(left, 1))):
                    work.pop(0)()
            while g + 1 < total and counted < min(units, (piece - begin) * units // (end - begin)):
                score(g + 1, counted)
                counted += 1
        if pending:
            pending.pop()()
        for _ in range(bridge):
            if work and g % GROUPS:
                work.pop(0)()
        pe.wait(peaks_in[g % SLOTS].landed())
        for n, (kind, tile, half) in enumerate(steps):
            made = window_weights(g, tile, between) if kind else picked_weights(g, tile, half, between)
            if pending:
                pending.pop()()
            pending.append(made)
            if n == 0 and g % GROUPS == 0:
                ending = end_of(b - 1) if g else []
                work = prepare(b + 1) if b + 1 < B else []
            if n == 2:
                assert not ending
            if g + 1 < total and n == len(steps) - 2:
                peaks(g + 1)
    pending.pop()()
    for step in end_of(B - 1):
        step()
    s.close()


KH, KD, KC = 4, 32, 32
CPT = P // KC
CPB = T // KC
PAIRS = TPB // 2
FIR_TAPS = (3, 7, 15, 31)
HISTORY = max(FIR_TAPS) - 1
BRANCHES = len(FIR_TAPS) + 2
GATED = KH * BRANCHES
GATE_WIDE = 256
GB = GATE_WIDE // P
LEVELS = 5
FLOOR = 0.05
AHEAD_RATE, END_RATE = 0.5, 1.9
L2_EPS, O_EPS = 1e-12, 1e-5


def delta_stage(nc, net):
    s = Stage(nc, net, "delta")
    dram = net.dram
    pe, act, dve, pool, sp = s.pe, s.act, s.dve, s.pool, s.sp
    loads = s.landing("loads")

    def load(name, shape):
        buffer = s.sbuf(name, shape)
        sp.dma(loads, buffer[:], dram["d_" + name])
        return buffer
    w_qkv = load("w_qkv", [P, 3, P])
    w_beta = load("w_beta", [P, P])
    conv_w = load("conv_w", [P, 3, TAPS])
    fir_w = load("fir_w", [P, sum(FIR_TAPS)])
    w_gate = load("w_gate", [P, GATE_WIDE])
    w_stats = load("w_stats", [P, GATE_WIDE])
    b_gate = load("b_gate", [P, GB])
    w_logit = load("w_logit", [P, GB, GATED])
    w_alpha = load("w_alpha", [P, GATED])
    log_temp = load("log_temp", [P, GATED])
    o_gain = load("o_gain", [P, 1])
    w_out = load("w_out", [P, P])
    block_ones = load("block_ones", [P, P])
    eye = load("eye", [P, KC])
    masks = load("masks", [P, LEVELS + 2, KC])
    stat_select = load("stat_select", [P, BRANCHES, P])
    stat_one = load("stat_one", [P, 1])
    xT = s.sbuf("xT", [P, B * T])
    raw = s.sbuf("raw", [P, 3, TAPS - 1 + T])
    qk_all = s.sbuf("qk", [P, 2, 2, T])
    v_all = s.sbuf("v", [P, 3, HISTORY + T])
    beta_all = s.sbuf("beta", [P, 2, T])
    norm = raw[:, 0:2, TAPS - 1:]
    kbq_all = s.sbuf("kbq", [P, 2, 2, CPB, KC])
    keep = s.sbuf("keep", [P, 2, CPB, 2, 2, KC])
    state = s.sbuf("state", [P, 2, CPB, KC])
    at_all = s.sbuf("at", [P, 2, KH, 2, KC])
    n_all = s.sbuf("n", [P, 2, 2, KH, 2, KC])
    t_all = s.sbuf("t", [P, 2, KH, 2, KC])
    kat_all = s.sbuf("kat", [P, 2, KH, 2, 2, KC])
    vk_all = s.sbuf("vk", [P, 2, 2, KH, 2, KC])
    uw_all = s.sbuf("uw", [P, 2, 2, KH, 2, KC])
    branch = s.sbuf("branch", [P, BRANCHES - 1, T])
    absolute = s.sbuf("absolute", [P, 2, BANK])
    stats = s.sbuf("stats", [P, BANK])
    hidden = s.sbuf("hidden", [P, GB, BANK])
    logits = s.sbuf("logits", [P, TPC, KH, BRANCHES])
    small = s.sbuf("small", [P, 2, TPC * KH])
    product = s.sbuf("product", [P, BRANCHES, P])
    o = s.sbuf("o", [P, TPC, P])
    o_sq = s.sbuf("o_sq", [P, TPC, P])
    oT = s.sbuf("oT", [P, BANK])
    temper = s.sbuf("temper", [P, 2, GATED])
    eps = s.sbuf("eps", [P, 2])
    ps = s.psum("ps", [P, 8, BANK])
    cross = Ring([ps[:, 0:CPT, 0:8 * KC].rearrange(
        "p a (m t n) -> p a m t n", m=2, t=2)])
    diag = Ring([ps[:, 4, 0:256], ps[:, 5, 0:256]])
    wide = Ring(banks(ps, 2, 6))

    xn = branch[:, 0:4, :].rearrange("p a (t d) -> p (a t) d", d=P)
    marks = layer_norm(s, net, xn)
    ready = to_feature_major(s, net, Ring(banks(ps, 8)), xn, marks, xT)
    act.wait(loads.landed(), ready[-1])
    dve.wait(loads.landed(), pe.mark())
    pe.wait(loads.landed(), ready[-1])
    pos, soft = temper[:, 0, :], temper[:, 1, :]
    act.activation(soft, log_temp[:], ACT.Abs)
    act.settle()
    act.activation(soft, soft, ACT.Exp, scale=-1.0)
    act.settle()
    act.activation(soft, soft, ACT.Ln, bias=1.0)
    dve.tensor_scalar(pos, log_temp[:], 0.0, None, ALU.max)
    dve.wait(act.mark())
    dve.settle()
    dve.scalar_tensor_tensor(soft, pos, 1e-4, soft, ALU.add, ALU.add)
    dve.settle()
    dve.reciprocal(pos, soft)
    act.activation(w_out[:], w_out[:], ACT.Copy, scale=o_gain[:, 0:1])
    dve.memset(raw[:, :, 0:TAPS - 1], 0.0)
    dve.memset(v_all[:, :, 0:HISTORY], 0.0)
    dve.memset(state[:, :, 0, :], 0.0)
    dve.memset(eps[:, 0:1], L2_EPS)
    dve.memset(eps[:, 1:2], O_EPS)
    for e in (pe, act, dve, pool):
        e.wait(dve.mark(), act.mark(), loads.landed())
    inv_temp = pos
    free = {}

    def project(weights, b, half, stop=True):
        i, bank, readers = wide.take()
        pe.wait(*readers)
        t0 = b * T + half * BANK
        pe.matmul(bank, weights, xT[:, t0:t0 + BANK], start=True, stop=stop)
        return i, bank

    def prepare(b):
        qk, beta, kbq = qk_all[:, b % 2], beta_all[:, b % 2], kbq_all[:, b % 2]
        act.wait(*free.get("raw", ()))
        for n in range(3):
            for half in range(2):
                i, bank = project(w_qkv[:, n, :], b, half)
                act.wait(pe.mark())
                t0 = TAPS - 1 + half * BANK
                act.copy(raw[:, n, t0:t0 + BANK], bank)
                wide.release(i, act.mark())
            yield
        act.wait(*free.get(("operands", b % 2), ()))
        for half in range(2):
            i, bank = project(w_beta[:], b, half)
            act.wait(pe.mark())
            act.activation(beta[:, half * BANK:(half + 1) * BANK], bank, ACT.Sigmoid)
            wide.release(i, act.mark())
        yield
        v = v_all[:, b % 3, HISTORY:]
        outs = (qk[:, 0, :], qk[:, 1, :], v)
        dve.wait(act.mark(), *free.get(("operands", b % 2), ()), *free.get(("v", b % 3), ()))
        for n in (1, 0, 2):
            dve.tensor_scalar(outs[n], raw[:, n, 0:T], conv_w[:, n, 0:1], None, ALU.mult)
        for k in range(1, TAPS):
            dve.settle()
            for n in (1, 0, 2):
                dve.scalar_tensor_tensor(outs[n], raw[:, n, k:k + T], conv_w[:, n, k:k + 1], outs[n],
                                         ALU.mult, ALU.add)
            yield
        act.wait(dve.mark())
        for n in (1, 0, 2):
            act.activation(outs[n], outs[n], ACT.Silu)
        act.settle()
        silu = act.mark()
        for n in (1, 0):
            act.activation(norm[:, n, :], outs[n], ACT.Square)
        yield
        for n in (1, 0):
            for half in range(2):
                cols = slice(half * BANK, (half + 1) * BANK)
                i, bank, readers = wide.take()
                pe.wait(act.mark(), *readers)
                pe.matmul(bank, block_ones[:], norm[:, n, cols], start=True, stop=True)
                act.wait(pe.mark())
                act.activation(norm[:, n, cols], bank, ACT.Sqrt, bias=eps[:, 0:1])
                wide.release(i, act.mark())
            dve.wait(act.mark())
            dve.reciprocal(norm[:, n, :], norm[:, n, :])
            yield
        pool.wait(dve.mark())
        chunked = lambda a: a.rearrange("p (c t) -> p c t", t=KC)
        pool.wait(*free.get(("operands", b % 2), ()))
        pool.tensor_tensor(qk[:, 1, :], qk[:, 1, :], norm[:, 1, :], ALU.mult)
        dve.wait(pool.mark(), *free.get(("operands", b % 2), ()))
        dve.tensor_tensor(kbq[:, 0], chunked(qk[:, 1, :]), chunked(beta), ALU.mult)
        pool.tensor_tensor(kbq[:, 1], chunked(qk[:, 0, :]), chunked(norm[:, 0, :]), ALU.mult)
        dve.wait(silu)
        dve.settle()
        dve.tensor_tensor(beta, v, beta, ALU.mult)
        free["raw"] = (dve.mark(), pool.mark())
        free["prepared", b % 2] = (dve.mark(), pool.mark(), silu)
        yield

    def blocks(slot, left, right):
        for tile in range(2):
            for h in range(KH):
                for c in range(CPT):
                    rows = slice(KC * c, KC * (c + 1))
                    pe.matmul(slot[rows, h, tile, :], left[rows, h, tile, :], right[rows, h, tile, :],
                              start=True, stop=True)

    def pair_of_tiles(b, pair, way):
        at, kat, t1 = at_all[:, way], kat_all[:, way], t_all[:, way]
        n, nT = n_all[:, way, 0], n_all[:, way, 1]
        vk, uw = vk_all[:, way], uw_all[:, way]
        busy = free.get(("way", way), ())
        pe.wait(*free["prepared", b % 2])
        qk, beta, kbq = qk_all[:, b % 2], beta_all[:, b % 2], kbq_all[:, b % 2]
        first = pair * 2 * CPT
        for tile in range(2):
            i, bank, readers = wide.take()
            pe.wait(*readers)
            t0 = (2 * pair + tile) * P
            cols = slice(t0, t0 + P)
            kb = kbq[:, 0, first + tile * CPT:first + (tile + 1) * CPT, :]
            for m, source in enumerate((qk[:, 1, cols], beta[:, cols], kb.rearrange("p c t -> p (c t)"))):
                pe.transpose(bank[:, m * P:(m + 1) * P], source, net.ident[:])
            act.wait(pe.mark(), *busy)
            heads = lambda m: bank[:, m * P:(m + 1) * P].rearrange("p (h d) -> p h d", h=KH)
            act.copy(kat[:, :, tile, 0, :], heads(0))
            act.copy(vk[:, tile, :, 0, :], heads(1))
            act.copy(vk[:, tile, :, 1, :], heads(2))
            wide.release(i, act.mark())
        tokens = act.mark()
        i, slot, readers = cross.take()
        slot = slot[:, :, 0]
        pe.wait(*readers)
        for tile in range(2):
            for c in range(CPT):
                at_chunk = first + tile * CPT + c
                out = slice(KC * c, KC * (c + 1))
                for h in range(KH):
                    rows = slice(KC * h, KC * (h + 1))
                    pe.matmul(slot[out, h, tile, :], qk[rows, 1, at_chunk * KC:(at_chunk + 1) * KC],
                              kbq[rows, :, at_chunk, :], start=True, stop=True)
        dve.wait(pe.mark(), *busy)
        mask = lambda k: masks[:, k, :].unsqueeze(1).unsqueeze(1).broadcast_to([P, KH, 2, KC])
        dve.tensor_tensor(at, slot[:, :, :, 0:KC], mask(0), ALU.mult)
        dve.tensor_tensor(kat[:, :, :, 1, :], slot[:, :, :, KC:], mask(1), ALU.mult)
        cross.release(i, dve.mark())
        kat_mark = dve.mark()
        dve.settle()
        dve.tensor_tensor(t1, at, mask(2), ALU.mult)
        dve.settle()
        identity = eye[:].unsqueeze(1).unsqueeze(1).broadcast_to([P, KH, 2, KC])
        dve.tensor_tensor(nT, t1, identity, ALU.add)
        dve.settle()
        flat = lambda a: a.rearrange("p h t n -> p (h t n)")
        dve.op(lambda e, o_=flat(n), i_=flat(nT): e.transpose(o_, i_))
        ready = dve.mark()
        yield
        for level in range(1, LEVELS):
            i, slot, readers = diag.take()
            pe.wait(ready, *readers)
            grid = slot.rearrange("p (h t n) -> p h t n", h=KH, t=2)
            blocks(grid, at, n)
            dve.wait(pe.mark())
            dve.tensor_tensor(t1, grid, mask(2 + level), ALU.mult)
            ready = dve.mark()
            diag.release(i, ready)
            yield
            i, slot, readers = diag.take()
            pe.wait(ready, *readers)
            grid = slot.rearrange("p (h t n) -> p h t n", h=KH, t=2)
            if level < LEVELS - 1:
                blocks(grid, nT, t1)
                dve.wait(pe.mark())
                dve.tensor_tensor(n, n, grid, ALU.add)
                diag.release(i, dve.mark())
                dve.settle()
                dve.op(lambda e, o_=flat(nT), i_=flat(n): e.transpose(o_, i_))
            else:
                blocks(grid, t1, nT)
                dve.wait(pe.mark())
                dve.tensor_tensor(nT, nT, grid, ALU.add)
                diag.release(i, dve.mark())
            ready = dve.mark()
            yield
        for tile in range(2):
            i, slot, readers = diag.take()
            pe.wait(ready, tokens, *readers)
            for h in range(KH):
                for c in range(CPT):
                    rows = slice(KC * c, KC * (c + 1))
                    pe.matmul(slot[rows, 2 * KC * h:2 * KC * (h + 1)], nT[rows, h, tile, :],
                              vk[rows, tile, h, :, :], start=True, stop=True)
            act.wait(pe.mark(), *busy)
            act.copy(uw[:, tile].rearrange("p h a n -> p (h a n)"), slot)
            diag.release(i, act.mark())
        ready = act.mark()
        yield
        i, slot, readers = cross.take()
        pe.wait(ready, kat_mark, *readers)
        with_w, with_u = slot[:, :, 0], slot[:, :, 1]
        for tile in range(2):
            for h in range(KH):
                out = slice(KC * h, KC * (h + 1))
                for product_of in range(3):
                    for c in range(CPT):
                        rows = slice(KC * c, KC * (c + 1))
                        u, w = uw[rows, tile, h, 0, :], uw[rows, tile, h, 1, :]
                        if product_of == 0:
                            pe.matmul(with_w[out, c, tile, :], w, kat[rows, h, tile, :, :],
                                      start=True, stop=True)
                        elif product_of == 1:
                            pe.matmul(with_u[out, c, tile, 0:KC], kat[rows, h, tile, 0, :], u,
                                      start=True, stop=True)
                        else:
                            pe.matmul(with_u[out, c, tile, KC:], u, kat[rows, h, tile, 1, :],
                                      start=True, stop=True)
        by_chunk = lambda a: a.rearrange("p (t c) n -> p c t n", t=2)
        mine = keep[:, b % 2, first:first + 2 * CPT]
        dve.wait(pe.mark(), *free.get(("keep", b % 2), ()))
        dve.tensor_tensor(by_chunk(mine[:, :, 0, 0, :]), identity, with_w[:, :, :, 0:KC],
                          ALU.subtract)
        dve.tensor_tensor(by_chunk(mine[:, :, 0, 1, :]), by_chunk(kbq[:, 1, first:first + 2 * CPT, :]),
                          with_w[:, :, :, KC:], ALU.subtract)
        act.wait(dve.mark())
        by_two = lambda a: a.rearrange("p (t c) a n -> p c t (a n)", t=2)
        act.copy(by_two(mine[:, :, 1]), with_u)
        cross.release(i, act.mark())
        free["way", way] = (pe.mark(),)
        free["kept", b % 2] = (dve.mark(), act.mark())
        free["operands", b % 2] = (pe.mark(), dve.mark())
        yield

    def filters(b):
        v = v_all[:, b % 3, :]
        dve.wait(*free["prepared", b % 2], *free.get("branch", ()))
        for k in range(max(FIR_TAPS)):
            for n, count in enumerate(FIR_TAPS):
                if k >= count:
                    continue
                first = HISTORY + k - count + 1
                shifted = v[:, first:first + T]
                tap = sum(FIR_TAPS[:n]) + k
                weight = fir_w[:, tap:tap + 1]
                if k == 0:
                    dve.tensor_scalar(branch[:, n, :], shifted, weight, None, ALU.mult)
                else:
                    dve.settle()
                    dve.scalar_tensor_tensor(branch[:, n, :], shifted, weight, branch[:, n, :],
                                             ALU.mult, ALU.add)
                yield
        free["filtered"] = (dve.mark(),)

    def finish(b):
        kept = keep[:, b % 2]
        filtering = filters(b)
        S = state[:, b % 2]
        pe.wait(*free["kept", b % 2], free["zero"])
        dve.wait(*free["kept", b % 2], *free.get(("state", b % 2), ()))
        for c in range(CPB - 1):
            i, bank, readers = wide.take()
            slot = bank[:, 0:KC]
            pe.wait(*readers)
            if c:
                pe.wait(stepped)
            for h in range(KH):
                rows = slice(KC * h, KC * (h + 1))
                pe.matmul(slot[rows, :], kept[rows, c, 0, 0, :], S[rows, c, :], start=True, stop=True)
            dve.wait(pe.mark())
            dve.tensor_tensor(S[:, c + 1, :], slot, kept[:, c, 1, 0, :], ALU.add)
            stepped = dve.mark()
            wide.release(i, stepped)
            next(filtering, None)
            yield
        for _ in filtering:
            yield
        v = v_all[:, b % 3, HISTORY:]
        for half in range(2):
            cols = slice(half * BANK, (half + 1) * BANK)
            c0 = half * CPB // 2
            i, bank, readers = wide.take()
            pe.wait(stepped, *readers)
            for c in range(CPB // 2):
                for h in range(KH):
                    rows = slice(KC * h, KC * (h + 1))
                    pe.matmul(bank[rows, KC * c:KC * (c + 1)], S[rows, c0 + c, :],
                              kept[rows, c0 + c, 0, 1, :], start=True, stop=True)
            dve.wait(pe.mark())
            dve.tensor_tensor(branch[:, 4, cols].rearrange("p (c t) -> p c t", t=KC),
                              bank.rearrange("p (c t) -> p c t", t=KC),
                              kept[:, c0:c0 + CPB // 2, 1, 1, :], ALU.add)
            ruled = dve.mark()
            wide.release(i, ruled)
            if half:
                free["keep", b % 2] = free["state", b % 2] = (pe.mark(), dve.mark())
            source = lambda p, at=cols: v[:, at] if p == 4 else branch[:, min(p, 4), at]
            yield
            j, sums, readers = wide.take()
            pe.wait(*readers)
            for p in range(BRANCHES):
                act.wait(ruled, *free["filtered"], *free.get(("absolute", p % 2), ()))
                act.activation(absolute[:, p % 2, :], source(p), ACT.Abs)
                pe.wait(act.mark())
                pe.matmul(sums, stat_select[:, p, :], absolute[:, p % 2, :], start=p == 0,
                          stop=p == BRANCHES - 1)
                free["absolute", p % 2] = (pe.mark(),)
            act.wait(pe.mark(), *free.get("stats", ()))
            act.activation(stats[:], sums, ACT.Identity, bias=stat_one[:, 0:1])
            ready = act.mark()
            wide.release(j, ready)
            yield
            for m in range(GB):
                i, bank = project(w_gate[:, m * P:(m + 1) * P], b, half, stop=False)
                pe.wait(ready)
                pe.matmul(bank, w_stats[:, m * P:(m + 1) * P], stats[:], start=False, stop=True)
                act.wait(pe.mark(), *free.get("hidden", ()))
                act.activation(hidden[:, m, :], bank, ACT.Gelu, bias=b_gate[:, m:m + 1])
                wide.release(i, act.mark())
            ready = act.mark()
            yield
            i, bank, readers = wide.take()
            pe.wait(ready, *readers)
            for t in range(TPC):
                tok = slice(t * P, (t + 1) * P)
                out = bank[:, t * GATED:(t + 1) * GATED]
                for m in range(GB):
                    pe.matmul(out, hidden[:, m, tok], w_logit[:, m, :], start=m == 0, stop=False)
                pe.matmul(out, stats[:, tok], w_alpha[:], start=False, stop=True)
            free["stats"] = free["hidden"] = (pe.mark(),)
            grid = lambda a: a.rearrange("p (t h) -> p t h", h=KH)
            most, total = grid(small[:, 0, :]), grid(small[:, 1, :])
            over = lambda a: a.unsqueeze(3).broadcast_to([P, TPC, KH, BRANCHES])
            dve.wait(pe.mark(), *free.get("logits", ()))
            step = Chained(dve)
            lg = logits[:].rearrange("p t h n -> p t (h n)")
            step.tensor_tensor(lg, bank[:, 0:TPC * GATED].rearrange("p (t g) -> p t g", g=GATED),
                               inv_temp.unsqueeze(1).broadcast_to([P, TPC, GATED]), ALU.mult)
            wide.release(i, dve.mark())
            step.tensor_reduce(most, logits[:], AX_X, ALU.max)
            step.tensor_tensor(logits[:], logits[:], over(most), ALU.subtract)
            act.wait(dve.mark())
            act.activation(logits[:], logits[:], ACT.Exp)
            ready = act.mark()
            yield
            dve.wait(ready)
            step.tensor_reduce(total, logits[:], AX_X, ALU.add)
            step.reciprocal(most, total)
            step.tensor_scalar(most, most, 1.0 - FLOOR, None, ALU.mult)
            step.tensor_tensor(logits[:], logits[:], over(most), ALU.mult)
            step.tensor_scalar(logits[:, :, :, BRANCHES - 1], logits[:, :, :, BRANCHES - 1], FLOOR,
                               None, ALU.add)
            yield
            for t in range(TPC):
                tok = slice(half * BANK + t * P, half * BANK + (t + 1) * P)
                dve.wait(*free.get("product", ()))
                for part in range(2):
                    i, bank, readers = wide.take()
                    pe.wait(*readers)
                    for p in range(3):
                        n = 3 * part + p
                        pe.transpose(bank[:, p * P:(p + 1) * P],
                                     source(n, tok), net.ident[:])
                    dve.wait(pe.mark())
                    for p in range(3):
                        n = 3 * part + p
                        weight = logits[:, t, :, n:n + 1].broadcast_to([P, KH, KD])
                        dve.tensor_tensor(product[:, n, :].rearrange("p (h d) -> p h d", h=KH),
                                          bank[:, p * P:(p + 1) * P].rearrange("p (h d) -> p h d", h=KH),
                                          weight, ALU.mult)
                    wide.release(i, dve.mark())
                dve.settle()
                dve.wait(*free.get("o", ()))
                dve.tensor_reduce(o[:, t, :], product[:].rearrange("p n d -> p d n"), AX_X, ALU.add)
                dve.settle()
                yield
            free["logits"] = ()
            if half:
                free["branch"] = free["v", b % 3] = (pe.mark(), act.mark())
            act.wait(dve.mark())
            act.activation(o_sq[:], o[:], ACT.Square)
            ready = act.mark()
            yield
            dve.wait(ready)
            heads = lambda a: a.rearrange("p t (h d) -> p (t h) d", d=KD)
            flat = small[:, 1, :]
            dve.tensor_reduce(flat, heads(o_sq[:]), AX_X, ALU.add)
            act.wait(dve.mark())
            act.activation(flat, flat, ACT.Sqrt, scale=1.0 / KD, bias=eps[:, 1:2])
            ready = act.mark()
            yield
            dve.wait(ready)
            step.reciprocal(small[:, 0, :], flat)
            step.tensor_tensor(heads(o[:]), heads(o[:]),
                               small[:, 0, :].unsqueeze(2).broadcast_to([P, TPC * KH, KD]), ALU.mult)
            ready = dve.mark()
            yield
            i, bank, readers = wide.take()
            pe.wait(ready, *readers)
            for t in range(TPC):
                pe.transpose(bank[:, t * P:(t + 1) * P], o[:, t, :], net.ident[:])
            act.wait(pe.mark(), *free.get("oT", ()))
            free["o"] = (pe.mark(),)
            act.copy(oT[:], bank)
            ready = act.mark()
            wide.release(i, ready)
            yield
            i, bank, readers = wide.take()
            pe.wait(ready, *readers)
            for t in range(TPC):
                pe.matmul(bank[:, t * P:(t + 1) * P], oT[:, t * P:(t + 1) * P], w_out[:],
                          start=True, stop=True)
            free["oT"] = (pe.mark(),)
            dve.wait(pe.mark())
            first = b * TPB + half * TPC
            x = net.residual[:, first:first + TPC, :].rearrange("p t d -> p (t d)")
            dve.tensor_tensor(x, x, bank, ALU.add)
            wide.release(i, dve.mark())
            yield

    free["zero"] = dve.mark()

    def pairs_of_tiles(b):
        for pair in range(0, PAIRS, 2):
            both = [pair_of_tiles(b, pair + way, way) for way in range(2)]
            while both:
                for one in list(both):
                    if next(one, free) is free:
                        both.remove(one)
                    yield

    def interleave(work, *others):
        due = [0.0 for _ in others]
        for _ in work:
            for n, (other, rate) in enumerate(others):
                due[n] += rate
                while due[n] >= 1:
                    due[n] -= 1
                    next(other, None)

    interleave(prepare(0))
    ending = iter(())
    for b in range(B):
        ahead = prepare(b + 1) if b + 1 < B else iter(())
        interleave(pairs_of_tiles(b), (ahead, AHEAD_RATE), (ending, END_RATE))
        for _ in ahead:
            pass
        for _ in ending:
            pass
        ending = finish(b)
    for _ in ending:
        pass
    s.close()


class Net:
    pass


def load_stage(nc, net, stack, dram):
    def sbuf(name, shape, dtype=F32):
        return stack.enter_context(nc.sbuf_tensor(name, shape, dtype))

    s = Stage(nc, net, "load")
    loads = s.landing("loads")

    def load(name, shape, source, dtype=F32):
        buffer = sbuf("w_" + name, shape, dtype)
        s.sp.dma(loads, buffer[:], source)
        return buffer
    net.residual = sbuf("residual", [P, TILES, P])
    s.sp.dma(loads, net.residual[:], dram["x"].rearrange("b (t p) d -> p (b t) d", p=P))
    net.ident = load("ident", [P, P], dram["ident"])
    net.expert_rank = load("expert_rank", [P, EXPERTS], dram["expert_rank"])
    net.router = load("router", [P, EXPERTS], dram["router"])
    net.dram = dram
    s.act.wait(loads.landed())
    s.dve.wait(loads.landed())
    s.pe.wait(loads.landed())
    s.close()


def store_stage(nc, net):
    s = Stage(nc, net, "store")
    stored = s.landing("stored")
    s.sp.dma(stored, net.dram["out"].rearrange("b (t p) d -> p (b t) d", p=P), net.residual[:])
    s.sp.wait(stored.landed())
    s.close()


def build_network(nc, dram, stages="012345678"):
    net = Net()
    net.done = []
    with ExitStack() as stack:
        load_stage(nc, net, stack, dram)
        if "0" in stages:
            attention_stage(nc, net)
        if "1" in stages:
            moe_stage(nc, net, "moe0")
        if "2" in stages:
            mamba_stage(nc, net)
        if "3" in stages:
            moe_stage(nc, net, "moe1")
        if "4" in stages:
            sparse_stage(nc, net)
        if "5" in stages:
            ffn_stage(nc, net, "ffn0")
        if "6" in stages:
            delta_stage(nc, net)
        if "7" in stages:
            ffn_stage(nc, net, "ffn1")
        store_stage(nc, net)


def layouts(given):
    def flipped(name):
        return np.ascontiguousarray(np.asarray(given[name]).T)

    def columns(name, n=P):
        return np.ascontiguousarray(np.asarray(given[name]).reshape(-1, n).T)
    a = {
        "x": given["L0_attn_a_x"],
        "router": flipped("L0_ffn_router_w"), "w13": given["L0_ffn_w13"], "w2": given["L0_ffn_w2"],
        "w1": flipped("L1_ffn_w1_w"), "w2w": flipped("L1_ffn_w2_w"), "h1": flipped("L1_ffn_h1_w"),
        "h2": flipped("L1_ffn_h2_w"), "w3": flipped("L1_ffn_w3_w"),
        "s1": columns("L1_ffn_w1_s"), "s2": columns("L1_ffn_w2_s"), "h1s": columns("L1_ffn_h1_s"),
        "h2s": columns("L1_ffn_h2_s"), "s3": given["L1_ffn_w3_s"],
    }
    w_qkv = np.asarray(given["L0_attn_a_w_qkv"])
    b_qkv = np.asarray(given["L0_attn_a_b_qkv"])
    w_rel = np.asarray(given["L0_attn_a_w_rel"])
    a.update({
        "a_qkv": w_qkv, "a_out": given["L0_attn_a_w_out"],
        "a_bqk": b_qkv[:2 * D].reshape(2, D).T, "a_bv": b_qkv[2 * D:].reshape(1, D),
        "a_bout": np.asarray(given["L0_attn_a_b_out"]).reshape(1, D),
        "a_gain": np.stack([given["L0_attn_a_ln_g"], given["L0_attn_a_ln_b"]], 1),
        "a_rel": np.stack([np.repeat(w_rel[0::2], 2, 0).T.reshape(-1),
                           np.repeat(w_rel[1::2], 2, 0).T.reshape(-1)], 1),
    })
    def mamba(name):
        return np.asarray(given["L0_attn_b_" + name])
    dbc, dbc_b = mamba("dbc_W"), mamba("dbc_b")
    blocks = lambda w: w.reshape(CB, P, -1).transpose(1, 0, 2)
    a.update({
        "m_w_in": mamba("in_W"), "m_b_in": mamba("in_b").reshape(2 * CB, P).T,
        "m_conv_w": blocks(mamba("conv_w")), "m_conv_b": mamba("conv_b").reshape(CB, P).T,
        "m_rates": mamba("A_log").reshape(CH // PER, P).T,
        "m_w_delta": blocks(dbc[:, :RANK]),
        "m_w_b": blocks(np.tile(dbc[:, RANK:RANK + STATES], (1, PER))),
        "m_w_c": blocks(np.tile(dbc[:, RANK + STATES:], (1, PER))),
        "m_b_delta": dbc_b[:RANK].reshape(RANK, 1),
        "m_b_bc": np.stack([np.tile(dbc_b[RANK:RANK + STATES], PER),
                            np.tile(dbc_b[RANK + STATES:], PER)], 1),
        "m_w_up": mamba("dup_W"), "m_b_up": mamba("dup_b").reshape(CB, P).T,
        "m_w_out": blocks(mamba("out_W")), "m_b_out": mamba("out_b").reshape(1, P),
        "m_gain": mamba("rms_w").reshape(P, 1),
    })
    def sparse(name):
        return np.asarray(given["L1_attn_a_" + name])
    w_gate = sparse("Wg")
    a.update({
        "s_w_qkv": np.concatenate([sparse("Wq"), sparse("Wk"), sparse("Wv")], 1),
        "s_w_out": sparse("Wo"), "s_w_gate": np.repeat(w_gate[:, :, None], P, 2),
        "s_b_gate": np.tile(sparse("bg"), (P, 1)),
        "s_b_qkv": np.stack([sparse("bq"), sparse("bk"), sparse("bv")], 1),
        "s_b_v": sparse("bv").reshape(1, D), "s_b_out": sparse("bo").reshape(1, D),
    })
    def delta(name):
        return np.asarray(given["L1_attn_b_" + name])
    f = np.float32
    w1, w2 = delta("gate_w1").T, delta("gate_w2").T
    w_stats = np.zeros((P, GATE_WIDE), f)
    w_stats[:GATED] = w1[P:]
    w_alpha = np.zeros((P, GATED), f)
    w_alpha[np.arange(GATED), np.arange(GATED)] = np.tile(delta("alpha_stat"), KH)
    w_alpha[GATED] = delta("gate_b2")
    a.update({
        "d_w_qkv": np.stack([delta(n + "_proj_w").T for n in "qkv"], 1),
        "d_w_beta": np.repeat(delta("b_proj_w"), KD, 0).T,
        "d_conv_w": np.stack([delta(n + "_conv_w") for n in "qkv"], 1),
        "d_fir_w": np.concatenate([delta("fir_w%d" % n) for n in FIR_TAPS], 1),
        "d_w_gate": w1[:P], "d_w_stats": w_stats, "d_b_gate": delta("gate_b1").reshape(GB, P).T,
        "d_w_logit": w2.reshape(GB, P, GATED).transpose(1, 0, 2), "d_w_alpha": w_alpha,
        "d_log_temp": np.tile(np.repeat(delta("gate_log_temp"), BRANCHES), (P, 1)),
        "d_o_gain": np.tile(delta("o_norm_w"), KH).reshape(P, 1), "d_w_out": delta("o_proj_w").T,
    })
    a.update(constants())
    return a


FILL_ROWS = 66 + 4 - QROWS


def constants():
    f = np.float32
    c = {"ident": np.eye(P, dtype=f),
         "expert_rank": np.tile(np.arange(EXPERTS, 0, -1, dtype=f), (P, 1))}
    freq = np.exp(np.arange(0, HD, 2) * (-math.log(10000.0) / HD))
    angle = freq[:, None] * np.arange(T)
    sin, cos = np.sin(angle), np.cos(angle)
    by_sine = np.stack([sin, -cos], 1).reshape(HD, T)
    by_cosine = np.stack([cos, sin], 1).reshape(HD, T)
    c["tables"] = np.stack([np.tile(by_sine, (HEADS, 1)), np.tile(by_cosine, (HEADS, 1))], 1).astype(f)
    psi = np.stack([cos, sin], 1).reshape(HD, T).astype(f)
    bf = mybir.dt.np(BF16)
    parts = []
    rest = psi
    for _ in range(SPLITS):
        parts.append(rest.astype(bf))
        rest = rest - parts[-1].astype(f)
    c["psi"] = np.concatenate([parts[k] for _, k in TERMS] + [np.ones((2, T), bf)])
    select = np.zeros((P, 2, 32), f)
    for h in range(GROUP):
        for d in range(HD):
            select[32 * h + d, 0, HD * h + d] = 1
            select[32 * h + HD, 1, HD * h + d] = 1
    c["head_select"] = select
    c["s_own"] = np.repeat(np.eye(HEADS, dtype=f), HD, 0)
    c["s_block_ones"] = np.kron(np.eye(P // 32), np.ones((32, 32))).astype(f)
    spread_peaks = np.zeros((2 * HEADS, GROUPS, P), f)
    for h in range(HEADS):
        spread_peaks[2 * h:2 * h + 2, h // GROUP, 32 * (h % GROUP):32 * (h % GROUP + 1)] = 1
    c["s_peak_spread"] = spread_peaks.astype(bf)
    c["s_row_base"] = (np.arange(P) // PICKED * BLOCKS).astype(f).reshape(P, 1)
    i = np.arange(P)
    own_tile = np.where(i[None, :] <= i[:, None], 0.0, MASKED)
    before = np.where(i[None, :] > i[:, None], 0.0, MASKED)
    c["s_mask_q"] = np.stack([before, own_tile], 1).astype(bf)
    c["s_mask_k"] = np.stack([own_tile.T, before.T], 1).astype(bf)
    fill = np.zeros((FILL_ROWS, T), f)
    c["s_fill"] = fill.astype(bf)
    for name, at in (("s_fill_picked", FILL_ROWS - 4), ("s_fill_window", FILL_ROWS - 2)):
        rows = fill.copy()
        rows[at:at + 2] = 1
        c[name] = rows.astype(bf)
    spread = np.zeros((SPLITS, 32, SUBS, P), f)
    gather = np.zeros((P, SUBS, 32), f)
    for sub in range(SUBS):
        for ch in range(PER):
            spread[:, PER * sub + ch, sub, STATES * ch:STATES * (ch + 1)] = 1
            gather[STATES * ch:STATES * (ch + 1), sub, PER * sub + ch] = 1
    c["m_spread"] = spread.reshape(SPLITS * 32, SUBS, P).astype(bf)
    c["m_gather"] = gather
    c["d_block_ones"] = c["s_block_ones"]
    c["d_eye"] = np.tile(np.eye(KC), (CPT, 1)).astype(f)
    row, col = np.indices((KC, KC))
    masks = [-(col > row).astype(f), (col >= row).astype(f), ((row ^ col) == 1) & (col > row)]
    for n in range(1, LEVELS):
        masks.append((row >> n == (col >> n) + 1) & (row >> (n + 1) == col >> (n + 1)))
    c["d_masks"] = np.tile(np.stack(masks, 1).astype(f), (CPT, 1, 1))
    select = np.zeros((P, BRANCHES, P), f)
    for h in range(KH):
        for n in range(BRANCHES):
            select[KD * h:KD * (h + 1), n, BRANCHES * h + n] = 1.0 / KD
    c["d_stat_select"] = select
    c["d_stat_one"] = (np.arange(P) == GATED).astype(f).reshape(P, 1)
    return c


def kernel(**inputs):
    import concourse.bacc as bacc
    from concourse.bass_utils import run_bass_kernel_spmd

    nc = bacc.Bacc("TRN2", target_bir_lowering=False, num_devices=1)
    arrays = {f"in_{name}": np.ascontiguousarray(a) for name, a in layouts(inputs).items()}
    dram = {name[3:]: nc.dram_tensor(name, a.shape, mybir.dt.from_np(a.dtype), kind="ExternalInput").ap()
            for name, a in arrays.items()}
    dram["out"] = nc.dram_tensor("out", (B, T, D), F32, kind="ExternalOutput").ap()
    build_network(nc, dram)
    result = run_bass_kernel_spmd(nc, [arrays], core_ids=[0])
    return result.results[0]["out"]
```
